# Optimizing a Trainium2 kernel written in Bass

```python
import numpy as np
import jax
import jax.numpy as jnp

def _softmax(x, axis=-1):
    return jax.nn.softmax(x, axis=axis)

def _gelu(x):
    return jax.nn.gelu(x, approximate=True)

def _silu(x):
    return jax.nn.silu(x)

def _sigmoid(x):
    return jax.nn.sigmoid(x)

def _layernorm(x, axis=-1, eps=1e-05):
    m = jnp.mean(x, axis=axis, keepdims=True)
    v = jnp.var(x, axis=axis, keepdims=True)
    return (x - m) / jnp.sqrt(v + eps)

def _scatter_add(tgt, idx, src, axis=0):
    return tgt.at[idx].add(src)

def _segment_sum(src, seg, n):
    return jax.ops.segment_sum(src, seg, n)
kernel_name = 'mk_gnn_ffn_d1_gnn_r8_590dad'

def setup_inputs(seed: int=0):
    np.random.seed(seed)
    _w = jnp.asarray

    def _rec_inputs():
        import jax
        import jax.numpy as jnp
        _gk = jax.random.key(seed)
        x = -0.0003713 + 1 * jax.random.normal(jax.random.fold_in(_gk, 1), (6250, 256), jnp.float32)
        src = jax.random.randint(jax.random.fold_in(_gk, 2), (200000,), 0, 6250, jnp.int32)
        dst = jnp.minimum((6250 * jax.random.uniform(jax.random.fold_in(_gk, 3), (200000,)) ** 2.0).astype(jnp.int32), 49999)
        _o = jnp.argsort(dst, stable=True)
        src = src[_o]
        dst = dst[_o]
        edge_weight = jax.random.uniform(jax.random.fold_in(_gk, 12), (200000,), jnp.float32, 0.0, 0.999998)
        return (x, src, dst, edge_weight)
    x, src, dst, edge_weight = _rec_inputs()

    def _L0_gnn_setup():
        import jax, jax.numpy as jnp
        import numpy as np
        N_NODES = 6250
        N_EDGES = 37500
        D = 256
        EPS = 1e-12

        def _gcn_layer(x, W, b, src, dst, norm, n_nodes):
            xt = x @ W
            msg = xt[src] * norm[:, None]
            agg = jax.ops.segment_sum(msg, dst, num_segments=n_nodes)
            return jax.nn.relu(agg + b)
        key = jax.random.key(seed)
        ks = jax.random.split(key, 10)
        h5_all = jax.random.normal(ks[0], (N_NODES, D), dtype=jnp.float32)
        edge_index = jax.random.randint(ks[1], (2, N_EDGES), 0, N_NODES, dtype=jnp.int64)
        edge_weight = jax.random.uniform(ks[2], (N_EDGES,), dtype=jnp.float32)
        s = 1.0 / np.sqrt(D)
        W6 = jax.random.normal(ks[3], (D, D), dtype=jnp.float32) * s
        b6 = jnp.zeros((D,), dtype=jnp.float32)
        W7 = jax.random.normal(ks[4], (D, D), dtype=jnp.float32) * s
        b7 = jnp.zeros((D,), dtype=jnp.float32)
        Wp = jax.random.normal(ks[5], (D, D), dtype=jnp.float32) * s
        bp = jnp.zeros((D,), dtype=jnp.float32)
        return {'h5_all': h5_all, 'edge_index': edge_index, 'edge_weight': edge_weight, 'W6': W6, 'b6': b6, 'W7': W7, 'b7': b7, 'Wp': Wp, 'bp': bp}
    _L0_gnn_all = _L0_gnn_setup()
    _L0_gnn_in = {k: v for k, v in _L0_gnn_all.items() if k in ('W6', 'b6', 'W7', 'b7', 'Wp', 'bp')}
    del _L0_gnn_all

    def _L0_ffn_setup():
        import jax, jax.numpy as jnp
        import numpy as np
        TOP_K = 2
        key = jax.random.key(seed)
        ks = jax.random.split(key, 4)
        B, L, D, H, E = (8, 512, 256, 1024, 8)
        s = 0.02
        return {'x': jax.random.normal(ks[0], (B, L, D), jnp.float32), 'Wg': jax.random.normal(ks[1], (D, E), jnp.float32) * s, 'bg': jnp.zeros((E,), jnp.float32), 'W1': jax.random.normal(ks[2], (E, D, H), jnp.float32) * s, 'b1': jnp.zeros((E, H), jnp.float32), 'W2': jax.random.normal(ks[3], (E, H, D), jnp.float32) * s, 'b2': jnp.zeros((E, D), jnp.float32)}
    _L0_ffn_all = _L0_ffn_setup()
    _L0_ffn_in = {k: v for k, v in _L0_ffn_all.items() if k in ('Wg', 'bg', 'W1', 'b1', 'W2', 'b2')}
    del _L0_ffn_all
    return {'x': x, 'src': src, 'dst': dst, 'edge_weight': edge_weight, 'L0_gnn_W6': _L0_gnn_in['W6'], 'L0_gnn_b6': _L0_gnn_in['b6'], 'L0_gnn_W7': _L0_gnn_in['W7'], 'L0_gnn_b7': _L0_gnn_in['b7'], 'L0_gnn_Wp': _L0_gnn_in['Wp'], 'L0_gnn_bp': _L0_gnn_in['bp'], 'L0_ffn_Wg': _L0_ffn_in['Wg'], 'L0_ffn_bg': _L0_ffn_in['bg'], 'L0_ffn_W1': _L0_ffn_in['W1'], 'L0_ffn_b1': _L0_ffn_in['b1'], 'L0_ffn_W2': _L0_ffn_in['W2'], 'L0_ffn_b2': _L0_ffn_in['b2']}

def reference(x, src, dst, edge_weight, L0_gnn_W6, L0_gnn_b6, L0_gnn_W7, L0_gnn_b7, L0_gnn_Wp, L0_gnn_bp, L0_ffn_Wg, L0_ffn_bg, L0_ffn_W1, L0_ffn_b1, L0_ffn_W2, L0_ffn_b2):
    import jax
    import jax.numpy as jnp

    def _L0_gnn_ref(h5_all, edge_index, edge_weight, W6, b6, W7, b7, Wp, bp):
        import jax, jax.numpy as jnp
        import numpy as np
        N_NODES = 6250
        N_EDGES = 37500
        D = 256
        EPS = 1e-12

        def _gcn_layer(x, W, b, src, dst, norm, n_nodes):
            xt = x @ W
            msg = xt[src] * norm[:, None]
            agg = jax.ops.segment_sum(msg, dst, num_segments=n_nodes)
            return jax.nn.relu(agg + b)
        src, dst = (edge_index[0], edge_index[1])
        deg_out = jax.ops.segment_sum(edge_weight, src, num_segments=N_NODES)
        deg_in = jax.ops.segment_sum(edge_weight, dst, num_segments=N_NODES)
        norm = edge_weight * jax.lax.rsqrt(deg_out[src] * deg_in[dst] + EPS)
        h6 = _gcn_layer(h5_all, W6, b6, src, dst, norm, N_NODES)
        h7 = _gcn_layer(h6, W7, b7, src, dst, norm, N_NODES)
        out = h7 @ Wp + bp
        return out

    def _L0_ffn_ref(x, Wg, bg, W1, b1, W2, b2):
        import jax, jax.numpy as jnp
        import numpy as np
        TOP_K = 2
        B, L, D = x.shape
        E = W1.shape[0]
        xf = x.reshape(-1, D)
        gate_logits = xf @ Wg + bg
        top_w, top_i = jax.lax.top_k(gate_logits, TOP_K)
        top_w = jax.nn.softmax(top_w, axis=-1)
        w_dense = jnp.sum(jax.nn.one_hot(top_i, E, dtype=xf.dtype) * top_w[..., None], axis=1)
        out = jnp.zeros_like(xf)
        for e in range(E):
            h = jax.nn.gelu(xf @ W1[e] + b1[e], approximate=False)
            out = out + w_dense[:, e:e + 1] * (h @ W2[e] + b2[e])
        return out.reshape(B, L, D)
    edge_index = jnp.stack([src, dst])
    x = x + _L0_gnn_ref(_layernorm(x, axis=-1), edge_index, edge_weight, L0_gnn_W6, L0_gnn_b6, L0_gnn_W7, L0_gnn_b7, L0_gnn_Wp, L0_gnn_bp)
    x = x + _L0_ffn_ref(_layernorm(x, axis=-1)[None], L0_ffn_Wg, L0_ffn_bg, L0_ffn_W1, L0_ffn_b1, L0_ffn_W2, L0_ffn_b2)[0]
    return x

_drawn_inputs = setup_inputs


def setup_inputs(seed=0):
    import zlib

    import numpy as np

    out = dict(_drawn_inputs(seed))
    spreads = {'L0_gnn_b6': (0.0, 0.1),
     'L0_gnn_b7': (0.0, 0.1),
     'L0_gnn_bp': (0.0, 0.1),
     'L0_ffn_bg': (0.0, 0.1),
     'L0_ffn_b1': (0.0, 0.308),
     'L0_ffn_b2': (0.0, 0.1)}
    factors = {'edge_weight': 3.616, 'L0_gnn_W6': 2.749}
    for name, (base, spread) in spreads.items():
        noise = np.random.default_rng([zlib.crc32(name.encode()), seed]).standard_normal(out[name].shape)
        drawn = base * np.exp(spread * noise) if base else spread * noise
        out[name] = jnp.asarray(drawn.astype(out[name].dtype))
    for name, factor in factors.items():
        out[name] = (out[name] * factor).astype(out[name].dtype)
    return out
```

```python
import concourse.bass as bass
from concourse import mybir
from contextlib import ExitStack

F32 = mybir.dt.float32
BF16 = mybir.dt.bfloat16
I32 = mybir.dt.int32
ALU = mybir.AluOpType
ACT = mybir.ActivationFunctionType
AX = mybir.AxisListType

P = 128
NODES, EDGES, D = 6250, 200000, 256
KD = D // P
NW = -(-NODES // P)
LASTW = NODES - (NW - 1) * P
PADN = NW * P
FULLT = EDGES // P
HALF = EDGES - FULLT * P
TILES = -(-EDGES // P)
U = 4
C = -(-TILES // U)
TC = C * U
RING = 17
ROUNDS = C // RING
assert RING * ROUNDS == C
GROUPS = [(0, 5), (5, 9), (9, 13), (13, 17)]
G = -(-TC // P)
LASTG = TILES - (G - 1) * P
HB = 17
HN = TC // HB
assert HB * HN == TC and HN % 2 == 0
ROW1 = D + 1
EPS_N, EPS_LN = 1e-12, 1e-5
NE, H = 8, 1024
KH = H // P
MAXB = 2 * NW + NE
LW = 7
assert LW * LW == NW
T_CS, T_CE, T_OFF, T_REL, T_RND = range(5)


def bank(nc, ctx, name, shape):
    whole = ctx.enter_context(nc.psum_tensor(name, [P, 512], F32))
    if len(shape) == 2:
        return whole[0:shape[0], 0:shape[1]]
    return whole[0:shape[0], 0:shape[1] * shape[2]].rearrange("p (a b) -> p a b", a=shape[1])


def semaphores(nc, ctx):
    taken = []

    def clear():
        nc.clear_and_free_semaphores(taken)
        nc.all_engine_barrier()

    def take(name):
        taken.append(nc.alloc_semaphore(name=name))
        return taken[-1]

    ctx.callback(clear)
    return take


def load_edges_and_histogram(nc, x, src, dst, ew, S, rows1):
    with ExitStack() as ctx:
        sb = lambda n, s, d=F32: ctx.enter_context(nc.sbuf_tensor(n, s, d))
        ps = lambda n, s: bank(nc, ctx, n, s)
        sem = semaphores(nc, ctx)
        natural = sb("natural", [P, G, P], I32)
        shifted = sb("shifted", [P, G, P], I32)
        nat_f = sb("nat_f", [P, G, P])
        nat_w = sb("nat_w", [P, G, P])
        xin = sb("xin", [P, NW, D])
        row1 = sb("row1", [P, 7, ROW1])
        lo_i = sb("lo_i", [P, TC], I32)
        lo = sb("lo", [P, TC])
        hi = sb("hi", [P, TC])
        one_lo = [sb(f"one_lo{b}", [P, HB, P]) for b in range(2)]
        one_hi = [sb(f"one_hi{b}", [P, HB, NW]) for b in range(2)]
        w_hi = [sb(f"w_hi{b}", [P, HB, NW]) for b in range(2)]
        iota_i = sb("iota_i", [P, P], I32)
        wi_i = sb("wi_i", [P, NW + 1], I32)
        part_i = sb("part_i", [P, 1], I32)
        first4 = sb("first4", [P, 1])
        thr = sb("thr", [P, NW + 1])
        t0 = sb("t0", [P, G])
        cmp = sb("cmp", [P, NW + 1, G])
        below = sb("below", [P, NW + 1])
        viol = sb("viol", [P, 2])
        rowf = sb("rowf", [1, 12, NW + 1])
        stats = sb("stats", [P, NW, 6])
        mv = sb("mv", [P, NW, 2])
        rstd = sb("rstd", [P, NW])
        std = sb("std", [P, NW])
        nbias = sb("nbias", [P, NW])
        pt = [ps(f"pt{i}", [P, 4, P]) for i in range(2)]
        pcnt = ps("pcnt", [1, NW + 1])
        pviol = ps("pviol", [1, 2])
        pdeg = ps("pdeg", [P, NW])

        padded, x_in = sem("padded"), sem("x_in")
        src_in, dst_in, shift_in, w_in = sem("src_in"), sem("dst_in"), sem("shift_in"), sem("w_in")
        iotas, consts_ready = sem("iotas"), sem("consts_ready")
        nat_ready, nat_turned = sem("nat_ready"), sem("nat_turned")
        columns_ready = sem("columns_ready")
        tables_in, tables_summed = sem("tables_in"), sem("tables_summed")
        lohi_ready, norm_ready = sem("lohi_ready"), sem("norm_ready")
        hist_lo, hist_hi, hist_w, hist_used = sem("hist_lo"), sem("hist_hi"), sem("hist_w"), sem("hist_used")
        deg_done, deg_ready = sem("deg_done"), sem("deg_ready")
        row_made, row_stored = sem("row_made"), sem("row_stored")
        var_ready, std_ready = sem("var_ready"), sem("std_ready")
        step = sem("step")
        block = ctx.enter_context(nc.Block())

        MAIN = (G - 1) * P * P
        TAIL = FULLT * P

        @block.sync
        def _(sp):
            sp.wait_ge(padded, 5)
            for arr, to, s in ((dst, natural, dst_in), (ew, nat_w, w_in)):
                sp.dma_start(to[:, 0:G - 1, :], arr[0:MAIN].rearrange("(g p e) -> p g e", p=P, e=P)).then_inc(s, 16)
                sp.dma_start(to[0:LASTG - 1, G - 1, :], arr[MAIN:TAIL].rearrange("(p e) -> p e", e=P)).then_inc(s, 16)
                sp.dma_start(to[LASTG - 1:LASTG, G - 1, 0:HALF], arr[TAIL:EDGES].rearrange("(p e) -> p e", p=1)).then_inc(s, 16)
            sp.dma_start(shifted[:, 0:G - 1, :], dst[1:MAIN + 1].rearrange("(g p e) -> p g e", p=P, e=P)).then_inc(shift_in, 16)
            sp.dma_start(shifted[0:LASTG - 1, G - 1, :], dst[MAIN + 1:TAIL + 1].rearrange("(p e) -> p e", e=P)).then_inc(shift_in, 16)
            sp.dma_start(shifted[LASTG - 1:LASTG, G - 1, 0:HALF - 1], dst[TAIL + 1:EDGES].rearrange("(p e) -> p e", p=1)).then_inc(shift_in, 16)
            sp.dma_start(xin[:, 0:NW - 1, :], x[0:(NW - 1) * P, :].rearrange("(w p) d -> p w d", p=P)).then_inc(x_in, 16)
            sp.dma_start(xin[0:LASTW, NW - 1, :], x[(NW - 1) * P:NODES, :]).then_inc(x_in, 16)
            sp.wait_ge(nat_ready, 2)
            sp.dma_start(natural[:, 0:G - 1, :], src[0:MAIN].rearrange("(g p e) -> p g e", p=P, e=P)).then_inc(src_in, 16)
            sp.dma_start(natural[0:LASTG - 1, G - 1, :], src[MAIN:TAIL].rearrange("(p e) -> p e", e=P)).then_inc(src_in, 16)
            sp.dma_start(natural[LASTG - 1:LASTG, G - 1, 0:HALF], src[TAIL:EDGES].rearrange("(p e) -> p e", p=1)).then_inc(src_in, 16)
            for s in range(NW // 7):
                sp.wait_ge(row_made, s + 1)
                sp.dma_start(rows1[s * 7 * P:(s + 1) * 7 * P, :].rearrange("(w p) d -> p w d", p=P), row1[:, :, :]).then_inc(row_stored, 16)
            sp.wait_ge(row_stored, 16 * (NW // 7))

        @block.gpsimd
        def _(pool):
            nc.gpsimd.memset(natural[:, G - 1, :], 0).then_inc(padded, 1)
            nc.gpsimd.memset(nat_w[:, G - 1, :], 0.0).then_inc(padded, 1)
            nc.gpsimd.memset(shifted[:, G - 1, :], 1000000).then_inc(padded, 1)
            nc.gpsimd.memset(xin[:, NW - 1, :], 0.0).then_inc(padded, 1)
            nc.gpsimd.memset(t0[:, :], 1e6).then_inc(padded, 1)
            pool.iota(iota_i[:, :], [[1, P]], base=0, channel_multiplier=0).then_inc(iotas, 1)
            pool.iota(wi_i[:, :], [[1, NW + 1]], base=0, channel_multiplier=0).then_inc(iotas, 1)
            pool.iota(part_i[:, :], [[0, 1]], base=0, channel_multiplier=1).then_inc(iotas, 1)
            nc.gpsimd.memset(S.ident[:, :], 0.0).then_inc(iotas, 1)
            pool.wait_ge(iotas, 4)
            pool.affine_select(out=S.ident[:, :], in_=S.ident[:, :], compare_op=ALU.not_equal, fill=1.0, base=0,
                               pattern=[[-1, P]], channel_multiplier=1).then_inc(consts_ready, 1)
            pool.wait_ge(columns_ready, 12)
            with pool.Fori(0, HN // 2) as i:
                for b in range(2):
                    pool.wait_ge(hist_hi, 2 * i + b + 1)
                    pool.sem_inc(S.pool_turn, 1)
                    pool.wait_ge(hist_used, 2 * i + b + 1)
                    pool.sem_inc(S.pool_turn, 1)
                    nc.gpsimd.tensor_tensor(w_hi[b][:, :, :], one_hi[b][:, :, :],
                                            S.w_col[:, bass.ds((2 * i + b) * HB, HB)].unsqueeze(2).to_broadcast([P, HB, NW]),
                                            ALU.mult).then_inc(hist_w, 1)

        @block.vector
        def _(dve):
            n = [0]

            def link(ins):
                n[0] += 1
                ins.then_inc(step, 1)
                dve.wait_ge(step, n[0])

            link(nc.vector.memset(S.eps_ln[:, :], EPS_LN))
            link(nc.vector.memset(S.eps_n[:, :], EPS_N))
            nc.vector.memset(S.ones[:, :], 1.0).then_inc(consts_ready, 1)
            nc.vector.memset(S.zeros[:, :], 0.0).then_inc(consts_ready, 1)
            nc.vector.memset(S.q_col[:, :], 0.0).then_inc(consts_ready, 1)
            dve.wait_ge(iotas, 3)
            link(nc.vector.tensor_copy(S.iota[:, :], iota_i[:, :]))
            link(nc.vector.tensor_copy(thr[:, :], wi_i[:, :]))
            link(nc.vector.tensor_scalar(thr[:, :], thr[:, :], float(P), None, ALU.mult))
            link(nc.vector.tensor_copy(S.base[:, :], thr[:, 0:NW]))
            link(nc.vector.tensor_single_scalar(part_i[:, :], part_i[:, :], U - 1, ALU.bitwise_and))
            link(nc.vector.tensor_copy(first4[:, :], part_i[:, :]))
            link(nc.vector.tensor_scalar(first4[:, :], first4[:, :], 0.0, None, ALU.is_equal))
            dve.wait_ge(dst_in, 48)
            nc.vector.tensor_copy(nat_f[:, :, :], natural[:, :, :]).then_inc(nat_ready, 1)
            dve.wait_ge(nat_ready, 1)
            dve.wait_ge(shift_in, 48)
            dve.wait_ge(padded, 5)
            link(nc.vector.tensor_copy(t0[:, 0:G - 1], nat_f[:, 0:G - 1, 0]))
            link(nc.vector.tensor_copy(t0[0:LASTG, G - 1:G], nat_f[0:LASTG, G - 1, 0:1]))
            link(nc.vector.tensor_tensor(natural[:, :, :], natural[:, :, :], shifted[:, :, :], ALU.is_gt))
            link(nc.vector.tensor_reduce(viol[:, 0:1], natural[:, :, :], AX.XY, ALU.max))
            nc.vector.memset(viol[:, 1:2], 0.0)
            dve.wait_ge(nat_turned, G)
            nc.vector.memset(natural[:, G - 1, :], 0).then_inc(nat_ready, 1)
            link(nc.vector.tensor_tensor(cmp[:, :, :], t0[:, :].unsqueeze(1).to_broadcast([P, NW + 1, G]),
                                         thr[:, :].unsqueeze(2).to_broadcast([P, NW + 1, G]), ALU.is_lt))
            nc.vector.tensor_reduce(below[:, :], cmp[:, :, :], AX.X, ALU.add).then_inc(tables_in, 1)
            dve.wait_ge(x_in, 32)
            with dve.Fori(0, NW) as w:
                nc.vector.bn_stats(stats[:, bass.ds(w, 1), :], xin[:, bass.ds(w, 1), :])
            nc.vector.memset(rstd[:, :], 0.0).then_inc(norm_ready, 1)
            dve.wait_ge(norm_ready, 1)
            link(nc.vector.tensor_tensor(mv[:, :, :], stats[:, :, 1:3], stats[:, :, 4:6], ALU.add))
            link(nc.vector.tensor_tensor(std[:, :], stats[:, :, 1], stats[:, :, 4], ALU.subtract))
            link(nc.vector.tensor_tensor(nbias[:, :], std[:, :], std[:, :], ALU.mult))
            link(nc.vector.tensor_scalar(mv[:, :, 0], mv[:, :, 0], 0.5, None, ALU.mult))
            link(nc.vector.tensor_scalar(mv[:, :, 1], mv[:, :, 1], 1.0 / D, None, ALU.mult))
            link(nc.vector.scalar_tensor_tensor(mv[:, :, 1], nbias[:, :], 0.25, mv[:, :, 1], ALU.mult, ALU.add))
            nc.vector.memset(rstd[:, :], 0.0).then_inc(var_ready, 1)
            dve.wait_ge(std_ready, 1)
            link(nc.vector.reciprocal(rstd[:, :], std[:, :]))
            link(nc.vector.tensor_tensor(nbias[:, :], mv[:, :, 0], rstd[:, :], ALU.mult))
            nc.vector.tensor_scalar(nbias[:, :], nbias[:, :], -1.0, None, ALU.mult).then_inc(norm_ready, 1)
            dve.wait_ge(src_in, 48)
            dve.wait_ge(columns_ready, 4)
            nc.vector.tensor_copy(nat_f[:, :, :], natural[:, :, :]).then_inc(nat_ready, 1)
            dve.wait_ge(columns_ready, 12)
            link(nc.vector.tensor_single_scalar(lo_i[:, :], S.src_col[:, :], P - 1, ALU.bitwise_and))
            link(nc.vector.tensor_copy(lo[:, :], lo_i[:, :]))
            link(nc.vector.tensor_single_scalar(lo_i[:, :], S.src_col[:, :], 7, ALU.logical_shift_right))
            link(nc.vector.tensor_copy(hi[:, :], lo_i[:, :]))
            with dve.Fori(0, HN // 2) as i:
                for b in range(2):
                    dve.wait_ge(hist_used, 2 * i + b + 1)
                    at = bass.ds((2 * i + b) * HB, HB)
                    nc.vector.tensor_tensor(one_hi[b][:, :, :], hi[:, at].unsqueeze(2).to_broadcast([P, HB, NW]),
                                            S.iota[:, 0:NW].unsqueeze(1).to_broadcast([P, HB, NW]), ALU.is_equal).then_inc(hist_hi, 1)
                    nc.vector.tensor_tensor(one_lo[b][:, :, :], lo[:, at].unsqueeze(2).to_broadcast([P, HB, P]),
                                            S.iota[:, :].unsqueeze(1).to_broadcast([P, HB, P]), ALU.is_equal).then_inc(hist_lo, 1)
            dve.wait_ge(deg_done, 1)
            nc.vector.tensor_copy(S.deg[:, :], pdeg[:, :]).then_inc(deg_ready, 1)
            dve.wait_ge(tables_summed, 1)
            row = lambda k: rowf[0:1, k, :]
            FIRST, CSS, CES, ALLC, UNS, SRT, T1, T2 = range(8)
            fl = S.sorted_f[0:1, 0:1]
            nf = S.sorted_f[0:1, 1:2]
            link(nc.vector.tensor_copy(row(FIRST), pcnt[0:1, :]))
            link(nc.vector.tensor_scalar(fl, pviol[0:1, 0:1], 0.5, None, ALU.is_lt))
            link(nc.vector.tensor_scalar(nf, fl, -1.0, 1.0, ALU.mult, ALU.add))
            link(nc.vector.tensor_scalar(row(CSS), row(FIRST), -1.0, 0.0, ALU.add, ALU.max))
            link(nc.vector.tensor_scalar(row(CES), row(FIRST), 1.0, None, ALU.max))
            link(nc.vector.tensor_scalar(row(ALLC), thr[0:1, :], float(C) / P, nf, ALU.mult, ALU.mult))
            a, b_ = slice(0, NW), slice(1, NW + 1)
            tab = lambda k: S.tab_f[0:1, k, 0:NW]
            link(nc.vector.memset(S.tab_f[:, :, :], 0.0))
            link(nc.vector.tensor_scalar(rowf[0:1, T1, :], row(CSS), fl, None, ALU.mult))
            link(nc.vector.tensor_tensor(tab(T_CS), rowf[0:1, T1, a], rowf[0:1, ALLC, a], ALU.add))
            link(nc.vector.tensor_scalar(rowf[0:1, T2, :], row(CES), fl, None, ALU.mult))
            link(nc.vector.tensor_tensor(tab(T_CE), rowf[0:1, T2, b_], rowf[0:1, ALLC, b_], ALU.add))
            link(nc.vector.tensor_scalar(tab(T_OFF), thr[0:1, a], 1.0 / P, fl, ALU.mult, ALU.mult))
            link(nc.vector.tensor_scalar(tab(T_REL), tab(T_CE), fl, None, ALU.subtract))
            link(nc.vector.tensor_copy(S.tab_f[0:1, T_REL, NW - 1:NW], S.tab_f[0:1, T_CE, NW - 1:NW]))
            link(nc.vector.tensor_scalar(S.tab_f[0:1, T_RND, 0:1], nf, float((NW - 1) * ROUNDS), float(ROUNDS), ALU.mult, ALU.add))
            link(nc.vector.tensor_copy(S.tab[:, :, :], S.tab_f[:, :, :]))

        @block.scalar
        def _(act):
            k = 0
            for a, (cols) in enumerate((S.dst_col, S.w_col, S.src_col)):
                for q in range(4):
                    g0, g1 = 4 * q, min(4 * q + 4, G)
                    act.wait_ge(nat_turned, G * a + g1)
                    c0, c1 = g0 * P, min(g1 * P, TC)
                    nc.scalar.copy(cols[:, c0:c1], pt[k % 2][:, 0:g1 - g0, :].rearrange("p g e -> p (g e)")[:, 0:c1 - c0]).then_inc(columns_ready, 1)
                    k += 1
                if a == 1:
                    act.wait_ge(var_ready, 1)
                    nc.scalar.activation(std[:, :], mv[:, :, 1], ACT.Sqrt, bias=S.eps_ln[:, :]).then_inc(std_ready, 1)
                    act.wait_ge(norm_ready, 2)
                    with act.Fori(0, NW) as w:
                        nc.scalar.activation(xin[:, bass.ds(w, 1), :], xin[:, bass.ds(w, 1), :], ACT.Identity,
                                             bias=nbias[:, bass.ds(w, 1)], scale=rstd[:, bass.ds(w, 1)])
            act.wait_ge(deg_ready, 1)
            for s in range(NW // 7):
                act.wait_ge(row_stored, 16 * s)
                nc.scalar.copy(row1[:, :, 0:D], xin[:, 7 * s:7 * s + 7, :])
                nc.scalar.copy(row1[:, :, D:ROW1], S.deg[:, 7 * s:7 * s + 7].unsqueeze(2)).then_inc(row_made, 1)

        @block.tensor
        def _(pe):
            pe.wait_ge(consts_ready, 4)
            k = 0
            for a, (s, nat) in enumerate(((1, nat_f), (0, nat_w), (3, nat_f))):
                if s:
                    pe.wait_ge(nat_ready, s)
                else:
                    pe.wait_ge(w_in, 48)
                for q in range(4):
                    if k >= 2:
                        pe.wait_ge(columns_ready, k - 1)
                    for g in range(4 * q, min(4 * q + 4, G)):
                        nc.tensor.transpose(pt[k % 2][:, g - 4 * q, :], nat[:, g, :], S.ident[:, :]).then_inc(nat_turned, 1)
                    k += 1
                if a == 1:
                    pe.wait_ge(tables_in, 1)
                    nc.tensor.matmul(pcnt[0:1, :], first4[:, :], below[:, :], start=True, stop=True)
                    nc.tensor.matmul(pviol[0:1, :], S.ones[:, 0:1], viol[:, :], start=True, stop=True).then_inc(tables_summed, 1)
            pe.sem_inc(hist_used, 2)
            pe.wait_ge(consts_ready, 4)
            nc.tensor.matmul(pdeg[:, :], S.zeros[:, 0:P], S.zeros[:, 0:NW], start=True, stop=False)
            with pe.Fori(0, HN // 2) as i:
                for b in range(2):
                    pe.wait_ge(hist_lo, 2 * i + b + 1)
                    pe.wait_ge(hist_w, 2 * i + b + 1)
                    for j in range(HB):
                        last = nc.tensor.matmul(pdeg[:, :], one_lo[b][:, j, :], w_hi[b][:, j, :], start=False, stop=False)
                    last.then_inc(hist_used, 1)
            nc.tensor.matmul(pdeg[:, :], S.zeros[:, 0:P], S.zeros[:, 0:NW], start=False, stop=True).then_inc(deg_done, 1)


def gnn_layer(nc, S, table, width, weight, bias, h_out, first, x=None, Wp=None, bp=None, Wg=None, bg=None):
    with ExitStack() as ctx:
        sb = lambda n, s, d=F32: ctx.enter_context(nc.sbuf_tensor(n, s, d))
        ps = lambda n, s: bank(nc, ctx, n, s)
        t = "a" if first else "b"
        alloc = semaphores(nc, ctx)
        sem = lambda n: alloc(n + t)
        ring = sb("ring" + t, [P, RING * U, width])
        staged = sb("staged" + t, [P, RING * U], I32)
        sel = sb("sel" + t, [P, U, P])
        mark = sb("mark" + t, [P, U, P])
        junk = sb("junk" + t, [P, U, P])
        q4 = sb("q4" + t, [P, U])
        t4 = sb("t4" + t, [P, U])
        r4 = sb("r4" + t, [P, U])
        root4 = sb("root4" + t, [P, U])
        win = sb("win" + t, [P, P])
        di = sb("di" + t, [P, 1])
        diag = sb("diag" + t, [P, P])
        dib = sb("dib" + t, [P, P])
        wt = sb("wt" + t, [P, KD, D])
        brow = sb("brow" + t, [1, D])
        agg = sb("agg" + t, [P, D])
        aggT = sb("aggT" + t, [P, KD, P])
        h = sb("h" + t, [P, D])
        if first:
            p_di = ps("p_di" + t, [P, 1])
            p_dib = ps("p_dib" + t, [P, P])
        p_agg = ps("p_agg" + t, [P, D])
        p_t = ps("p_t" + t, [P, KD, P])
        p_h = ps("p_h" + t, [P, D])
        if not first:
            wp, bprow = sb("wp", [P, KD, D]), sb("bprow", [1, D])
            wg, bgrow = sb("wg", [P, KD, NE]), sb("bgrow", [1, NE])
            hT = sb("hT", [P, KD, P])
            x2w = sb("x2w", [P, D])
            st, mv, sd, rs = sb("st", [P, 6]), sb("mv2", [P, 2]), sb("sd", [P, 1]), sb("rs", [P, 1])
            xn, xnT = sb("xn", [P, D]), sb("xnT", [P, KD, P])
            p_hT, p_o, p_xT, p_g = ps("p_hT", [P, KD, P]), ps("p_o", [P, D]), ps("p_xT", [P, KD, P]), ps("p_g", [P, NE])
            x_pad, x_in = sem("x_pad"), sem("x_in2")
            h_turned, hT_ready, o_done, post = sem("h_turned"), sem("hT_ready"), sem("o_done"), sem("post")
            var_ready, sd_ready, xn_ready = sem("var_ready2"), sem("sd_ready"), sem("xn_ready")
            xn_turned, xnT_ready, gate_done, gate_ready, xn_stored = sem("xn_turned"), sem("xnT_ready"), sem("gate_done"), sem("gate_ready"), sem("xn_stored")

        row_in = [sem(f"row_in{s}_") for s in range(RING)]
        idx_staged, arrived, released = sem("idx_staged"), sem("arrived"), sem("released")
        weights_in = sem("weights_in")
        win_ready, mark_ready, mark_used = sem("win_ready"), sem("mark_ready"), sem("mark_used")
        di_done, diag_ready, dib_done, dib_ready = sem("di_done"), sem("diag_ready"), sem("dib_done"), sem("dib_ready")
        chain, sel_ready, sel_used = sem("chain"), sem("sel_ready"), sem("sel_used")
        product_ready, root_ready = sem("product_ready"), sem("root_ready")
        di_step = sem("di_step")
        agg_done, agg_copied, agg_turned, aggT_ready = sem("agg_done"), sem("agg_copied"), sem("agg_turned"), sem("aggT_ready")
        h_done, h_ready, h_stored = sem("h_done"), sem("h_ready"), sem("h_stored")
        block = ctx.enter_context(nc.Block())

        def entry(eng, k, w, hi):
            return eng.value_load(S.tab[0:1, k, bass.ds(w, 1)], min_val=0, max_val=hi)

        def visits(eng, w):
            return entry(eng, T_CS, w, NW * C - 1), entry(eng, T_CE, w, NW * C), entry(eng, T_OFF, w, NW - 1)

        @block.gpsimd
        def _(pool):
            rounds = pool.value_load(S.tab[0:1, T_RND, 0:1], min_val=ROUNDS, max_val=ROUNDS * NW)

            def stage(g, at):
                s0, s1 = GROUPS[g]
                nc.gpsimd.tensor_copy(staged[:, s0 * U:s1 * U], S.src_col[:, bass.ds(at * (RING * U) + s0 * U, (s1 - s0) * U)]).then_inc(idx_staged, 1)

            stage(0, 0)
            with pool.Fori(0, rounds) as it:
                here = it % ROUNDS
                there = (it + 1) % ROUNDS
                for g, (s0, s1) in enumerate(GROUPS):
                    if g < 3:
                        pool.wait_ge(released, RING * it + GROUPS[g + 1][1])
                        pool.sem_inc(S.pool_turn, 1)
                        stage(g + 1, here)
                    else:
                        pool.wait_ge(released, RING * it + RING + GROUPS[0][1])
                        pool.sem_inc(S.pool_turn, 1)
                        stage(0, there)
                    pool.wait_ge(idx_staged, 4 * it + g + 1)
                    pool.sem_inc(S.pool_turn, 1)
                    for s in range(s0, s1):
                        for j in range(U):
                            k = s * U + j
                            pool.indirect_dma_start(out=ring[:, k, :], out_offset=None, in_=table[:, :],
                                                    in_offset=bass.IndirectOffsetOnAxis(ap=staged[:, k:k + 1], axis=0)).then_inc(row_in[s], 16)

        @block.sync
        def _(sp):
            sp.dma_start(wt[:, :, :], weight.rearrange("(k p) n -> p k n", p=P)).then_inc(weights_in, 16)
            sp.dma_start(brow[:, :], bias.rearrange("(a n) -> a n", a=1)).then_inc(weights_in, 16)
            if not first:
                sp.dma_start(wp[:, :, :], Wp.rearrange("(k p) n -> p k n", p=P)).then_inc(weights_in, 16)
                sp.dma_start(wg[:, :, :], Wg.rearrange("(k p) n -> p k n", p=P)).then_inc(weights_in, 16)
                sp.dma_start(bprow[:, :], bp.rearrange("(a n) -> a n", a=1)).then_inc(weights_in, 16)
                sp.dma_start(bgrow[:, :], bg.rearrange("(a n) -> a n", a=1)).then_inc(weights_in, 16)
                sp.wait_ge(x_pad, 1)
                sp.dma_start(S.x2[:, 0:NW - 1, :], x[0:(NW - 1) * P, :].rearrange("(w p) d -> p w d", p=P)).then_inc(x_in, 16)
                sp.dma_start(S.x2[0:LASTW, NW - 1, :], x[(NW - 1) * P:NODES, :]).then_inc(x_in, 16)
            rounds = sp.value_load(S.tab[0:1, T_RND, 0:1], min_val=ROUNDS, max_val=ROUNDS * NW)
            with sp.Fori(0, rounds) as it:
                for s in range(RING):
                    sp.wait_ge(row_in[s], 16 * U * (it + 1))
                    sp.sem_inc(arrived, 1)

        @block.vector
        def _(dve):
            def window(w):
                cs, ce, off = visits(dve, w)
                dve.wait_ge(sel_ready, U * (cs + off))
                nc.vector.tensor_scalar(win[:, :], S.iota[:, :], S.base[:, bass.ds(w, 1)], None, ALU.add).then_inc(win_ready, 1)
                dve.wait_ge(win_ready, w + 1)
                dve.sem_inc(S.dve_turn, 1)
                if first:
                    with dve.Fori(cs, ce) as c:
                        rc = c % C
                        for j in range(U):
                            dve.wait_ge(mark_used, (c + off) * U + j + 1)
                            nc.vector.tensor_scalar(mark[:, j, :], win[:, :], S.dst_col[:, bass.ds(rc * U + j, 1)], None, ALU.is_equal).then_inc(mark_ready, 1)
                    dve.wait_ge(di_done, w + 1)
                    nc.vector.tensor_copy(di[:, :], p_di[:, :]).then_inc(di_step, 1)
                    dve.wait_ge(di_step, w + 1)
                    nc.vector.tensor_scalar(diag[:, :], S.ident[:, :], di[:, 0:1], None, ALU.mult).then_inc(diag_ready, 1)
                    dve.wait_ge(dib_done, w + 1)
                    nc.vector.tensor_copy(dib[:, :], p_dib[:, :]).then_inc(dib_ready, 1)
                    dve.wait_ge(dib_ready, w + 1)
                    dve.sem_inc(S.dve_turn, 1)
                with dve.Fori(cs, ce) as c:
                    rc = c % C
                    v = c + off
                    if first:
                        slot = rc % RING
                        dve.wait_ge(arrived, c + 1)
                        for j in range(U):
                            nc.vector.scalar_tensor_tensor(junk[:, j, :], win[:, :], S.dst_col[:, bass.ds(rc * U + j, 1)], dib[:, :],
                                                           ALU.is_equal, ALU.mult, accum_out=q4[:, j:j + 1]).then_inc(chain, 1)
                        here = bass.ds(rc * U, U)
                        dve.wait_ge(chain, 7 * v + 4)
                        nc.vector.tensor_tensor(S.q_col[:, here], S.q_col[:, here], q4[:, :], ALU.add).then_inc(chain, 1)
                        dve.wait_ge(chain, 7 * v + 5)
                        nc.vector.tensor_tensor(t4[:, :].unsqueeze(2), S.q_col[:, here].unsqueeze(2), ring[:, bass.ds(slot * U, U), D:ROW1], ALU.mult).then_inc(product_ready, 1)
                        dve.wait_ge(root_ready, v + 1)
                        nc.vector.reciprocal(r4[:, :], root4[:, :]).then_inc(chain, 1)
                        dve.wait_ge(chain, 7 * v + 6)
                        nc.vector.tensor_tensor(S.norm_col[:, here], r4[:, :], S.w_col[:, here], ALU.mult).then_inc(chain, 1)
                        dve.wait_ge(chain, 7 * v + 7)
                    for j in range(U):
                        dve.wait_ge(sel_used, v * U + j + 1)
                        nc.vector.tensor_scalar(sel[:, j, :], win[:, :], S.dst_col[:, bass.ds(rc * U + j, 1)],
                                                S.norm_col[:, bass.ds(rc * U + j, 1)], ALU.is_equal, ALU.mult).then_inc(sel_ready, 1)

            def residual(w):
                dve.wait_ge(o_done, w + 1)
                nc.vector.tensor_tensor(x2w[:, :].unsqueeze(1), p_o.unsqueeze(1), S.x2[:, bass.ds(w, 1), :], ALU.add).then_inc(post, 1)
                dve.wait_ge(post, 5 * w + 1)
                dve.sem_inc(S.dve_turn, 1)
                nc.vector.tensor_copy(S.x2[:, bass.ds(w, 1), :], x2w[:, :].unsqueeze(1)).then_inc(post, 1)
                nc.vector.bn_stats(st[:, :], x2w[:, :]).then_inc(post, 1)
                dve.wait_ge(post, 5 * w + 3)
                dve.sem_inc(S.dve_turn, 1)
                nc.vector.bn_aggr(mv[:, :], st[:, :]).then_inc(var_ready, 1)
                dve.wait_ge(sd_ready, w + 1)
                nc.vector.reciprocal(rs[:, :], sd[:, :]).then_inc(post, 1)
                dve.wait_ge(post, 5 * w + 4)
                dve.wait_ge(xn_stored, 16 * w)
                dve.wait_ge(xn_turned, KD * w)
                dve.sem_inc(S.dve_turn, 1)
                nc.vector.tensor_scalar(xn[:, :], x2w[:, :], mv[:, 0:1], rs[:, 0:1], ALU.subtract, ALU.mult).then_inc(xn_ready, 1)
                dve.wait_ge(xn_ready, w + 1)
                dve.sem_inc(post, 1)

            if first:
                with dve.Fori(0, NW) as w:
                    window(w)
            else:
                nc.vector.memset(S.x2[:, NW - 1, :], 0.0).then_inc(x_pad, 1)
                dve.wait_ge(x_in, 32)
                window(0)
                with dve.Fori(1, NW) as w:
                    window(w)
                    residual(w - 1)
                residual(NW - 1)

        @block.tensor
        def _(pe):
            pe.sem_inc(mark_used, U)
            pe.sem_inc(sel_used, U)
            pe.sem_inc(released, RING)
            pe.wait_ge(weights_in, 32 if first else 96)

            def window(w):
                cs, ce, off = visits(pe, w)
                rel = entry(pe, T_REL, w, NW * C)
                if first:
                    nc.tensor.matmul(p_di[:, :], S.zeros[:, 0:P], S.zeros[:, 0:1], start=True, stop=False)
                    with pe.Fori(cs, ce) as c:
                        rc = c % C
                        for j in range(U):
                            pe.wait_ge(mark_ready, (c + off) * U + j + 1)
                            nc.tensor.matmul(p_di[:, :], mark[:, j, :], S.w_col[:, bass.ds(rc * U + j, 1)], start=False, stop=False).then_inc(mark_used, 1)
                    nc.tensor.matmul(p_di[:, :], S.zeros[:, 0:P], S.zeros[:, 0:1], start=False, stop=True).then_inc(di_done, 1)
                    pe.wait_ge(diag_ready, w + 1)
                    nc.tensor.matmul(p_dib[:, :], S.ones[:, :], diag[:, :], start=True, stop=True).then_inc(dib_done, 1)
                nc.tensor.matmul(p_agg[:, :], S.zeros[:, 0:P], S.zeros[:, 0:D], start=True, stop=False)
                with pe.Fori(cs, ce) as c:
                    slot = c % RING
                    v = c + off
                    pe.wait_ge(arrived, c + 1)
                    for j in range(U):
                        pe.wait_ge(sel_ready, v * U + j + 1)
                        nc.tensor.matmul(p_agg[:, :], sel[:, j, :], ring[:, bass.ds(slot * U + j, 1), 0:D], start=False, stop=False).then_inc(sel_used, 1)
                    with pe.If(c < rel):
                        nc.tensor.matmul(p_agg[:, 0:1], S.zeros[:, 0:P], S.zeros[:, 0:1], start=False, stop=False).then_inc(released, 1)
                nc.tensor.matmul(p_agg[:, :], S.zeros[:, 0:P], S.zeros[:, 0:D], start=False, stop=True).then_inc(agg_done, 1)
                pe.wait_ge(agg_copied, w + 1)
                for k in range(KD):
                    nc.tensor.transpose(p_t[:, k, :], agg[:, k * P:(k + 1) * P], S.ident[:, :]).then_inc(agg_turned, 1)
                pe.wait_ge(aggT_ready, w + 1)
                nc.tensor.matmul(p_h[:, :], S.ones[0:1, :], brow[:, :], start=True, stop=False)
                for k in range(KD):
                    last = nc.tensor.matmul(p_h[:, :], aggT[:, k, :], wt[:, k, :], start=False, stop=k == KD - 1)
                last.then_inc(h_done, 1)
                if not first:
                    pe.wait_ge(h_ready, w + 1)
                    for k in range(KD):
                        nc.tensor.transpose(p_hT[:, k, :], h[:, k * P:(k + 1) * P], S.ident[:, :]).then_inc(h_turned, 1)
                    pe.wait_ge(hT_ready, w + 1)
                    nc.tensor.matmul(p_o[:, :], S.ones[0:1, :], bprow[:, :], start=True, stop=False)
                    for k in range(KD):
                        last = nc.tensor.matmul(p_o[:, :], hT[:, k, :], wp[:, k, :], start=False, stop=k == KD - 1)
                    last.then_inc(o_done, 1)

            def gate(w):
                pe.wait_ge(xn_ready, w + 1)
                for k in range(KD):
                    nc.tensor.transpose(p_xT[:, k, :], xn[:, k * P:(k + 1) * P], S.ident[:, :]).then_inc(xn_turned, 1)
                pe.wait_ge(xnT_ready, w + 1)
                nc.tensor.matmul(p_g[:, :], S.ones[0:1, :], bgrow[:, :], start=True, stop=False)
                for k in range(KD):
                    last = nc.tensor.matmul(p_g[:, :], xnT[:, k, :], wg[:, k, :], start=False, stop=k == KD - 1)
                last.then_inc(gate_done, 1)

            if first:
                with pe.Fori(0, NW) as w:
                    window(w)
            else:
                window(0)
                with pe.Fori(1, NW) as w:
                    window(w)
                    gate(w - 1)
                gate(NW - 1)

        @block.scalar
        def _(act):
            def window(w):
                if first:
                    cs, ce, off = visits(act, w)
                    with act.Fori(cs, ce) as c:
                        act.wait_ge(product_ready, c + off + 1)
                        nc.scalar.activation(root4[:, :], t4[:, :], ACT.Sqrt, bias=S.eps_n[:, :]).then_inc(root_ready, 1)
                act.wait_ge(agg_done, w + 1)
                nc.scalar.copy(agg[:, :], p_agg[:, :]).then_inc(agg_copied, 1)
                act.wait_ge(agg_turned, KD * (w + 1))
                nc.scalar.copy(aggT[:, :, :], p_t[:, :, :]).then_inc(aggT_ready, 1)
                act.wait_ge(h_done, w + 1)
                if first:
                    act.wait_ge(h_stored, 16 * w)
                nc.scalar.activation(h[:, :], p_h[:, :], ACT.Relu).then_inc(h_ready, 1)
                if first:
                    act.wait_ge(h_ready, w + 1)
                    act.dma_start(h_out[bass.ds(w * P, P), :], h[:, :]).then_inc(h_stored, 16)
                else:
                    act.wait_ge(h_turned, KD * (w + 1))
                    nc.scalar.copy(hT[:, :, :], p_hT[:, :, :]).then_inc(hT_ready, 1)

            def root(w):
                act.wait_ge(var_ready, w + 1)
                nc.scalar.activation(sd[:, :], mv[:, 1:2], ACT.Sqrt, bias=S.eps_ln[:, :]).then_inc(sd_ready, 1)

            def gate(w):
                act.wait_ge(xn_ready, w + 1)
                act.dma_start(h_out[bass.ds(w * P, P), :], xn[:, :]).then_inc(xn_stored, 16)
                act.wait_ge(xn_turned, KD * (w + 1))
                nc.scalar.copy(xnT[:, :, :], p_xT[:, :, :]).then_inc(xnT_ready, 1)
                act.wait_ge(gate_done, w + 1)
                nc.scalar.copy(S.logits[:, bass.ds(w, 1), :], p_g[:, :].unsqueeze(1)).then_inc(gate_ready, 1)

            if first:
                with act.Fori(0, NW) as w:
                    window(w)
                act.wait_ge(h_stored, 16 * NW)
            else:
                window(0)
                with act.Fori(1, NW) as w:
                    root(w - 1)
                    window(w)
                    gate(w - 1)
                root(NW - 1)
                gate(NW - 1)
                act.wait_ge(xn_stored, 16 * NW)




def route(nc, S, xn_rows, x_rows, y_rows):
    with ExitStack() as ctx:
        sb = lambda n, s, d=F32: ctx.enter_context(nc.sbuf_tensor(n, s, d))
        ps = lambda n, s: bank(nc, ctx, n, s)
        sem = semaphores(nc, ctx)
        TOK = [P, NW, NE]
        one1, one2, both, score, rest, place = (sb(n, TOK) for n in ("one1", "one2", "both", "score", "rest", "place"))
        total, upto = sb("total", TOK), sb("upto", TOK)
        m1, m2, top, ex = (sb(n, [P, NW]) for n in ("m1", "m2", "top", "ex"))
        prio, region = sb("prio", [P, NE]), sb("region", [P, NE])
        ones_nw = sb("ones_nw", [P, NW])
        pos_f = sb("pos_f", [P, NW, 2])
        before = sb("before", [P, P])
        count_i = sb("count_i", [P, NE], I32)
        count_f = sb("count_f", [1, NE])
        batch = sb("batch", [P, 3, NE])
        zero_rows = sb("zero_rows", [P, D])
        tile = [sb(f"tile{s}", [P, D]) for s in range(LW)]
        staged = sb("staged_d", [P, LW, 2], I32)
        p_rank, p_total = ps("p_rank", TOK), ps("p_total", TOK)
        before_ready, step, d_ready, e_ready = sem("before_ready"), sem("step_d"), sem("d_ready"), sem("e_ready")
        both_ready, ranked, pos_ready, zero_ready = sem("both_ready"), sem("ranked"), sem("pos_ready"), sem("zero_ready")
        tile_in = [sem(f"tile_in{s}") for s in range(LW)]
        tile_out = [sem(f"tile_out{s}") for s in range(LW)]
        idx_staged, zero_out, y_zeroed, etab_ready = sem("idx_staged_d"), sem("zero_out"), sem("y_zeroed"), sem("etab_ready")
        block = ctx.enter_context(nc.Block())

        @block.vector
        def _(dve):
            n = [0]

            def link(ins):
                n[0] += 1
                ins.then_inc(step, 1)
                dve.wait_ge(step, n[0])

            wide = lambda t: t[:, :].unsqueeze(2).to_broadcast(TOK)
            per = lambda t: t[:, :].unsqueeze(1).to_broadcast(TOK)
            nc.vector.memset(zero_rows[:, :], 0.0).then_inc(zero_ready, 1)
            link(nc.vector.memset(ones_nw[:, :], 1.0))
            link(nc.vector.tensor_scalar(prio[:, :], S.iota[:, 0:NE], -1.0, float(NE), ALU.mult, ALU.add))
            for logits, m, one in ((S.logits, m1, one1), (rest, m2, one2)):
                link(nc.vector.tensor_reduce(m[:, :], logits[:, :, :], AX.X, ALU.max))
                link(nc.vector.tensor_tensor(score[:, :, :], logits[:, :, :], wide(m), ALU.is_equal))
                link(nc.vector.tensor_tensor(score[:, :, :], score[:, :, :], per(prio), ALU.mult))
                link(nc.vector.tensor_reduce(top[:, :], score[:, :, :], AX.X, ALU.max))
                link(nc.vector.tensor_tensor(one[:, :, :], score[:, :, :], wide(top), ALU.is_equal))
                if one is one1:
                    link(nc.vector.scalar_tensor_tensor(rest[:, :, :], one1[:, :, :], -3e38, S.logits[:, :, :], ALU.mult, ALU.add))
            nc.vector.tensor_tensor(both[:, :, :], one1[:, :, :], one2[:, :, :], ALU.add).then_inc(both_ready, 1)
            nc.vector.tensor_tensor(m2[:, :], m2[:, :], m1[:, :], ALU.subtract).then_inc(d_ready, 1)
            dve.wait_ge(e_ready, 1)
            link(nc.vector.tensor_scalar(m1[:, :], ex[:, :], 1.0, None, ALU.add))
            link(nc.vector.reciprocal(S.share[:, :, 0], m1[:, :]))
            link(nc.vector.tensor_tensor(S.share[:, :, 1], ex[:, :], S.share[:, :, 0], ALU.mult))
            dve.wait_ge(ranked, 1)
            link(nc.vector.tensor_copy(total[:, :, :], p_total[:, :, :]))
            for e in range(NE):
                last = nc.vector.tensor_tensor_scan(upto[:, :, e], ones_nw[:, :], total[:, :, e], 0.0, ALU.mult, ALU.add)
                if e < NE - 1:
                    last.then_inc(pos_ready, 1)
            link(last)
            dve.wait_ge(pos_ready, NE - 1)
            link(nc.vector.tensor_scalar(batch[:, 0, :], upto[:, NW - 1, :], float(P - 1), None, ALU.add))
            link(nc.vector.tensor_copy(count_i[:, :], batch[:, 0, :]))
            link(nc.vector.tensor_single_scalar(count_i[:, :], count_i[:, :], 7, ALU.logical_shift_right))
            link(nc.vector.tensor_copy(batch[:, 0, :], count_i[:, :]))
            link(nc.vector.tensor_scalar(batch[:, 0, :], batch[:, 0, :], 1.0, None, ALU.max))
            link(nc.vector.tensor_tensor_scan(batch[:, 1, :], ones_nw[:, 0:NE], batch[:, 0, :], 0.0, ALU.mult, ALU.add))
            link(nc.vector.tensor_tensor(batch[:, 2, :], batch[:, 1, :], batch[:, 0, :], ALU.subtract))
            link(nc.vector.tensor_scalar(region[:, :], batch[:, 2, :], float(P), None, ALU.mult))
            link(nc.vector.tensor_tensor(count_f[0:1, :], upto[0:1, NW - 1, :], region[0:1, :], ALU.add))
            link(nc.vector.tensor_copy(S.etab[0:1, 0, :], count_f[0:1, :]))
            link(nc.vector.tensor_copy(S.etab[0:1, 1, :], batch[0:1, 0, :]))
            link(nc.vector.tensor_copy(S.etab[0:1, 3, :], batch[0:1, 1, :]))
            nc.vector.tensor_copy(S.etab[0:1, 2, :], batch[0:1, 2, :]).then_inc(etab_ready, 1)
            link(nc.vector.tensor_tensor(place[:, :, :], upto[:, :, :], total[:, :, :], ALU.subtract))
            link(nc.vector.tensor_tensor(place[:, :, :], place[:, :, :], p_rank[:, :, :], ALU.add))
            link(nc.vector.tensor_tensor(place[:, :, :], place[:, :, :], per(region), ALU.add))
            for k, one in enumerate((one1, one2)):
                link(nc.vector.tensor_tensor(score[:, :, :], place[:, :, :], one[:, :, :], ALU.mult))
                link(nc.vector.tensor_reduce(pos_f[:, :, k], score[:, :, :], AX.X, ALU.add))
            nc.vector.tensor_copy(S.pos[:, :, :], pos_f[:, :, :]).then_inc(pos_ready, 1)

        @block.scalar
        def _(act):
            act.wait_ge(d_ready, 1)
            nc.scalar.activation(ex[:, :], m2[:, :], ACT.Exp).then_inc(e_ready, 1)

        @block.tensor
        def _(pe):
            pe.wait_ge(before_ready, 2)
            pe.wait_ge(both_ready, 1)
            nc.tensor.matmul(p_rank[:, :, :], before[:, :], both[:, :, :], start=True, stop=True)
            nc.tensor.matmul(p_total[:, :, :], S.ones[:, :], both[:, :, :], start=True, stop=True).then_inc(ranked, 1)

        @block.sync
        def _(sp):
            sp.wait_ge(zero_ready, 1)
            sp.wait_ge(etab_ready, 1)
            with sp.Fori(0, NE) as e:
                end = sp.value_load(S.etab[0:1, 0, bass.ds(e, 1)], min_val=0, max_val=MAXB * P)
                sp.dma_start(x_rows[bass.ds(end, P), :], zero_rows[:, :]).then_inc(zero_out, 16)
            used = sp.value_load(S.etab[0:1, 3, NE - 1:NE], min_val=NE, max_val=MAXB)
            with sp.Fori(used, MAXB + 1) as g:
                sp.dma_start(y_rows[bass.ds(g * P, P), :], zero_rows[:, :]).then_inc(y_zeroed, 16)
            with sp.Fori(0, LW) as i:
                for s in range(LW):
                    sp.wait_ge(tile_out[s], 32 * i)
                    sp.dma_start(tile[s][:, :], xn_rows[bass.ds((i * LW + s) * P, P), :]).then_inc(tile_in[s], 16)
            with sp.Fori(0, used) as g:
                sp.sem_inc(y_zeroed, 16)
            sp.wait_ge(y_zeroed, 16 * (MAXB + 1))

        @block.gpsimd
        def _(pool):
            nc.gpsimd.memset(before[:, :], 1.0).then_inc(before_ready, 1)
            pool.wait_ge(before_ready, 1)
            pool.affine_select(out=before[:, :], in_=before[:, :], compare_op=ALU.is_gt, fill=0.0, base=0,
                               pattern=[[1, P]], channel_multiplier=-1).then_inc(before_ready, 1)
            pool.wait_ge(pos_ready, NE)
            pool.wait_ge(zero_out, 16 * NE)
            with pool.Fori(0, LW) as i:
                for s in range(LW):
                    pool.wait_ge(tile_out[s], 32 * i)
                    pool.sem_inc(S.pool_turn, 1)
                nc.gpsimd.tensor_copy(staged[:, :, :], S.pos[:, bass.ds(i * LW, LW), :]).then_inc(idx_staged, 1)
                pool.wait_ge(idx_staged, i + 1)
                pool.sem_inc(S.pool_turn, 1)
                for s in range(LW):
                    pool.wait_ge(tile_in[s], 16 * i + 16)
                    pool.sem_inc(S.pool_turn, 1)
                    for k in range(2):
                        pool.indirect_dma_start(out=x_rows[:, :], out_offset=bass.IndirectOffsetOnAxis(ap=staged[:, s, k:k + 1], axis=0),
                                                in_=tile[s][:, :], in_offset=None).then_inc(tile_out[s], 16)
            for s in range(LW):
                pool.wait_ge(tile_out[s], 32 * LW)


def experts(nc, S, x_rows, y_rows, W1, b1, W2, b2):
    with ExitStack() as ctx:
        sb = lambda n, s, d=F32: ctx.enter_context(nc.sbuf_tensor(n, s, d))
        ps = lambda n, s: bank(nc, ctx, n, s)
        sem = semaphores(nc, ctx)
        w1 = [sb(f"w1_{p}", [P, KD, H]) for p in range(2)]
        w2 = [sb(f"w2_{p}", [P, KH, D]) for p in range(2)]
        b1n, b1T = sb("b1n", [NE * KH, P]), sb("b1T", [P, NE * KH])
        b2b = sb("b2b", [P, NE, D])
        xb, xT = sb("xb", [P, D]), sb("xT", [P, KD, P])
        hid = sb("hid", [P, KH, P])
        y = sb("y", [P, D])
        p_x, p_y, p_b = ps("p_x", [P, KD, P]), ps("p_y", [P, D]), ps("p_b", [P, NE * KH])
        p_h = [ps(f"p_hid{i}", [P, P]) for i in range(4)]
        w_in = [sem(f"w_in{p}") for p in range(2)]
        w_used, bias_in, b1_turned, b1_ready = sem("w_used"), sem("bias_in"), sem("b1_turned"), sem("b1_ready")
        x_in, x_turned, xT_ready, hid_done, hid_ready = sem("x_in3"), sem("x_turned"), sem("xT_ready"), sem("hid_done"), sem("hid_ready")
        y_done, y_ready, y_stored = sem("y_done"), sem("y_ready"), sem("y_stored")
        block = ctx.enter_context(nc.Block())

        def batches(eng, e):
            return (eng.value_load(S.etab[0:1, 2, bass.ds(e, 1)], min_val=0, max_val=MAXB - 1),
                    eng.value_load(S.etab[0:1, 3, bass.ds(e, 1)], min_val=1, max_val=MAXB))

        @block.sync
        def _(sp):
            sp.dma_start(b1n[:, :], b1.rearrange("e (k p) -> (e k) p", p=P)).then_inc(bias_in, 16)
            sp.dma_start(b2b[:, :, :], b2.rearrange("e d -> (e d)").partition_broadcast(P)).then_inc(bias_in, 16)
            with sp.Fori(0, NE) as e:
                g0, g1 = batches(sp, e)
                with sp.Fori(g0, g1) as g:
                    sp.wait_ge(x_turned, KD * g)
                    sp.dma_start(xb[:, :], x_rows[bass.ds(g * P, P), :]).then_inc(x_in, 16)

        @block.scalar
        def _(act):
            act.wait_ge(b1_turned, 1)
            nc.scalar.copy(b1T[:, :], p_b).then_inc(b1_ready, 1)
            with act.Fori(0, NE) as e:
                g0, g1 = batches(act, e)
                with act.Fori(g0, g1) as g:
                    act.wait_ge(x_turned, KD * (g + 1))
                    nc.scalar.copy(xT[:, :, :], p_x[:, :, :]).then_inc(xT_ready, 1)
                    act.wait_ge(y_done, g)
                    for k in range(KH):
                        act.wait_ge(hid_done, g * KH + k + 1)
                        nc.scalar.activation(hid[:, k, :], p_h[k % 4], ACT.Gelu, bias=b1T[:, bass.ds(e * KH + k, 1)]).then_inc(hid_ready, 1)

        @block.tensor
        def _(pe):
            pe.wait_ge(bias_in, 32)
            nc.tensor.transpose(p_b, b1n[:, :], S.ident[0:NE * KH, 0:NE * KH]).then_inc(b1_turned, 1)
            with pe.Fori(0, NE // 2) as pair:
                for p in range(2):
                    g0, g1 = batches(pe, pair * 2 + p)
                    pe.wait_ge(w_in[p], 32 * (pair + 1))
                    pe.sem_inc(S.pe_turn, 1)
                    with pe.Fori(g0, g1) as g:
                        pe.wait_ge(x_in, 16 * (g + 1))
                        for k in range(KD):
                            nc.tensor.transpose(p_x[:, k, :], xb[:, k * P:(k + 1) * P], S.ident[:, :]).then_inc(x_turned, 1)
                        pe.wait_ge(xT_ready, g + 1)
                        for k in range(KH):
                            if k >= 4:
                                pe.wait_ge(hid_ready, g * KH + k - 3)
                            for d in range(KD):
                                last = nc.tensor.matmul(p_h[k % 4], w1[p][:, d, k * P:(k + 1) * P], xT[:, d, :], start=d == 0, stop=d == KD - 1)
                            last.then_inc(hid_done, 1)
                        pe.wait_ge(y_ready, g)
                        for k in range(KH):
                            pe.wait_ge(hid_ready, g * KH + k + 1)
                            last = nc.tensor.matmul(p_y, hid[:, k, :], w2[p][:, k, :], start=k == 0, stop=k == KH - 1)
                        last.then_inc(y_done, 1)
                    nc.tensor.matmul(p_b[:, 0:1], S.zeros[:, 0:P], S.zeros[:, 0:1], start=True, stop=True).then_inc(w_used, 1)

        @block.vector
        def _(dve):
            with dve.Fori(0, NE) as e:
                g0, g1 = batches(dve, e)
                with dve.Fori(g0, g1) as g:
                    dve.wait_ge(y_done, g + 1)
                    dve.wait_ge(y_stored, 16 * g)
                    dve.sem_inc(S.dve_turn, 1)
                    nc.vector.tensor_tensor(y[:, :].unsqueeze(1), p_y.unsqueeze(1), b2b[:, bass.ds(e, 1), :], ALU.add).then_inc(y_ready, 1)

        @block.gpsimd
        def _(pool):
            with pool.Fori(0, NE // 2) as pair:
                for p in range(2):
                    e = pair * 2 + p
                    if p == 0:
                        for q in range(2):
                            pool.wait_ge(w_used, 2 * pair)
                            pool.sem_inc(S.pool_turn, 1)
                            pool.dma_start(w1[q][:, :, :], W1[bass.ds(pair * 2 + q, 1), :, :].rearrange("a (k p) n -> p (a k) n", p=P)).then_inc(w_in[q], 16)
                            pool.dma_start(w2[q][:, :, :], W2[bass.ds(pair * 2 + q, 1), :, :].rearrange("a (k p) n -> p (a k) n", p=P)).then_inc(w_in[q], 16)
                    g0, g1 = batches(pool, e)
                    with pool.Fori(g0, g1) as g:
                        pool.wait_ge(y_ready, g + 1)
                        pool.sem_inc(S.pool_turn, 1)
                        pool.dma_start(y_rows[bass.ds(g * P, P), :], y[:, :]).then_inc(y_stored, 16)
            used = pool.value_load(S.etab[0:1, 3, NE - 1:NE], min_val=NE, max_val=MAXB)
            pool.wait_ge(y_stored, 16 * used)
            pool.sem_inc(S.pool_turn, 1)


def combine(nc, S, y_rows, out):
    with ExitStack() as ctx:
        sb = lambda n, s, d=F32: ctx.enter_context(nc.sbuf_tensor(n, s, d))
        sem = semaphores(nc, ctx)
        rows = [[sb(f"rows{s}_{k}", [P, D]) for k in range(2)] for s in range(LW)]
        part = [sb(f"part{s}", [P, D]) for s in range(LW)]
        res = [sb(f"res{s}", [P, D]) for s in range(LW)]
        staged = sb("staged_f", [P, LW, 2], I32)
        row_in = [sem(f"row_in_f{s}") for s in range(LW)]
        summed, stored, idx_staged, half = sem("summed"), [sem(f"stored{s}") for s in range(LW)], sem("idx_staged_f"), sem("half")
        block = ctx.enter_context(nc.Block())

        @block.gpsimd
        def _(pool):
            with pool.Fori(0, LW) as i:
                for s in range(LW):
                    pool.wait_ge(row_in[s], 32 * i)
                    pool.sem_inc(S.pool_turn, 1)
                nc.gpsimd.tensor_copy(staged[:, :, :], S.pos[:, bass.ds(i * LW, LW), :]).then_inc(idx_staged, 1)
                pool.wait_ge(idx_staged, i + 1)
                pool.sem_inc(S.pool_turn, 1)
                for s in range(LW):
                    pool.wait_ge(summed, LW * i + s + 1)
                    pool.sem_inc(S.pool_turn, 1)
                    for k in range(2):
                        pool.indirect_dma_start(out=rows[s][k][:, :], out_offset=None, in_=y_rows[:, :],
                                                in_offset=bass.IndirectOffsetOnAxis(ap=staged[:, s, k:k + 1], axis=0)).then_inc(row_in[s], 16)

        @block.vector
        def _(dve):
            dve.sem_inc(summed, LW)
            with dve.Fori(0, LW) as i:
                for s in range(LW):
                    w = i * LW + s
                    dve.wait_ge(row_in[s], 32 * i + 32)
                    dve.sem_inc(S.dve_turn, 1)
                    nc.vector.scalar_tensor_tensor(part[s][:, :].unsqueeze(1), rows[s][0][:, :].unsqueeze(1), S.share[:, bass.ds(w, 1), 0],
                                                   S.x2[:, bass.ds(w, 1), :], ALU.mult, ALU.add).then_inc(half, 1)
                    dve.wait_ge(half, w + 1)
                    dve.wait_ge(stored[s], 16 * i)
                    dve.sem_inc(S.dve_turn, 1)
                    nc.vector.scalar_tensor_tensor(res[s][:, :], rows[s][1][:, :], S.share[:, bass.ds(w, 1), 1],
                                                   part[s][:, :], ALU.mult, ALU.add).then_inc(summed, 1)

        @block.sync
        def _(sp):
            with sp.Fori(0, LW - 1) as i:
                for s in range(LW):
                    w = i * LW + s
                    sp.wait_ge(summed, LW + w + 1)
                    sp.dma_start(out[bass.ds(w * P, P), :], res[s][:, :]).then_inc(stored[s], 16)
            for s in range(LW):
                w = (LW - 1) * LW + s
                n = min(P, NODES - w * P)
                sp.wait_ge(summed, LW + w + 1)
                sp.dma_start(out[w * P:w * P + n, :], res[s][0:n, :]).then_inc(stored[s], 16)
            for s in range(LW):
                sp.wait_ge(stored[s], 16 * LW)


class Shared:
    pass


def build(nc, x, src, dst, edge_weight, W6, b6, W7, b7, Wp, bp, Wg, bg, W1, b1, W2, b2, out):
    rows1 = nc.dram_tensor("rows1", [PADN, ROW1], F32).ap()
    h6 = nc.dram_tensor("h6", [PADN, D], F32).ap()
    xn_rows = nc.dram_tensor("xn_rows", [PADN, D], F32).ap()
    x_rows = nc.dram_tensor("x_rows", [(MAXB + 1) * P, D], F32).ap()
    y_rows = nc.dram_tensor("y_rows", [(MAXB + 1) * P, D], F32).ap()
    S = Shared()
    with ExitStack() as ctx:
        sb = lambda n, s, d=F32: ctx.enter_context(nc.sbuf_tensor(n, s, d))
        S.pool_turn = ctx.enter_context(nc.semaphore("pool_turn"))
        S.pe_turn = ctx.enter_context(nc.semaphore("pe_turn"))
        S.dve_turn = ctx.enter_context(nc.semaphore("dve_turn"))
        S.src_col = sb("src_col", [P, TC], I32)
        S.dst_col = sb("dst_col", [P, TC])
        S.w_col = sb("w_col", [P, TC])
        S.q_col = sb("q_col", [P, TC])
        S.norm_col = sb("norm_col", [P, TC])
        S.ident = sb("ident", [P, P])
        S.ones = sb("ones", [P, P])
        S.zeros = sb("zeros", [P, D], BF16)
        S.iota = sb("iota", [P, P])
        S.base = sb("base", [P, NW])
        S.eps_ln = sb("eps_ln", [P, 1])
        S.eps_n = sb("eps_n", [P, 1])
        S.deg = sb("deg", [P, NW])
        S.sorted_f = sb("sorted_f", [1, 2])
        S.tab_f = sb("tab_f", [1, 5, NW + 1])
        S.tab = sb("tab", [1, 5, NW + 1], I32)
        load_edges_and_histogram(nc, x, src, dst, edge_weight, S, rows1)
        gnn_layer(nc, S, rows1, ROW1, W6, b6, h6, True)
        S.x2 = sb("x2", [P, NW, D])
        S.logits = sb("logits", [P, NW, NE])
        gnn_layer(nc, S, h6, D, W7, b7, xn_rows, False, x, Wp, bp, Wg, bg)
        S.share = sb("share", [P, NW, 2])
        S.pos = sb("pos", [P, NW, 2], I32)
        S.etab = sb("etab", [1, 4, NE], I32)
        route(nc, S, xn_rows, x_rows, y_rows)
        experts(nc, S, x_rows, y_rows, W1, b1, W2, b2)
        combine(nc, S, y_rows, out)


_INS = ['x', 'src', 'dst', 'edge_weight', 'L0_gnn_W6', 'L0_gnn_b6', 'L0_gnn_W7', 'L0_gnn_b7', 'L0_gnn_Wp', 'L0_gnn_bp',
        'L0_ffn_Wg', 'L0_ffn_bg', 'L0_ffn_W1', 'L0_ffn_b1', 'L0_ffn_W2', 'L0_ffn_b2']


def kernel(**inputs):
    import numpy as _np
    import concourse.bacc as _bacc
    from concourse.bass_utils import run_bass_kernel_spmd as _run
    nc = _bacc.Bacc("TRN2", target_bir_lowering=False, num_devices=1)
    arrays, args = {}, []
    for name in _INS:
        a = _np.ascontiguousarray(inputs[name])
        arrays[f"in_{name}_dram"] = a
        args.append(nc.dram_tensor(f"in_{name}_dram", a.shape, mybir.dt.from_np(a.dtype), kind="ExternalInput").ap())
    o = nc.dram_tensor("out_0_dram", (NODES, D), F32, kind="ExternalOutput").ap()
    build(nc, *args, o)
    r = _run(nc, [arrays], core_ids=[0])
    return r.results[0]["out_0_dram"]
```

```python
import concourse.bass as bass
from concourse import mybir
from contextlib import ExitStack

F32 = mybir.dt.float32
BF16 = mybir.dt.bfloat16
I32 = mybir.dt.int32
ALU = mybir.AluOpType
ACT = mybir.ActivationFunctionType
AX = mybir.AxisListType

P = 128
NODES, EDGES, D = 6250, 200000, 256
KD = D // P
NW = -(-NODES // P)
LASTW = NODES - (NW - 1) * P
PADN = NW * P
FULLT = EDGES // P
HALF = EDGES - FULLT * P
TILES = -(-EDGES // P)
U = 8
C = -(-TILES // U)
TC = C * U
RING = 7
ROUNDS = C // RING
assert RING * ROUNDS == C
GROUPS = [(0, 2), (2, 4), (4, 6), (6, 7)]
G = -(-TC // P)
LASTG = TILES - (G - 1) * P
HB = 16
HN = TC // HB
assert HB * HN == TC and HN % 2 == 0
LO, HI = P // 2, 2 * NW
ROW1 = D + 1
EPS_N, EPS_LN = 1e-12, 1e-5
NE, H = 8, 1024
KH = H // P
B = 2 * P
assert 2 * PADN % B == 0
MAXB = 2 * PADN // B + NE
LW = 7
assert LW * LW == NW
T_CS, T_CE, T_OFF, T_REL, T_RND = range(5)


def bank(nc, ctx, name, shape):
    whole = ctx.enter_context(nc.psum_tensor(name, [P, 512], F32))
    if len(shape) == 2:
        return whole[0:shape[0], 0:shape[1]]
    return whole[0:shape[0], 0:shape[1] * shape[2]].rearrange("p (a b) -> p a b", a=shape[1])


def semaphores(nc, ctx):
    taken = []

    def clear():
        nc.clear_and_free_semaphores(taken)
        nc.all_engine_barrier()

    def take(name):
        taken.append(nc.alloc_semaphore(name=name))
        return taken[-1]

    ctx.callback(clear)
    return take


def load_edges_and_histogram(nc, x, src, dst, ew, S, rows1):
    with ExitStack() as ctx:
        sb = lambda n, s, d=F32: ctx.enter_context(nc.sbuf_tensor(n, s, d))
        ps = lambda n, s: bank(nc, ctx, n, s)
        sem = semaphores(nc, ctx)
        natural = sb("natural", [P, G, P], I32)
        shifted = sb("shifted", [P, G, P], I32)
        nat_f = sb("nat_f", [P, G, P])
        nat_w = sb("nat_w", [P, G, P])
        xin = sb("xin", [P, NW, D])
        row1 = sb("row1", [P, 7, ROW1])
        lo_i = sb("lo_i", [P, TC], I32)
        lo = sb("lo", [P, TC])
        hi = sb("hi", [P, TC])
        one_lo = [sb(f"one_lo{b}", [P, HB, LO]) for b in range(2)]
        one_hi = [sb(f"one_hi{b}", [P, HB, HI]) for b in range(2)]
        w_hi = [sb(f"w_hi{b}", [P, HB, HI]) for b in range(2)]
        iota_i = sb("iota_i", [P, P], I32)
        wi_i = sb("wi_i", [P, NW + 1], I32)
        part_i = sb("part_i", [P, 1], I32)
        first4 = sb("first4", [P, 1])
        thr = sb("thr", [P, NW + 1])
        t0 = sb("t0", [P, G])
        cmp = sb("cmp", [P, NW + 1, G])
        below = sb("below", [P, NW + 1])
        viol = sb("viol", [P, 2])
        rowf = sb("rowf", [1, 12, NW + 1])
        stats = sb("stats", [P, NW, 6])
        mv = sb("mv", [P, NW, 2])
        rstd = sb("rstd", [P, NW])
        std = sb("std", [P, NW])
        nbias = sb("nbias", [P, NW])
        pt = [ps(f"pt{i}", [P, 4, P]) for i in range(2)]
        pcnt = ps("pcnt", [1, NW + 1])
        pviol = ps("pviol", [1, 2])
        phist = ps("phist", [LO, HI])
        pdeg = ps("pdeg", [P, NW])
        hist = sb("hist", [LO, 2, NW])
        lower = sb("lower", [LO, P])
        w_rest = sb("w_rest", [P, TC])

        padded, x_in = sem("padded"), sem("x_in")
        src_in, dst_in, shift_in, w_in = sem("src_in"), sem("dst_in"), sem("shift_in"), sem("w_in")
        iotas, consts_ready = sem("iotas"), sem("consts_ready")
        nat_ready, nat_turned = sem("nat_ready"), sem("nat_turned")
        columns_ready = sem("columns_ready")
        tables_in, tables_summed = sem("tables_in"), sem("tables_summed")
        lohi_ready, norm_ready = sem("lohi_ready"), sem("norm_ready")
        hist_lo, hist_hi, hist_w, hist_used = sem("hist_lo"), sem("hist_hi"), sem("hist_w"), sem("hist_used")
        hist_done, hist_ready = sem("hist_done"), sem("hist_ready")
        deg_done, deg_ready = sem("deg_done"), sem("deg_ready")
        row_made, row_stored = sem("row_made"), sem("row_stored")
        var_ready, std_ready = sem("var_ready"), sem("std_ready")
        step = sem("step")
        block = ctx.enter_context(nc.Block())

        MAIN = (G - 1) * P * P
        TAIL = FULLT * P

        @block.sync
        def _(sp):
            sp.wait_ge(padded, 5)
            for arr, to, s in ((dst, natural, dst_in), (ew, nat_w, w_in)):
                sp.dma_start(to[:, 0:G - 1, :], arr[0:MAIN].rearrange("(g p e) -> p g e", p=P, e=P)).then_inc(s, 16)
                sp.dma_start(to[0:LASTG - 1, G - 1, :], arr[MAIN:TAIL].rearrange("(p e) -> p e", e=P)).then_inc(s, 16)
                sp.dma_start(to[LASTG - 1:LASTG, G - 1, 0:HALF], arr[TAIL:EDGES].rearrange("(p e) -> p e", p=1)).then_inc(s, 16)
            sp.dma_start(shifted[:, 0:G - 1, :], dst[1:MAIN + 1].rearrange("(g p e) -> p g e", p=P, e=P)).then_inc(shift_in, 16)
            sp.dma_start(shifted[0:LASTG - 1, G - 1, :], dst[MAIN + 1:TAIL + 1].rearrange("(p e) -> p e", e=P)).then_inc(shift_in, 16)
            sp.dma_start(shifted[LASTG - 1:LASTG, G - 1, 0:HALF - 1], dst[TAIL + 1:EDGES].rearrange("(p e) -> p e", p=1)).then_inc(shift_in, 16)
            sp.dma_start(xin[:, 0:NW - 1, :], x[0:(NW - 1) * P, :].rearrange("(w p) d -> p w d", p=P)).then_inc(x_in, 16)
            sp.dma_start(xin[0:LASTW, NW - 1, :], x[(NW - 1) * P:NODES, :]).then_inc(x_in, 16)
            sp.wait_ge(nat_ready, 2)
            sp.dma_start(natural[:, 0:G - 1, :], src[0:MAIN].rearrange("(g p e) -> p g e", p=P, e=P)).then_inc(src_in, 16)
            sp.dma_start(natural[0:LASTG - 1, G - 1, :], src[MAIN:TAIL].rearrange("(p e) -> p e", e=P)).then_inc(src_in, 16)
            sp.dma_start(natural[LASTG - 1:LASTG, G - 1, 0:HALF], src[TAIL:EDGES].rearrange("(p e) -> p e", p=1)).then_inc(src_in, 16)
            for s in range(NW // 7):
                sp.wait_ge(row_made, s + 1)
                sp.dma_start(rows1[s * 7 * P:(s + 1) * 7 * P, :].rearrange("(w p) d -> p w d", p=P), row1[:, :, :]).then_inc(row_stored, 16)
            sp.wait_ge(row_stored, 16 * (NW // 7))

        @block.gpsimd
        def _(pool):
            nc.gpsimd.memset(natural[:, G - 1, :], 0).then_inc(padded, 1)
            nc.gpsimd.memset(nat_w[:, G - 1, :], 0.0).then_inc(padded, 1)
            nc.gpsimd.memset(shifted[:, G - 1, :], 1000000).then_inc(padded, 1)
            nc.gpsimd.memset(xin[:, NW - 1, :], 0.0).then_inc(padded, 1)
            nc.gpsimd.memset(t0[:, :], 1e6).then_inc(padded, 1)
            pool.iota(iota_i[:, :], [[1, P]], base=0, channel_multiplier=0).then_inc(iotas, 1)
            pool.iota(wi_i[:, :], [[1, NW + 1]], base=0, channel_multiplier=0).then_inc(iotas, 1)
            pool.iota(part_i[:, :], [[0, 1]], base=0, channel_multiplier=1).then_inc(iotas, 1)
            nc.gpsimd.memset(S.ident[:, :], 0.0).then_inc(iotas, 1)
            nc.gpsimd.memset(lower[:, :], 0.0).then_inc(iotas, 1)
            pool.wait_ge(iotas, 5)
            pool.affine_select(out=S.ident[:, :], in_=S.ident[:, :], compare_op=ALU.not_equal, fill=1.0, base=0,
                               pattern=[[-1, P]], channel_multiplier=1).then_inc(consts_ready, 1)
            pool.affine_select(out=lower[:, :], in_=lower[:, :], compare_op=ALU.not_equal, fill=1.0, base=LO,
                               pattern=[[-1, P]], channel_multiplier=1).then_inc(consts_ready, 1)
            pool.wait_ge(columns_ready, 12)
            with pool.Fori(0, HN // 2) as i:
                for b in range(2):
                    pool.wait_ge(hist_hi, 2 * i + b + 1)
                    pool.sem_inc(S.pool_turn, 1)
                    pool.wait_ge(hist_used, 2 * i + b + 1)
                    pool.sem_inc(S.pool_turn, 1)
                    nc.gpsimd.tensor_tensor(w_hi[b][:, :, :], one_hi[b][:, :, :],
                                            S.w_col[:, bass.ds((2 * i + b) * HB, HB)].unsqueeze(2).to_broadcast([P, HB, HI]),
                                            ALU.mult).then_inc(hist_w, 1)

        @block.vector
        def _(dve):
            n = [0]

            def link(ins):
                n[0] += 1
                ins.then_inc(step, 1)
                dve.wait_ge(step, n[0])

            link(nc.vector.memset(S.eps_ln[:, :], EPS_LN))
            link(nc.vector.memset(S.eps_n[:, :], EPS_N))
            nc.vector.memset(S.ones[:, :], 1.0).then_inc(consts_ready, 1)
            nc.vector.memset(S.zeros[:, :], 0.0).then_inc(consts_ready, 1)
            nc.vector.memset(S.q_col[:, :], 0.0).then_inc(consts_ready, 1)
            dve.wait_ge(iotas, 3)
            link(nc.vector.tensor_copy(S.iota[:, :], iota_i[:, :]))
            link(nc.vector.tensor_copy(thr[:, :], wi_i[:, :]))
            link(nc.vector.tensor_scalar(thr[:, :], thr[:, :], float(P), None, ALU.mult))
            link(nc.vector.tensor_copy(S.base[:, :], thr[:, 0:NW]))
            link(nc.vector.tensor_single_scalar(part_i[:, :], part_i[:, :], U - 1, ALU.bitwise_and))
            link(nc.vector.tensor_copy(first4[:, :], part_i[:, :]))
            link(nc.vector.tensor_scalar(first4[:, :], first4[:, :], 0.0, None, ALU.is_equal))
            dve.wait_ge(dst_in, 48)
            nc.vector.tensor_copy(nat_f[:, :, :], natural[:, :, :]).then_inc(nat_ready, 1)
            dve.wait_ge(nat_ready, 1)
            dve.wait_ge(shift_in, 48)
            dve.wait_ge(padded, 5)
            link(nc.vector.tensor_copy(t0[:, 0:G - 1], nat_f[:, 0:G - 1, 0]))
            link(nc.vector.tensor_copy(t0[0:LASTG, G - 1:G], nat_f[0:LASTG, G - 1, 0:1]))
            link(nc.vector.tensor_tensor(natural[:, :, :], natural[:, :, :], shifted[:, :, :], ALU.is_gt))
            link(nc.vector.tensor_reduce(viol[:, 0:1], natural[:, :, :], AX.XY, ALU.max))
            nc.vector.memset(viol[:, 1:2], 0.0)
            dve.wait_ge(nat_turned, G)
            nc.vector.memset(natural[:, G - 1, :], 0).then_inc(nat_ready, 1)
            link(nc.vector.tensor_tensor(cmp[:, :, :], t0[:, :].unsqueeze(1).to_broadcast([P, NW + 1, G]),
                                         thr[:, :].unsqueeze(2).to_broadcast([P, NW + 1, G]), ALU.is_lt))
            nc.vector.tensor_reduce(below[:, :], cmp[:, :, :], AX.X, ALU.add).then_inc(tables_in, 1)
            dve.wait_ge(x_in, 32)
            with dve.Fori(0, NW) as w:
                nc.vector.bn_stats(stats[:, bass.ds(w, 1), :], xin[:, bass.ds(w, 1), :])
            nc.vector.memset(rstd[:, :], 0.0).then_inc(norm_ready, 1)
            dve.wait_ge(norm_ready, 1)
            link(nc.vector.tensor_tensor(mv[:, :, :], stats[:, :, 1:3], stats[:, :, 4:6], ALU.add))
            link(nc.vector.tensor_tensor(std[:, :], stats[:, :, 1], stats[:, :, 4], ALU.subtract))
            link(nc.vector.tensor_tensor(nbias[:, :], std[:, :], std[:, :], ALU.mult))
            link(nc.vector.tensor_scalar(mv[:, :, 0], mv[:, :, 0], 0.5, None, ALU.mult))
            link(nc.vector.tensor_scalar(mv[:, :, 1], mv[:, :, 1], 1.0 / D, None, ALU.mult))
            link(nc.vector.scalar_tensor_tensor(mv[:, :, 1], nbias[:, :], 0.25, mv[:, :, 1], ALU.mult, ALU.add))
            nc.vector.memset(rstd[:, :], 0.0).then_inc(var_ready, 1)
            dve.wait_ge(std_ready, 1)
            link(nc.vector.reciprocal(rstd[:, :], std[:, :]))
            link(nc.vector.tensor_tensor(nbias[:, :], mv[:, :, 0], rstd[:, :], ALU.mult))
            nc.vector.tensor_scalar(nbias[:, :], nbias[:, :], -1.0, None, ALU.mult).then_inc(norm_ready, 1)
            dve.wait_ge(src_in, 48)
            dve.wait_ge(columns_ready, 4)
            nc.vector.tensor_copy(nat_f[:, :, :], natural[:, :, :]).then_inc(nat_ready, 1)
            dve.wait_ge(columns_ready, 12)
            link(nc.vector.tensor_single_scalar(lo_i[:, :], S.src_col[:, :], LO - 1, ALU.bitwise_and))
            link(nc.vector.tensor_copy(lo[:, :], lo_i[:, :]))
            link(nc.vector.tensor_single_scalar(lo_i[:, :], S.src_col[:, :], 6, ALU.logical_shift_right))
            link(nc.vector.tensor_copy(hi[:, :], lo_i[:, :]))
            with dve.Fori(0, HN // 2) as i:
                for b in range(2):
                    dve.wait_ge(hist_used, 2 * i + b + 1)
                    at = bass.ds((2 * i + b) * HB, HB)
                    nc.vector.tensor_tensor(one_hi[b][:, :, :], hi[:, at].unsqueeze(2).to_broadcast([P, HB, HI]),
                                            S.iota[:, 0:HI].unsqueeze(1).to_broadcast([P, HB, HI]), ALU.is_equal).then_inc(hist_hi, 1)
                    nc.vector.tensor_tensor(one_lo[b][:, :, :], lo[:, at].unsqueeze(2).to_broadcast([P, HB, LO]),
                                            S.iota[:, 0:LO].unsqueeze(1).to_broadcast([P, HB, LO]), ALU.is_equal).then_inc(hist_lo, 1)
            dve.wait_ge(hist_done, 1)
            nc.vector.tensor_copy(hist[:, :, :], phist[:, :].rearrange("p (w t) -> p t w", t=2)).then_inc(hist_ready, 1)
            link(nc.vector.tensor_copy(S.w3[:, :, 0], S.w_col[:, :]))
            link(nc.vector.tensor_tensor(w_rest[:, :], S.w_col[:, :], S.w3[:, :, 0], ALU.subtract))
            link(nc.vector.tensor_copy(S.w3[:, :, 1], w_rest[:, :]))
            link(nc.vector.tensor_tensor(w_rest[:, :], w_rest[:, :], S.w3[:, :, 1], ALU.subtract))
            nc.vector.tensor_copy(S.w3[:, :, 2], w_rest[:, :]).then_inc(step, 1)
            n[0] += 1
            dve.wait_ge(deg_done, 1)
            nc.vector.tensor_copy(S.deg[:, :], pdeg[:, :]).then_inc(deg_ready, 1)
            dve.wait_ge(tables_summed, 1)
            row = lambda k: rowf[0:1, k, :]
            FIRST, CSS, CES, ALLC, UNS, SRT, T1, T2 = range(8)
            fl = S.sorted_f[0:1, 0:1]
            nf = S.sorted_f[0:1, 1:2]
            link(nc.vector.tensor_copy(row(FIRST), pcnt[0:1, :]))
            link(nc.vector.tensor_scalar(fl, pviol[0:1, 0:1], 0.5, None, ALU.is_lt))
            link(nc.vector.tensor_scalar(nf, fl, -1.0, 1.0, ALU.mult, ALU.add))
            link(nc.vector.tensor_scalar(row(CSS), row(FIRST), -1.0, 0.0, ALU.add, ALU.max))
            link(nc.vector.tensor_scalar(row(CES), row(FIRST), 1.0, None, ALU.max))
            link(nc.vector.tensor_scalar(row(ALLC), thr[0:1, :], float(C) / P, nf, ALU.mult, ALU.mult))
            a, b_ = slice(0, NW), slice(1, NW + 1)
            tab = lambda k: S.tab_f[0:1, k, 0:NW]
            link(nc.vector.memset(S.tab_f[:, :, :], 0.0))
            link(nc.vector.tensor_scalar(rowf[0:1, T1, :], row(CSS), fl, None, ALU.mult))
            link(nc.vector.tensor_tensor(tab(T_CS), rowf[0:1, T1, a], rowf[0:1, ALLC, a], ALU.add))
            link(nc.vector.tensor_scalar(rowf[0:1, T2, :], row(CES), fl, None, ALU.mult))
            link(nc.vector.tensor_tensor(tab(T_CE), rowf[0:1, T2, b_], rowf[0:1, ALLC, b_], ALU.add))
            link(nc.vector.tensor_scalar(tab(T_OFF), thr[0:1, a], 1.0 / P, fl, ALU.mult, ALU.mult))
            link(nc.vector.tensor_scalar(tab(T_REL), tab(T_CE), fl, None, ALU.subtract))
            link(nc.vector.tensor_copy(S.tab_f[0:1, T_REL, NW - 1:NW], S.tab_f[0:1, T_CE, NW - 1:NW]))
            link(nc.vector.tensor_scalar(S.tab_f[0:1, T_RND, 0:1], nf, float((NW - 1) * ROUNDS), float(ROUNDS), ALU.mult, ALU.add))
            link(nc.vector.tensor_copy(S.tab[:, :, :], S.tab_f[:, :, :].rearrange("a k w -> a w k")))

        @block.scalar
        def _(act):
            k = 0
            for a, (cols) in enumerate((S.dst_col, S.w_col, S.src_col)):
                for q in range(4):
                    g0, g1 = 4 * q, min(4 * q + 4, G)
                    act.wait_ge(nat_turned, G * a + g1)
                    c0, c1 = g0 * P, min(g1 * P, TC)
                    nc.scalar.copy(cols[:, c0:c1], pt[k % 2][:, 0:g1 - g0, :].rearrange("p g e -> p (g e)")[:, 0:c1 - c0]).then_inc(columns_ready, 1)
                    k += 1
                if a == 1:
                    act.wait_ge(var_ready, 1)
                    nc.scalar.activation(std[:, :], mv[:, :, 1], ACT.Sqrt, bias=S.eps_ln[:, :]).then_inc(std_ready, 1)
                    act.wait_ge(norm_ready, 2)
                    with act.Fori(0, NW) as w:
                        nc.scalar.activation(xin[:, bass.ds(w, 1), :], xin[:, bass.ds(w, 1), :], ACT.Identity,
                                             bias=nbias[:, bass.ds(w, 1)], scale=rstd[:, bass.ds(w, 1)])
            act.wait_ge(deg_ready, 1)
            for s in range(NW // 7):
                act.wait_ge(row_stored, 16 * s)
                nc.scalar.copy(row1[:, :, 0:D], xin[:, 7 * s:7 * s + 7, :])
                nc.scalar.copy(row1[:, :, D:ROW1], S.deg[:, 7 * s:7 * s + 7].unsqueeze(2)).then_inc(row_made, 1)

        @block.tensor
        def _(pe):
            pe.wait_ge(consts_ready, 5)
            k = 0
            for a, (s, nat) in enumerate(((1, nat_f), (0, nat_w), (3, nat_f))):
                if s:
                    pe.wait_ge(nat_ready, s)
                else:
                    pe.wait_ge(w_in, 48)
                for q in range(4):
                    if k >= 2:
                        pe.wait_ge(columns_ready, k - 1)
                    for g in range(4 * q, min(4 * q + 4, G)):
                        nc.tensor.transpose(pt[k % 2][:, g - 4 * q, :], nat[:, g, :], S.ident[:, :]).then_inc(nat_turned, 1)
                    k += 1
                if a == 1:
                    pe.wait_ge(tables_in, 1)
                    nc.tensor.matmul(pcnt[0:1, :], first4[:, :], below[:, :], start=True, stop=True)
                    nc.tensor.matmul(pviol[0:1, :], S.ones[:, 0:1], viol[:, :], start=True, stop=True).then_inc(tables_summed, 1)
            pe.sem_inc(hist_used, 2)
            nc.tensor.matmul(phist[:, :], S.zeros[:, 0:LO], S.zeros[:, 0:HI], start=True, stop=False)
            with pe.Fori(0, HN // 2) as i:
                for b in range(2):
                    pe.wait_ge(hist_lo, 2 * i + b + 1)
                    pe.wait_ge(hist_w, 2 * i + b + 1)
                    for j in range(HB):
                        last = nc.tensor.matmul(phist[:, :], one_lo[b][:, j, :], w_hi[b][:, j, :], start=False, stop=False)
                    last.then_inc(hist_used, 1)
            nc.tensor.matmul(phist[:, :], S.zeros[:, 0:LO], S.zeros[:, 0:HI], start=False, stop=True).then_inc(hist_done, 1)
            pe.wait_ge(hist_ready, 1)
            nc.tensor.matmul(pdeg[:, :], S.ident[0:LO, :], hist[:, 0, :], start=True, stop=False)
            nc.tensor.matmul(pdeg[:, :], lower[:, :], hist[:, 1, :], start=False, stop=True).then_inc(deg_done, 1)


def gnn_layer(nc, S, table, width, weight, bias, h_out, first, x=None, Wp=None, bp=None, Wg=None, bg=None, x_rows=None):
    with ExitStack() as ctx:
        sb = lambda n, s, d=F32: ctx.enter_context(nc.sbuf_tensor(n, s, d))
        ps = lambda n, s: bank(nc, ctx, n, s)
        t = "a" if first else "b"
        alloc = semaphores(nc, ctx)
        sem = lambda n: alloc(n + t)
        ring = sb("ring" + t, [P, RING * U, width])
        staged = sb("staged" + t, [P, RING * U], I32)
        sel = sb("sel" + t, [P, U, P])
        win = sb("win" + t, [P, P])
        wt = sb("wt" + t, [P, KD, D])
        brow = sb("brow" + t, [1, D])
        agg = sb("agg" + t, [P, D])
        aggT = sb("aggT" + t, [P, KD, P])
        h = sb("h" + t, [P, D])
        if first:
            nodes = sb("nodes", [P, P, U], BF16)
            zero_rows = sb("zero_rows_a", [P, D])
            zero_ready, x_zeroed = sem("zero_ready_a"), sem("x_zeroed")
            near_a, near = sb("near_a", [P, U], BF16), sb("near", [P, U], BF16)
            mark = sb("mark", [P, P, U], BF16)
            w3_here = sb("w3_here", [P, U, 3], BF16)
            hot = sb("hot", [P, 2 * P, U], BF16)
            reach = sb("reach", [P, U, P])
            near_f, dib_w = sb("near_f", [P, U]), sb("dib_w", [P, P])
            di3 = sb("di3", [P, 3])
            dib = sb("dib", [P, 2 * P])
            q4, x4, y4 = sb("q4", [P, U]), sb("x4", [P, U]), sb("y4", [P, 2, U])
            s4, n4 = sb("s4", [P, U]), sb("n4", [P, U])
            p_di = ps("p_di" + t, [P, 3])
            p_dib = ps("p_dib" + t, [P, P])
        p_agg = ps("p_agg" + t, [P, D])
        p_t = ps("p_t" + t, [P, KD, P])
        p_h = ps("p_h" + t, [P, D])
        if not first:
            wp, bprow = sb("wp", [P, KD, D]), sb("bprow", [1, D])
            wg, bgrow = sb("wg", [P, KD, NE]), sb("bgrow", [1, NE])
            hT = sb("hT", [P, KD, P])
            x2w = sb("x2w", [P, D])
            st, mv, sd, rs = sb("st", [P, 6]), sb("mv2", [P, 2]), sb("sd", [P, 1]), sb("rs", [P, 1])
            xn, xnT = sb("xn", [P, D]), sb("xnT", [P, KD, P])
            p_hT, p_o, p_xT, p_g = ps("p_hT", [P, KD, P]), ps("p_o", [P, D]), ps("p_xT", [P, KD, P]), ps("p_g", [P, NE])
            x_pad, x_in = sem("x_pad"), sem("x_in2")
            product_ready, roots_ready, norm_step = sem("product_ready"), sem("roots_ready"), sem("norm_step")
            h_turned, hT_ready, o_done, post = sem("h_turned"), sem("hT_ready"), sem("o_done"), sem("post")
            var_ready, sd_ready, xn_ready = sem("var_ready2"), sem("sd_ready"), sem("xn_ready")
            xn_turned, xnT_ready, gate_done, gate_ready, xn_stored = sem("xn_turned"), sem("xnT_ready"), sem("gate_done"), sem("gate_ready"), sem("xn_stored")

        row_in = [sem(f"row_in{s}_") for s in range(RING)]
        idx_staged, arrived, released = sem("idx_staged"), sem("arrived"), sem("released")
        weights_in = sem("weights_in")
        nodes_ready, dib_here, near_a_ready, near_ready, win_ready, mark_ready, mark_used = sem("nodes_ready"), sem("dib_here"), sem("near_a_ready"), sem("near_ready"), sem("win_ready"), sem("mark_ready"), sem("mark_used")
        di_done, di3_ready, dib_done, dib_ready = sem("di_done"), sem("di3_ready"), sem("dib_done"), sem("dib_ready")
        chain, inverse_ready, share_step = sem("chain"), sem("inverse_ready"), sem("share_step")
        sel_ready, sel_used = sem("sel_ready"), sem("sel_used")
        agg_done, agg_copied, agg_turned, aggT_ready = sem("agg_done"), sem("agg_copied"), sem("agg_turned"), sem("aggT_ready")
        h_done, h_ready, h_stored = sem("h_done"), sem("h_ready"), sem("h_stored")
        block = ctx.enter_context(nc.Block())

        def entries(eng, w, n):
            at = S.tab[0:1, bass.ds(w, 1), 0:n]
            return nc.values_load_multi_w_load_instructions(at, engines=[eng.engine], min_val=0, max_val=NW * C)[1]

        def visits(eng, w):
            return entries(eng, w, 3)

        @block.gpsimd
        def _(pool):
            rounds = pool.value_load(S.tab[0:1, 0, T_RND:T_RND + 1], min_val=ROUNDS, max_val=ROUNDS * NW)

            def stage(g, at):
                s0, s1 = GROUPS[g]
                nc.gpsimd.tensor_copy(staged[:, s0 * U:s1 * U], S.src_col[:, bass.ds(at * (RING * U) + s0 * U, (s1 - s0) * U)]).then_inc(idx_staged, 1)

            stage(0, 0)
            with pool.Fori(0, rounds) as it:
                here = it % ROUNDS
                there = (it + 1) % ROUNDS
                for g, (s0, s1) in enumerate(GROUPS):
                    if g < 3:
                        pool.wait_ge(released, RING * it + GROUPS[g + 1][1])
                        pool.sem_inc(S.pool_turn, 1)
                        stage(g + 1, here)
                    else:
                        pool.wait_ge(released, RING * it + RING + GROUPS[0][1])
                        pool.sem_inc(S.pool_turn, 1)
                        stage(0, there)
                    pool.wait_ge(idx_staged, 4 * it + g + 1)
                    pool.sem_inc(S.pool_turn, 1)
                    for s in range(s0, s1):
                        for j in range(U):
                            k = s * U + j
                            pool.indirect_dma_start(out=ring[:, k, :], out_offset=None, in_=table[:, :],
                                                    in_offset=bass.IndirectOffsetOnAxis(ap=staged[:, k:k + 1], axis=0)).then_inc(row_in[s], 16)

        @block.sync
        def _(sp):
            sp.dma_start(wt[:, :, :], weight.rearrange("(k p) n -> p k n", p=P)).then_inc(weights_in, 16)
            sp.dma_start(brow[:, :], bias.rearrange("(a n) -> a n", a=1)).then_inc(weights_in, 16)
            if first:
                sp.wait_ge(zero_ready, 1)
                sp.dma_start(x_rows.rearrange("(b p) d -> p b d", p=P), zero_rows[:, :].unsqueeze(1).to_broadcast([P, (MAXB + 2) * B // P, D])).then_inc(x_zeroed, 16)
            if not first:
                sp.dma_start(wp[:, :, :], Wp.rearrange("(k p) n -> p k n", p=P)).then_inc(weights_in, 16)
                sp.dma_start(wg[:, :, :], Wg.rearrange("(k p) n -> p k n", p=P)).then_inc(weights_in, 16)
                sp.dma_start(bprow[:, :], bp.rearrange("(a n) -> a n", a=1)).then_inc(weights_in, 16)
                sp.dma_start(bgrow[:, :], bg.rearrange("(a n) -> a n", a=1)).then_inc(weights_in, 16)
                sp.wait_ge(x_pad, 1)
                sp.dma_start(S.x2[:, 0:NW - 1, :], x[0:(NW - 1) * P, :].rearrange("(w p) d -> p w d", p=P)).then_inc(x_in, 16)
                sp.dma_start(S.x2[0:LASTW, NW - 1, :], x[(NW - 1) * P:NODES, :]).then_inc(x_in, 16)
            rounds = sp.value_load(S.tab[0:1, 0, T_RND:T_RND + 1], min_val=ROUNDS, max_val=ROUNDS * NW)
            with sp.Fori(0, rounds) as it:
                for s in range(RING):
                    sp.wait_ge(row_in[s], 16 * U * (it + 1))
                    sp.sem_inc(arrived, 1)
            if first:
                sp.wait_ge(x_zeroed, 16)

        @block.vector
        def _(dve):
            every = lambda cols: cols.unsqueeze(1).to_broadcast([P, P, U])

            def marks(w):
                cs, ce, off = visits(dve, w)
                with dve.Fori(cs, ce) as c:
                    v = c + off
                    here = bass.ds((c % C) * U, U)
                    dve.wait_ge(mark_used, v)
                    nc.vector.tensor_scalar(near_a[:, :], S.dst_col[:, here], S.base[:, bass.ds(w, 1)], None, ALU.subtract).then_inc(near_a_ready, 1)
                    nc.vector.tensor_copy(w3_here[:, :, :], S.w3[:, here, :]).then_inc(mark_ready, 1)
                    dve.wait_ge(near_a_ready, v + 1)
                    nc.vector.tensor_tensor(mark[:, :, :], nodes[:, :, :], every(near_a[:, :]), ALU.is_equal).then_inc(mark_ready, 1)

            def inverses(w):
                cs, ce, off = visits(dve, w)
                dve.wait_ge(dib_ready, w + 1)
                dve.wait_ge(inverse_ready, cs + off)
                nc.vector.tensor_copy(dib_w[:, :], dib[:, bass.ds((w % 2) * P, P)]).then_inc(dib_here, 1)
                dve.wait_ge(dib_here, w + 1)
                dve.sem_inc(S.dve_turn, 1)
                with dve.Fori(cs, ce) as c:
                    v = c + off
                    at = bass.ds((v % 2) * P, P)
                    here = bass.ds((c % C) * U, U)
                    dve.wait_ge(inverse_ready, v)
                    nc.vector.tensor_scalar(near_f[:, :], S.dst_col[:, here], S.base[:, bass.ds(w, 1)], None, ALU.subtract).then_inc(near_ready, 1)
                    nc.vector.tensor_scalar(near[:, :], S.dst_col[:, here], S.base[:, bass.ds(w, 1)], None, ALU.subtract).then_inc(near_ready, 1)
                    dve.wait_ge(arrived, c + 1)
                    dve.sem_inc(S.dve_turn, 1)
                    nc.vector.tensor_copy(S.do_col[:, here].unsqueeze(2), ring[:, bass.ds((c % RING) * U, U), D:ROW1]).then_inc(chain, 1)
                    dve.wait_ge(near_ready, 2 * v + 2)
                    for j in range(U):
                        nc.vector.scalar_tensor_tensor(reach[:, j, :], S.iota[:, :], near_f[:, j:j + 1], dib_w[:, :], ALU.is_equal, ALU.mult,
                                                       accum_out=q4[:, j:j + 1]).then_inc(chain, 1)
                    dve.wait_ge(sel_ready, v * U)
                    nc.vector.tensor_tensor(hot[:, at, :], nodes[:, :, :], every(near[:, :]), ALU.is_equal).then_inc(chain, 1)
                    dve.wait_ge(chain, (U + 5) * v + U + 1)
                    nc.vector.tensor_tensor(x4[:, :], q4[:, :], S.do_col[:, here], ALU.mult).then_inc(chain, 1)
                    nc.vector.tensor_tensor(S.q_col[:, here], S.q_col[:, here], q4[:, :], ALU.add).then_inc(chain, 1)
                    dve.wait_ge(chain, (U + 5) * v + U + 4)
                    nc.vector.tensor_scalar(x4[:, :], x4[:, :], EPS_N, None, ALU.add).then_inc(chain, 1)
                    dve.wait_ge(chain, (U + 5) * v + U + 5)
                    nc.vector.reciprocal(y4[:, bass.ds(v % 2, 1), :], x4[:, :].unsqueeze(1)).then_inc(inverse_ready, 1)

            def window(w):
                cs, ce, off = visits(dve, w)
                dve.wait_ge(sel_ready, U * (cs + off))
                nc.vector.tensor_scalar(win[:, :], S.iota[:, :], S.base[:, bass.ds(w, 1)], None, ALU.add).then_inc(win_ready, 1)
                dve.wait_ge(win_ready, w + 1)
                dve.sem_inc(S.dve_turn, 1)
                with dve.Fori(cs, ce) as c:
                    tile = (c % C) * U
                    v = c + off
                    for j in range(U):
                        dve.wait_ge(sel_used, v * U + j + 1)
                        nc.vector.tensor_scalar(sel[:, j, :], win[:, :], S.dst_col[:, bass.ds(tile + j, 1)],
                                                S.q_col[:, bass.ds(tile + j, 1)], ALU.is_equal, ALU.mult).then_inc(sel_ready, 1)

            def residual(w):
                dve.wait_ge(o_done, w + 1)
                nc.vector.tensor_tensor(x2w[:, :].unsqueeze(1), p_o.unsqueeze(1), S.x2[:, bass.ds(w, 1), :], ALU.add).then_inc(post, 1)
                dve.wait_ge(post, 5 * w + 1)
                dve.sem_inc(S.dve_turn, 1)
                nc.vector.tensor_copy(S.x2[:, bass.ds(w, 1), :], x2w[:, :].unsqueeze(1)).then_inc(post, 1)
                nc.vector.bn_stats(st[:, :], x2w[:, :]).then_inc(post, 1)
                dve.wait_ge(post, 5 * w + 3)
                dve.sem_inc(S.dve_turn, 1)
                nc.vector.bn_aggr(mv[:, :], st[:, :]).then_inc(var_ready, 1)
                dve.wait_ge(sd_ready, w + 1)
                nc.vector.reciprocal(rs[:, :], sd[:, :]).then_inc(post, 1)
                dve.wait_ge(post, 5 * w + 4)
                dve.wait_ge(xn_stored, 16 * w)
                dve.wait_ge(xn_turned, KD * w)
                dve.sem_inc(S.dve_turn, 1)
                nc.vector.tensor_scalar(xn[:, :], x2w[:, :], mv[:, 0:1], rs[:, 0:1], ALU.subtract, ALU.mult).then_inc(xn_ready, 1)
                dve.wait_ge(xn_ready, w + 1)
                dve.sem_inc(post, 1)

            if first:
                nc.vector.memset(zero_rows[:, :], 0.0).then_inc(zero_ready, 1)
                nc.vector.tensor_copy(nodes[:, :, :], S.iota[:, :].unsqueeze(2).to_broadcast([P, P, U])).then_inc(nodes_ready, 1)
                dve.wait_ge(nodes_ready, 1)
                marks(0)
                with dve.Fori(0, NW - 1) as w:
                    marks(w + 1)
                    inverses(w)
                inverses(NW - 1)
            else:
                nc.vector.tensor_tensor(S.q_col[:, :], S.q_col[:, :], S.do_col[:, :], ALU.mult).then_inc(product_ready, 1)
                dve.wait_ge(roots_ready, 1)
                nc.vector.reciprocal(S.q_col[:, :], S.q_col[:, :]).then_inc(norm_step, 1)
                dve.wait_ge(norm_step, 1)
                nc.vector.tensor_tensor(S.q_col[:, :], S.q_col[:, :], S.w_col[:, :], ALU.mult).then_inc(norm_step, 1)
                dve.wait_ge(norm_step, 2)
                nc.vector.memset(S.x2[:, NW - 1, :], 0.0).then_inc(x_pad, 1)
                dve.wait_ge(x_in, 32)
                window(0)
                with dve.Fori(1, NW) as w:
                    window(w)
                    residual(w - 1)
                residual(NW - 1)

        @block.tensor
        def _(pe):
            pe.sem_inc(sel_used, U)
            pe.sem_inc(released, RING)
            pe.wait_ge(weights_in, 32 if first else 96)

            def count(w):
                cs, ce, off = visits(pe, w)
                nc.tensor.matmul(p_di[:, :], S.zeros[:, 0:P], S.zeros[:, 0:3], start=True, stop=False)
                with pe.Fori(cs, ce) as c:
                    pe.wait_ge(mark_ready, 2 * (c + off) + 2)
                    for j in range(U):
                        last = nc.tensor.matmul(p_di[:, :], mark[:, :, j], w3_here[:, j, :], start=False, stop=False)
                    last.then_inc(mark_used, 1)
                nc.tensor.matmul(p_di[:, :], S.zeros[:, 0:P], S.zeros[:, 0:3], start=False, stop=True).then_inc(di_done, 1)

            def spread(w):
                pe.wait_ge(di3_ready, w + 1)
                for k in range(3):
                    last = nc.tensor.matmul(p_dib[:, :], di3[:, k:k + 1].to_broadcast([P, P]), S.ident[:, :], start=k == 0, stop=k == 2)
                last.then_inc(dib_done, 1)

            def window(w):
                cs, ce, off, rel = entries(pe, w, 4)
                nc.tensor.matmul(p_agg[:, :], S.zeros[:, 0:P], S.zeros[:, 0:D], start=True, stop=False)
                ahead = U if first else 0
                with pe.Fori(cs, ce) as c:
                    slot = (c % RING) * U
                    v = c + off
                    pe.wait_ge(arrived, c + 1)
                    for j in range(U):
                        pe.wait_ge(sel_ready, v * U + j + 1 + ahead)
                        nc.tensor.matmul(p_agg[:, :], sel[:, j, :], ring[:, bass.ds(slot + j, 1), 0:D], start=False, stop=False).then_inc(sel_used, 1)
                    with pe.If(c < rel):
                        nc.tensor.matmul(p_agg[:, 0:1], S.zeros[:, 0:P], S.zeros[:, 0:1], start=False, stop=False).then_inc(released, 1)
                nc.tensor.matmul(p_agg[:, :], S.zeros[:, 0:P], S.zeros[:, 0:D], start=False, stop=True).then_inc(agg_done, 1)

            def turn(w):
                pe.wait_ge(agg_copied, w + 1)
                for k in range(KD):
                    nc.tensor.transpose(p_t[:, k, :], agg[:, k * P:(k + 1) * P], S.ident[:, :]).then_inc(agg_turned, 1)

            def dense(w):
                pe.wait_ge(aggT_ready, w + 1)
                pe.wait_ge(h_ready, w)
                nc.tensor.matmul(p_h[:, :], S.ones[0:1, :], brow[:, :], start=True, stop=False)
                for k in range(KD):
                    last = nc.tensor.matmul(p_h[:, :], aggT[:, k, :], wt[:, k, :], start=False, stop=k == KD - 1)
                last.then_inc(h_done, 1)

            def project(w):
                pe.wait_ge(h_ready, w + 1)
                for k in range(KD):
                    nc.tensor.transpose(p_hT[:, k, :], h[:, k * P:(k + 1) * P], S.ident[:, :]).then_inc(h_turned, 1)
                pe.wait_ge(hT_ready, w + 1)
                nc.tensor.matmul(p_o[:, :], S.ones[0:1, :], bprow[:, :], start=True, stop=False)
                for k in range(KD):
                    last = nc.tensor.matmul(p_o[:, :], hT[:, k, :], wp[:, k, :], start=False, stop=k == KD - 1)
                last.then_inc(o_done, 1)

            def gate(w):
                pe.wait_ge(xn_ready, w + 1)
                for k in range(KD):
                    nc.tensor.transpose(p_xT[:, k, :], xn[:, k * P:(k + 1) * P], S.ident[:, :]).then_inc(xn_turned, 1)
                pe.wait_ge(xnT_ready, w + 1)
                nc.tensor.matmul(p_g[:, :], S.ones[0:1, :], bgrow[:, :], start=True, stop=False)
                for k in range(KD):
                    last = nc.tensor.matmul(p_g[:, :], xnT[:, k, :], wg[:, k, :], start=False, stop=k == KD - 1)
                last.then_inc(gate_done, 1)

            if first:
                count(0)
                spread(0)
                count(1)
                spread(1)
                window(0)
                with pe.Fori(1, NW - 1) as w:
                    count(w + 1)
                    turn(w - 1)
                    spread(w + 1)
                    dense(w - 1)
                    window(w)
                turn(NW - 2)
                dense(NW - 2)
                window(NW - 1)
                turn(NW - 1)
                dense(NW - 1)
            else:
                def whole(w):
                    window(w)
                    turn(w)
                    dense(w)
                    project(w)

                whole(0)
                with pe.Fori(1, NW) as w:
                    whole(w)
                    gate(w - 1)
                gate(NW - 1)

        @block.scalar
        def _(act):
            def parts(w):
                act.wait_ge(di_done, w + 1)
                nc.scalar.copy(di3[:, :], p_di[:, :]).then_inc(di3_ready, 1)

            def spread(w):
                act.wait_ge(dib_done, w + 1)
                nc.scalar.copy(dib[:, bass.ds((w % 2) * P, P)], p_dib[:, :]).then_inc(dib_ready, 1)

            def selections(w):
                cs, ce, off = visits(act, w)
                with act.Fori(cs, ce) as c:
                    tile = (c % C) * U
                    v = c + off
                    at = bass.ds((v % 2) * P, P)
                    act.wait_ge(inverse_ready, v + 1)
                    nc.scalar.activation(s4[:, :].unsqueeze(1), y4[:, bass.ds(v % 2, 1), :], ACT.Sqrt).then_inc(share_step, 1)
                    act.wait_ge(share_step, (U + 1) * v + 1)
                    act.wait_ge(sel_ready, (v + 1) * U)
                    for j in range(U):
                        nc.scalar.activation(n4[:, j:j + 1], s4[:, j:j + 1], ACT.Copy, scale=S.w_col[:, bass.ds(tile + j, 1)]).then_inc(share_step, 1)
                    act.wait_ge(share_step, (U + 1) * (v + 1))
                    for j in range(U):
                        act.wait_ge(sel_used, v * U + j + 1)
                        nc.scalar.activation(sel[:, j:j + 1, :], hot[:, at, j].unsqueeze(1), ACT.Copy, scale=n4[:, j:j + 1]).then_inc(sel_ready, 1)

            def summed(w):
                act.wait_ge(agg_done, w + 1)
                nc.scalar.copy(agg[:, :], p_agg[:, :]).then_inc(agg_copied, 1)

            def turned(w):
                act.wait_ge(agg_turned, KD * (w + 1))
                nc.scalar.copy(aggT[:, :, :], p_t[:, :, :]).then_inc(aggT_ready, 1)

            def hidden(w):
                act.wait_ge(h_done, w + 1)
                if first:
                    act.wait_ge(h_stored, 16 * w)
                    nc.scalar.activation(h[:, :], p_h[:, :], ACT.Relu).then_inc(h_ready, 1)
                    act.wait_ge(h_ready, w + 1)
                    act.dma_start(h_out[bass.ds(w * P, P), :], h[:, :]).then_inc(h_stored, 16)
                else:
                    nc.scalar.activation(h[:, :], p_h[:, :], ACT.Relu).then_inc(h_ready, 1)
                    act.wait_ge(h_turned, KD * (w + 1))
                    nc.scalar.copy(hT[:, :, :], p_hT[:, :, :]).then_inc(hT_ready, 1)

            def deviation(w):
                act.wait_ge(var_ready, w + 1)
                nc.scalar.activation(sd[:, :], mv[:, 1:2], ACT.Sqrt, bias=S.eps_ln[:, :]).then_inc(sd_ready, 1)

            def gate(w):
                act.wait_ge(xn_ready, w + 1)
                act.dma_start(h_out[bass.ds(w * P, P), :], xn[:, :]).then_inc(xn_stored, 16)
                act.wait_ge(xn_turned, KD * (w + 1))
                nc.scalar.copy(xnT[:, :, :], p_xT[:, :, :]).then_inc(xnT_ready, 1)
                act.wait_ge(gate_done, w + 1)
                nc.scalar.copy(S.logits[:, bass.ds(w, 1), :], p_g[:, :].unsqueeze(1)).then_inc(gate_ready, 1)

            if first:
                act.sem_inc(sel_ready, U)
                for w in range(2):
                    parts(w)
                    spread(w)
                selections(0)
                with act.Fori(1, NW - 1) as w:
                    summed(w - 1)
                    parts(w + 1)
                    turned(w - 1)
                    spread(w + 1)
                    selections(w)
                    hidden(w - 1)
                summed(NW - 2)
                turned(NW - 2)
                selections(NW - 1)
                hidden(NW - 2)
                summed(NW - 1)
                turned(NW - 1)
                hidden(NW - 1)
                act.wait_ge(h_stored, 16 * NW)
            else:
                act.wait_ge(product_ready, 1)
                nc.scalar.activation(S.q_col[:, :], S.q_col[:, :], ACT.Sqrt, bias=S.eps_n[:, :]).then_inc(roots_ready, 1)

                def dense(w):
                    summed(w)
                    turned(w)
                    hidden(w)

                dense(0)
                with act.Fori(1, NW) as w:
                    deviation(w - 1)
                    dense(w)
                    gate(w - 1)
                deviation(NW - 1)
                gate(NW - 1)
                act.wait_ge(xn_stored, 16 * NW)


def route(nc, S, xn_rows, x_rows, y_rows):
    with ExitStack() as ctx:
        sb = lambda n, s, d=F32: ctx.enter_context(nc.sbuf_tensor(n, s, d))
        ps = lambda n, s: bank(nc, ctx, n, s)
        sem = semaphores(nc, ctx)
        TOK = [P, NW, NE]
        one1, one2, both, score, rest, place = (sb(n, TOK) for n in ("one1", "one2", "both", "score", "rest", "place"))
        total, upto = sb("total", TOK), sb("upto", TOK)
        m1, m2, top, ex = (sb(n, [P, NW]) for n in ("m1", "m2", "top", "ex"))
        prio, region = sb("prio", [P, NE]), sb("region", [P, NE])
        ones_nw = sb("ones_nw", [P, NW])
        pos_f = sb("pos_f", [P, NW, 2])
        before = sb("before", [P, P])
        count_i = sb("count_i", [P, NE], I32)
        batch = sb("batch", [P, 3, NE])
        zero_rows = sb("zero_rows", [P, D])
        tile = [sb(f"tile{s}", [P, D]) for s in range(LW)]
        staged = sb("staged_d", [P, LW, 2], I32)
        p_rank, p_total = ps("p_rank", TOK), ps("p_total", TOK)
        before_ready, step, d_ready, e_ready = sem("before_ready"), sem("step_d"), sem("d_ready"), sem("e_ready")
        both_ready, ranked, pos_ready, zero_ready = sem("both_ready"), sem("ranked"), sem("pos_ready"), sem("zero_ready")
        tile_in = [sem(f"tile_in{s}") for s in range(LW)]
        tile_out = [sem(f"tile_out{s}") for s in range(LW)]
        idx_staged, y_zeroed, etab_ready = sem("idx_staged_d"), sem("y_zeroed"), sem("etab_ready")
        block = ctx.enter_context(nc.Block())

        @block.vector
        def _(dve):
            n = [0]

            def link(ins):
                n[0] += 1
                ins.then_inc(step, 1)
                dve.wait_ge(step, n[0])

            wide = lambda t: t[:, :].unsqueeze(2).to_broadcast(TOK)
            per = lambda t: t[:, :].unsqueeze(1).to_broadcast(TOK)
            nc.vector.memset(zero_rows[:, :], 0.0).then_inc(zero_ready, 1)
            link(nc.vector.memset(ones_nw[:, :], 1.0))
            link(nc.vector.tensor_scalar(prio[:, :], S.iota[:, 0:NE], -1.0, float(NE), ALU.mult, ALU.add))
            for logits, m, one in ((S.logits, m1, one1), (rest, m2, one2)):
                link(nc.vector.tensor_reduce(m[:, :], logits[:, :, :], AX.X, ALU.max))
                link(nc.vector.tensor_tensor(score[:, :, :], logits[:, :, :], wide(m), ALU.is_equal))
                link(nc.vector.tensor_tensor(score[:, :, :], score[:, :, :], per(prio), ALU.mult))
                link(nc.vector.tensor_reduce(top[:, :], score[:, :, :], AX.X, ALU.max))
                link(nc.vector.tensor_tensor(one[:, :, :], score[:, :, :], wide(top), ALU.is_equal))
                if one is one1:
                    link(nc.vector.scalar_tensor_tensor(rest[:, :, :], one1[:, :, :], -3e38, S.logits[:, :, :], ALU.mult, ALU.add))
            nc.vector.tensor_tensor(both[:, :, :], one1[:, :, :], one2[:, :, :], ALU.add).then_inc(both_ready, 1)
            nc.vector.tensor_tensor(m2[:, :], m2[:, :], m1[:, :], ALU.subtract).then_inc(d_ready, 1)
            dve.wait_ge(e_ready, 1)
            link(nc.vector.tensor_scalar(m1[:, :], ex[:, :], 1.0, None, ALU.add))
            link(nc.vector.reciprocal(S.share[:, :, 0], m1[:, :]))
            link(nc.vector.tensor_tensor(S.share[:, :, 1], ex[:, :], S.share[:, :, 0], ALU.mult))
            dve.wait_ge(ranked, 1)
            link(nc.vector.tensor_copy(total[:, :, :], p_total[:, :, :]))
            for e in range(NE):
                last = nc.vector.tensor_tensor_scan(upto[:, :, e], ones_nw[:, :], total[:, :, e], 0.0, ALU.mult, ALU.add)
                if e < NE - 1:
                    last.then_inc(pos_ready, 1)
            link(last)
            dve.wait_ge(pos_ready, NE - 1)
            link(nc.vector.tensor_scalar(batch[:, 0, :], upto[:, NW - 1, :], float(B - 1), None, ALU.add))
            link(nc.vector.tensor_copy(count_i[:, :], batch[:, 0, :]))
            link(nc.vector.tensor_single_scalar(count_i[:, :], count_i[:, :], 8, ALU.logical_shift_right))
            link(nc.vector.tensor_copy(batch[:, 0, :], count_i[:, :]))
            link(nc.vector.tensor_scalar(batch[:, 0, :], batch[:, 0, :], 1.0, None, ALU.max))
            link(nc.vector.tensor_tensor_scan(batch[:, 1, :], ones_nw[:, 0:NE], batch[:, 0, :], 0.0, ALU.mult, ALU.add))
            link(nc.vector.tensor_tensor(batch[:, 2, :], batch[:, 1, :], batch[:, 0, :], ALU.subtract))
            link(nc.vector.tensor_scalar(region[:, :], batch[:, 2, :], float(B), None, ALU.mult))
            link(nc.vector.tensor_copy(S.etab[0:1, 1, :], batch[0:1, 1, :]))
            nc.vector.tensor_copy(S.etab[0:1, 0, :], batch[0:1, 2, :]).then_inc(etab_ready, 1)
            link(nc.vector.tensor_tensor(place[:, :, :], upto[:, :, :], total[:, :, :], ALU.subtract))
            link(nc.vector.tensor_tensor(place[:, :, :], place[:, :, :], p_rank[:, :, :], ALU.add))
            link(nc.vector.tensor_tensor(place[:, :, :], place[:, :, :], per(region), ALU.add))
            for k, one in enumerate((one1, one2)):
                link(nc.vector.tensor_tensor(score[:, :, :], place[:, :, :], one[:, :, :], ALU.mult))
                link(nc.vector.tensor_reduce(pos_f[:, :, k], score[:, :, :], AX.X, ALU.add))
            nc.vector.tensor_copy(S.pos[:, :, :], pos_f[:, :, :]).then_inc(pos_ready, 1)

        @block.scalar
        def _(act):
            act.wait_ge(d_ready, 1)
            nc.scalar.activation(ex[:, :], m2[:, :], ACT.Exp).then_inc(e_ready, 1)

        @block.tensor
        def _(pe):
            pe.wait_ge(before_ready, 2)
            pe.wait_ge(both_ready, 1)
            nc.tensor.matmul(p_rank[:, :, :], before[:, :], both[:, :, :], start=True, stop=True)
            nc.tensor.matmul(p_total[:, :, :], S.ones[:, :], both[:, :, :], start=True, stop=True).then_inc(ranked, 1)

        @block.sync
        def _(sp):
            sp.wait_ge(zero_ready, 1)
            sp.wait_ge(etab_ready, 1)
            used = sp.value_load(S.etab[0:1, 1, NE - 1:NE], min_val=NE, max_val=MAXB)
            with sp.Fori(used, MAXB + 1) as g:
                for k in range(B // P):
                    sp.dma_start(y_rows[bass.ds(g * B + k * P, P), :], zero_rows[:, :]).then_inc(y_zeroed, 16)
            with sp.Fori(0, LW) as i:
                for s in range(LW):
                    sp.wait_ge(tile_out[s], 32 * i)
                    sp.dma_start(tile[s][:, :], xn_rows[bass.ds((i * LW + s) * P, P), :]).then_inc(tile_in[s], 16)
            with sp.Fori(0, used) as g:
                sp.sem_inc(y_zeroed, 16 * B // P)
            sp.wait_ge(y_zeroed, 16 * B // P * (MAXB + 1))

        @block.gpsimd
        def _(pool):
            nc.gpsimd.memset(before[:, :], 1.0).then_inc(before_ready, 1)
            pool.wait_ge(before_ready, 1)
            pool.affine_select(out=before[:, :], in_=before[:, :], compare_op=ALU.is_gt, fill=0.0, base=0,
                               pattern=[[1, P]], channel_multiplier=-1).then_inc(before_ready, 1)
            pool.wait_ge(pos_ready, NE)
            with pool.Fori(0, LW) as i:
                for s in range(LW):
                    pool.wait_ge(tile_out[s], 32 * i)
                    pool.sem_inc(S.pool_turn, 1)
                nc.gpsimd.tensor_copy(staged[:, :, :], S.pos[:, bass.ds(i * LW, LW), :]).then_inc(idx_staged, 1)
                pool.wait_ge(idx_staged, i + 1)
                pool.sem_inc(S.pool_turn, 1)
                for s in range(LW):
                    pool.wait_ge(tile_in[s], 16 * i + 16)
                    pool.sem_inc(S.pool_turn, 1)
                    for k in range(2):
                        pool.indirect_dma_start(out=x_rows[:, :], out_offset=bass.IndirectOffsetOnAxis(ap=staged[:, s, k:k + 1], axis=0),
                                                in_=tile[s][:, :], in_offset=None).then_inc(tile_out[s], 16)
            for s in range(LW):
                pool.wait_ge(tile_out[s], 32 * LW)


def experts(nc, S, x_rows, y_rows, W1, b1, W2, b2):
    HALVES = B // P
    with ExitStack() as ctx:
        sb = lambda n, s, d=F32: ctx.enter_context(nc.sbuf_tensor(n, s, d))
        ps = lambda n, s: bank(nc, ctx, n, s)
        sem = semaphores(nc, ctx)
        w1 = [sb(f"w1_{p}", [P, KD, H]) for p in range(2)]
        w2 = [sb(f"w2_{p}", [P, KH, D]) for p in range(2)]
        b1n, b1T = sb("b1n", [NE * KH, P]), sb("b1T", [P, NE * KH])
        b2b = sb("b2b", [P, NE, D])
        xb, xT = sb("xb", [P, HALVES, D]), sb("xT", [P, KD, B])
        hid = sb("hid", [P, KH, B])
        y = sb("y", [P, HALVES, D])
        p_x, p_b = ps("p_x", [P, KD, B]), ps("p_b", [P, NE * KH])
        p_y = [ps(f"p_y{t}", [P, D]) for t in range(HALVES)]
        p_h = [ps(f"p_hid{i}", [P, B]) for i in range(4)]
        w_in = [sem(f"w_in{p}") for p in range(2)]
        w_used, bias_in, b1_turned, b1_ready = sem("w_used"), sem("bias_in"), sem("b1_turned"), sem("b1_ready")
        x_in, x_turned, xT_ready, hid_done, hid_ready = sem("x_in3"), sem("x_turned"), sem("xT_ready"), sem("hid_done"), sem("hid_ready")
        y_done, y_ready, y_stored = sem("y_done"), sem("y_ready"), sem("y_stored")
        TURNS = KD * HALVES
        block = ctx.enter_context(nc.Block())

        def batches(eng, e):
            return (eng.value_load(S.etab[0:1, 0, bass.ds(e, 1)], min_val=0, max_val=MAXB - 1),
                    eng.value_load(S.etab[0:1, 1, bass.ds(e, 1)], min_val=1, max_val=MAXB))

        def used(eng):
            return eng.value_load(S.etab[0:1, 1, NE - 1:NE], min_val=NE, max_val=MAXB)

        @block.sync
        def _(sp):
            sp.dma_start(b1n[:, :], b1.rearrange("e (k p) -> (e k) p", p=P)).then_inc(bias_in, 16)
            sp.dma_start(b2b[:, :, :], b2.rearrange("e d -> (e d)").partition_broadcast(P)).then_inc(bias_in, 16)
            with sp.Fori(0, used(sp) + 1) as g:
                sp.wait_ge(x_turned, TURNS * g)
                sp.dma_start(xb[:, :, :], x_rows[bass.ds(g * B, B), :].rearrange("(t p) d -> p t d", p=P)).then_inc(x_in, 16)

        @block.scalar
        def _(act):
            act.wait_ge(b1_turned, 1)
            nc.scalar.copy(b1T[:, :], p_b).then_inc(b1_ready, 1)
            act.wait_ge(b1_ready, 1)
            with act.Fori(0, NE) as e:
                g0, g1 = batches(act, e)
                with act.Fori(g0, g1) as g:
                    act.wait_ge(y_done, g)
                    for k in range(KH):
                        act.wait_ge(hid_done, g * KH + k + 1)
                        nc.scalar.activation(hid[:, k, :], p_h[k % 4], ACT.Gelu, bias=b1T[:, bass.ds(e * KH + k, 1)]).then_inc(hid_ready, 1)

        @block.tensor
        def _(pe):
            def turn(g):
                pe.wait_ge(x_in, 16 * (g + 1))
                for t in range(HALVES):
                    for k in range(KD):
                        nc.tensor.transpose(p_x[:, k, t * P:(t + 1) * P], xb[:, t, k * P:(k + 1) * P], S.ident[:, :]).then_inc(x_turned, 1)

            pe.sem_inc(w_used, 1)
            pe.wait_ge(bias_in, 32)
            nc.tensor.transpose(p_b, b1n[:, :], S.ident[0:NE * KH, 0:NE * KH]).then_inc(b1_turned, 1)
            turn(0)
            with pe.Fori(0, NE // 2) as pair:
                for p in range(2):
                    g0, g1 = batches(pe, pair * 2 + p)
                    pe.wait_ge(w_in[p], 32 * (pair + 1))
                    pe.sem_inc(S.pe_turn, 1)
                    with pe.Fori(g0, g1) as g:
                        pe.wait_ge(xT_ready, g + 1)
                        for k in range(KH):
                            if k >= 4:
                                pe.wait_ge(hid_ready, g * KH + k - 3)
                            for d in range(KD):
                                last = nc.tensor.matmul(p_h[k % 4], w1[p][:, d, k * P:(k + 1) * P], xT[:, d, :], start=d == 0, stop=d == KD - 1)
                            last.then_inc(hid_done, 1)
                        turn(g + 1)
                        pe.wait_ge(y_ready, HALVES * g)
                        for k in range(KH):
                            pe.wait_ge(hid_ready, g * KH + k + 1)
                            for t in range(HALVES):
                                last = nc.tensor.matmul(p_y[t], hid[:, k, t * P:(t + 1) * P], w2[p][:, k, :], start=k == 0, stop=k == KH - 1)
                        last.then_inc(y_done, 1)
                    nc.tensor.matmul(p_b[:, 0:1], S.zeros[:, 0:P], S.zeros[:, 0:1], start=True, stop=True).then_inc(w_used, 1)

        @block.vector
        def _(dve):
            dve.wait_ge(x_turned, TURNS)
            nc.vector.tensor_copy(xT[:, :, :], p_x[:, :, :]).then_inc(xT_ready, 1)
            with dve.Fori(0, NE) as e:
                g0, g1 = batches(dve, e)
                with dve.Fori(g0, g1) as g:
                    dve.wait_ge(x_turned, TURNS * (g + 2))
                    dve.sem_inc(S.dve_turn, 1)
                    nc.vector.tensor_copy(xT[:, :, :], p_x[:, :, :]).then_inc(xT_ready, 1)
                    dve.wait_ge(y_done, g + 1)
                    dve.wait_ge(y_stored, 16 * g)
                    dve.sem_inc(S.dve_turn, 1)
                    for t in range(HALVES):
                        nc.vector.tensor_tensor(y[:, t:t + 1, :], p_y[t].unsqueeze(1), b2b[:, bass.ds(e, 1), :], ALU.add).then_inc(y_ready, 1)

        @block.gpsimd
        def _(pool):
            def load(e, p):
                pool.wait_ge(w_used, e)
                pool.sem_inc(S.pool_turn, 1)
                pool.dma_start(w1[p][:, :, :], W1[bass.ds(e, 1), :, :].rearrange("a (k p) n -> p (a k) n", p=P)).then_inc(w_in[p], 16)
                pool.dma_start(w2[p][:, :, :], W2[bass.ds(e, 1), :, :].rearrange("a (k p) n -> p (a k) n", p=P)).then_inc(w_in[p], 16)

            def store(e):
                g0, g1 = batches(pool, e)
                with pool.Fori(g0, g1) as g:
                    pool.wait_ge(y_ready, HALVES * (g + 1))
                    pool.sem_inc(S.pool_turn, 1)
                    pool.dma_start(y_rows[bass.ds(g * B, B), :].rearrange("(t p) d -> p t d", p=P), y[:, :, :]).then_inc(y_stored, 16)

            pool.dma_start(w1[0][:, :, :], W1[0, :, :].rearrange("(k p) n -> p k n", p=P)).then_inc(w_in[0], 16)
            pool.dma_start(w2[0][:, :, :], W2[0, :, :].rearrange("(k p) n -> p k n", p=P)).then_inc(w_in[0], 16)
            with pool.Fori(0, NE // 2 - 1) as pair:
                for p in range(2):
                    load(pair * 2 + p + 1, 1 - p)
                    store(pair * 2 + p)
            load(NE - 1, 1)
            store(NE - 2)
            store(NE - 1)
            pool.wait_ge(y_stored, 16 * used(pool))
            pool.sem_inc(S.pool_turn, 1)


def combine(nc, S, y_rows, out):
    with ExitStack() as ctx:
        sb = lambda n, s, d=F32: ctx.enter_context(nc.sbuf_tensor(n, s, d))
        sem = semaphores(nc, ctx)
        rows = [[sb(f"rows{s}_{k}", [P, D]) for k in range(2)] for s in range(LW)]
        part = [sb(f"part{s}", [P, D]) for s in range(LW)]
        res = [sb(f"res{s}", [P, D]) for s in range(LW)]
        staged = sb("staged_f", [P, LW, 2], I32)
        row_in = [sem(f"row_in_f{s}") for s in range(LW)]
        summed, stored, idx_staged, half = sem("summed"), [sem(f"stored{s}") for s in range(LW)], sem("idx_staged_f"), sem("half")
        block = ctx.enter_context(nc.Block())

        @block.gpsimd
        def _(pool):
            with pool.Fori(0, LW) as i:
                for s in range(LW):
                    pool.wait_ge(row_in[s], 32 * i)
                    pool.sem_inc(S.pool_turn, 1)
                nc.gpsimd.tensor_copy(staged[:, :, :], S.pos[:, bass.ds(i * LW, LW), :]).then_inc(idx_staged, 1)
                pool.wait_ge(idx_staged, i + 1)
                pool.sem_inc(S.pool_turn, 1)
                for s in range(LW):
                    pool.wait_ge(summed, LW * i + s + 1)
                    pool.sem_inc(S.pool_turn, 1)
                    for k in range(2):
                        pool.indirect_dma_start(out=rows[s][k][:, :], out_offset=None, in_=y_rows[:, :],
                                                in_offset=bass.IndirectOffsetOnAxis(ap=staged[:, s, k:k + 1], axis=0)).then_inc(row_in[s], 16)

        @block.vector
        def _(dve):
            dve.sem_inc(summed, LW)
            with dve.Fori(0, LW) as i:
                for s in range(LW):
                    w = i * LW + s
                    dve.wait_ge(row_in[s], 32 * i + 32)
                    dve.sem_inc(S.dve_turn, 1)
                    nc.vector.scalar_tensor_tensor(part[s][:, :].unsqueeze(1), rows[s][0][:, :].unsqueeze(1), S.share[:, bass.ds(w, 1), 0],
                                                   S.x2[:, bass.ds(w, 1), :], ALU.mult, ALU.add).then_inc(half, 1)
                    dve.wait_ge(half, w + 1)
                    dve.wait_ge(stored[s], 16 * i)
                    dve.sem_inc(S.dve_turn, 1)
                    nc.vector.scalar_tensor_tensor(res[s][:, :], rows[s][1][:, :], S.share[:, bass.ds(w, 1), 1],
                                                   part[s][:, :], ALU.mult, ALU.add).then_inc(summed, 1)

        @block.sync
        def _(sp):
            with sp.Fori(0, LW - 1) as i:
                for s in range(LW):
                    w = i * LW + s
                    sp.wait_ge(summed, LW + w + 1)
                    sp.dma_start(out[bass.ds(w * P, P), :], res[s][:, :]).then_inc(stored[s], 16)
            for s in range(LW):
                w = (LW - 1) * LW + s
                n = min(P, NODES - w * P)
                sp.wait_ge(summed, LW + w + 1)
                sp.dma_start(out[w * P:w * P + n, :], res[s][0:n, :]).then_inc(stored[s], 16)
            for s in range(LW):
                sp.wait_ge(stored[s], 16 * LW)


class Shared:
    pass


def build(nc, x, src, dst, edge_weight, W6, b6, W7, b7, Wp, bp, Wg, bg, W1, b1, W2, b2, out):
    rows1 = nc.dram_tensor("rows1", [PADN, ROW1], F32).ap()
    h6 = nc.dram_tensor("h6", [PADN, D], F32).ap()
    xn_rows = nc.dram_tensor("xn_rows", [PADN, D], F32).ap()
    x_rows = nc.dram_tensor("x_rows", [(MAXB + 2) * B, D], F32).ap()
    y_rows = nc.dram_tensor("y_rows", [(MAXB + 1) * B, D], F32).ap()
    S = Shared()
    with ExitStack() as ctx:
        sb = lambda n, s, d=F32: ctx.enter_context(nc.sbuf_tensor(n, s, d))
        S.pool_turn = ctx.enter_context(nc.semaphore("pool_turn"))
        S.pe_turn = ctx.enter_context(nc.semaphore("pe_turn"))
        S.dve_turn = ctx.enter_context(nc.semaphore("dve_turn"))
        S.src_col = sb("src_col", [P, TC], I32)
        S.dst_col = sb("dst_col", [P, TC])
        S.w_col = sb("w_col", [P, TC])
        S.q_col = sb("q_col", [P, TC])
        S.do_col = sb("do_col", [P, TC])
        S.ident = sb("ident", [P, P])
        S.ones = sb("ones", [P, P])
        S.zeros = sb("zeros", [P, D], BF16)
        S.iota = sb("iota", [P, P])
        S.base = sb("base", [P, NW])
        S.eps_ln = sb("eps_ln", [P, 1])
        S.eps_n = sb("eps_n", [P, 1])
        S.deg = sb("deg", [P, NW])
        S.sorted_f = sb("sorted_f", [1, 2])
        S.tab_f = sb("tab_f", [1, 5, NW + 1])
        S.tab = sb("tab", [1, NW + 1, 5], I32)
        with nc.sbuf_tensor("w3", [P, TC, 3], BF16) as S.w3:
            load_edges_and_histogram(nc, x, src, dst, edge_weight, S, rows1)
            gnn_layer(nc, S, rows1, ROW1, W6, b6, h6, True, x_rows=x_rows)
        S.x2 = sb("x2", [P, NW, D])
        S.logits = sb("logits", [P, NW, NE])
        gnn_layer(nc, S, h6, D, W7, b7, xn_rows, False, x, Wp, bp, Wg, bg)
        S.share = sb("share", [P, NW, 2])
        S.pos = sb("pos", [P, NW, 2], I32)
        S.etab = sb("etab", [1, 2, NE], I32)
        route(nc, S, xn_rows, x_rows, y_rows)
        experts(nc, S, x_rows, y_rows, W1, b1, W2, b2)
        combine(nc, S, y_rows, out)


_INS = ['x', 'src', 'dst', 'edge_weight', 'L0_gnn_W6', 'L0_gnn_b6', 'L0_gnn_W7', 'L0_gnn_b7', 'L0_gnn_Wp', 'L0_gnn_bp',
        'L0_ffn_Wg', 'L0_ffn_bg', 'L0_ffn_W1', 'L0_ffn_b1', 'L0_ffn_W2', 'L0_ffn_b2']


def kernel(**inputs):
    import numpy as _np
    import concourse.bacc as _bacc
    from concourse.bass_utils import run_bass_kernel_spmd as _run
    nc = _bacc.Bacc("TRN2", target_bir_lowering=False, num_devices=1)
    arrays, args = {}, []
    for name in _INS:
        a = _np.ascontiguousarray(inputs[name])
        arrays[f"in_{name}_dram"] = a
        args.append(nc.dram_tensor(f"in_{name}_dram", a.shape, mybir.dt.from_np(a.dtype), kind="ExternalInput").ap())
    o = nc.dram_tensor("out_0_dram", (NODES, D), F32, kind="ExternalOutput").ap()
    build(nc, *args, o)
    r = _run(nc, [arrays], core_ids=[0])
    return r.results[0]["out_0_dram"]
```

```python
import concourse.bass as bass
from concourse import mybir
from contextlib import ExitStack

F32 = mybir.dt.float32
BF16 = mybir.dt.bfloat16
I32 = mybir.dt.int32
ALU = mybir.AluOpType
ACT = mybir.ActivationFunctionType
AX = mybir.AxisListType

P = 128
NODES, EDGES, D = 6250, 200000, 256
KD = D // P
NW = -(-NODES // P)
LASTW = NODES - (NW - 1) * P
PADN = NW * P
FULLT = EDGES // P
HALF = EDGES - FULLT * P
TILES = -(-EDGES // P)
U = 8
C = 198
TC = C * U
RING = 9
ROUNDS = C // RING
AHEAD = 3
EARLY = (NW - 1) // AHEAD
assert AHEAD * EARLY == NW - 1
assert RING * ROUNDS == C
G = -(-TC // P)
LASTG = TILES - (G - 1) * P
HB = 18
HN = TC // HB
assert HB * HN == TC and HN % 2 == 0
LO, HI = P // 2, 2 * NW
ROW1 = D + 1
EPS_N, EPS_LN = 1e-12, 1e-5
NE, H = 8, 1024
KH = H // P
B = 2 * P
assert 2 * PADN % B == 0
MAXB = 2 * PADN // B + NE
HALVES = B // P
SLOTS = HALVES * (MAXB + 2)
LT = 7
LSTEPS = 2 * NW // LT
assert LT * LSTEPS == 2 * NW and LSTEPS % 2 == 0
DUMP = B
T_CS, T_CE, T_OFF, T_REL, T_RND = range(5)


def bank(nc, ctx, name, shape):
    whole = ctx.enter_context(nc.psum_tensor(name, [P, 512], F32))
    if len(shape) == 2:
        return whole[0:shape[0], 0:shape[1]]
    return whole[0:shape[0], 0:shape[1] * shape[2]].rearrange("p (a b) -> p a b", a=shape[1])


def semaphores(nc, ctx):
    taken = []

    def clear():
        nc.clear_and_free_semaphores(taken)
        nc.all_engine_barrier()

    def take(name):
        taken.append(nc.alloc_semaphore(name=name))
        return taken[-1]

    ctx.callback(clear)
    return take


def load_edges_and_histogram(nc, x, src, dst, ew, S, rows1):
    with ExitStack() as ctx:
        sb = lambda n, s, d=F32: ctx.enter_context(nc.sbuf_tensor(n, s, d))
        ps = lambda n, s: bank(nc, ctx, n, s)
        sem = semaphores(nc, ctx)
        nat_src, nat_dst, shifted = (sb(n, [P, G, P], I32) for n in ("nat_src", "nat_dst", "shifted"))
        src_f, dst_f, nat_w = (sb(n, [P, G, P]) for n in ("src_f", "dst_f", "nat_w"))
        xin = sb("xin", [P, NW, D])
        digit_i = sb("digit_i", [P, TC], I32)
        lo, hi = sb("lo", [P, TC], BF16), sb("hi", [P, TC], BF16)
        w_rest = sb("w_rest", [P, TC])
        digits = sb("digits", [P, HI, HB], BF16)
        one_lo = [sb(f"one_lo{b}", [P, LO, HB], BF16) for b in range(2)]
        one_hi = [sb(f"one_hi{b}", [P, HI, HB], BF16) for b in range(2)]
        w_lo = [sb(f"w_lo{b}", [P, 3 * LO, HB], BF16) for b in range(2)]
        iota_i = sb("iota_i", [P, P], I32)
        wi_i = sb("wi_i", [P, NW + 1], I32)
        part_i = sb("part_i", [P, 1], I32)
        first = sb("first", [P, 1])
        thr = sb("thr", [P, NW + 1])
        t0 = sb("t0", [P, G])
        cmp = sb("cmp", [P, NW + 1, G])
        below = sb("below", [P, NW + 1])
        viol = sb("viol", [P, 2])
        rowf = sb("rowf", [1, 12, NW + 1])
        stats = sb("stats", [P, NW, 6])
        mv = sb("mv", [P, NW, 2])
        rstd, std, nbias = (sb(n, [P, NW]) for n in ("rstd", "std", "nbias"))
        hist = sb("hist", [HI, 3 * LO])
        by_lo = sb("by_lo", [LO, 2, NW])
        lower = sb("lower", [LO, P])
        pt = [ps(f"pt{i}", [P, 4, P]) for i in range(2)]
        pcnt = ps("pcnt", [1, NW + 1])
        pviol = ps("pviol", [1, 2])
        phist = ps("phist", [HI, 3 * LO])
        p_lo = ps("p_lo", [LO, HI])
        pdeg = ps("pdeg", [P, NW])

        padded, x_in = sem("padded"), sem("x_in")
        src_in, dst_in, shift_in, w_in = sem("src_in"), sem("dst_in"), sem("shift_in"), sem("w_in")
        iotas, consts_ready = sem("iotas"), sem("consts_ready")
        src_ready, dst_ready, nat_turned, columns_ready = sem("src_ready"), sem("dst_ready"), sem("nat_turned"), sem("columns_ready")
        tables_in, tables_summed, norm_ready = sem("tables_in"), sem("tables_summed"), sem("norm_ready")
        hist_lo, hist_hi = sem("hist_lo"), sem("hist_hi")
        part0_ready, parts_ready, hist_used = sem("part0_ready"), sem("parts_ready"), sem("hist_used")
        hist_done, hist_ready, lo_done, lo_ready = sem("hist_done"), sem("hist_ready"), sem("lo_done"), sem("lo_ready")
        deg_done, deg_ready = sem("deg_done"), sem("deg_ready")
        rows_ready, rows_stored = sem("rows_ready"), sem("rows_stored")
        var_ready, std_ready = sem("var_ready"), sem("std_ready")
        step = sem("step")
        block = ctx.enter_context(nc.Block())

        MAIN = (G - 1) * P * P
        TAIL = FULLT * P

        @block.sync
        def _(sp):
            sp.wait_ge(padded, 8)
            for arr, to, s in ((src, nat_src, src_in), (ew, nat_w, w_in), (dst, nat_dst, dst_in)):
                sp.dma_start(to[:, 0:G - 1, :], arr[0:MAIN].rearrange("(g p e) -> p g e", p=P, e=P)).then_inc(s, 16)
                sp.dma_start(to[0:LASTG - 1, G - 1, :], arr[MAIN:TAIL].rearrange("(p e) -> p e", e=P)).then_inc(s, 16)
                sp.dma_start(to[LASTG - 1:LASTG, G - 1, 0:HALF], arr[TAIL:EDGES].rearrange("(p e) -> p e", p=1)).then_inc(s, 16)
            sp.dma_start(shifted[:, 0:G - 1, :], dst[1:MAIN + 1].rearrange("(g p e) -> p g e", p=P, e=P)).then_inc(shift_in, 16)
            sp.dma_start(shifted[0:LASTG - 1, G - 1, :], dst[MAIN + 1:TAIL + 1].rearrange("(p e) -> p e", e=P)).then_inc(shift_in, 16)
            sp.dma_start(shifted[LASTG - 1:LASTG, G - 1, 0:HALF - 1], dst[TAIL + 1:EDGES].rearrange("(p e) -> p e", p=1)).then_inc(shift_in, 16)
            sp.dma_start(xin[:, 0:NW - 1, :], x[0:(NW - 1) * P, :].rearrange("(w p) d -> p w d", p=P)).then_inc(x_in, 16)
            sp.dma_start(xin[0:LASTW, NW - 1, :], x[(NW - 1) * P:NODES, :]).then_inc(x_in, 16)
            sp.wait_ge(rows_ready, 1)
            sp.dma_start(rows1[:, 0:D].rearrange("(w p) d -> p w d", p=P), xin[:, :, :]).then_inc(rows_stored, 16)
            sp.wait_ge(deg_ready, 1)
            sp.dma_start(rows1[:, D:ROW1].rearrange("(w p) d -> p w d", p=P), S.deg[:, :].unsqueeze(2), allow_slow_non_contiguous=True).then_inc(rows_stored, 16)
            sp.wait_ge(rows_stored, 32)

        @block.gpsimd
        def _(pool):
            nc.gpsimd.memset(nat_src[:, G - 1, :], 0).then_inc(padded, 1)
            nc.gpsimd.memset(nat_w[:, G - 1, :], 0.0).then_inc(padded, 1)
            nc.gpsimd.memset(nat_dst[:, G - 1, :], 0).then_inc(padded, 1)
            nc.gpsimd.memset(shifted[:, G - 1, :], 1000000).then_inc(padded, 1)
            nc.gpsimd.memset(xin[:, NW - 1, :], 0.0).then_inc(padded, 1)
            nc.gpsimd.memset(t0[:, 0:G - 1], 1e6).then_inc(padded, 1)
            nc.gpsimd.memset(t0[:, G - 1:G], 1e6).then_inc(padded, 1)
            pool.wait_ge(padded, 7)
            nc.gpsimd.memset(t0[0:TC - (G - 1) * P, G - 1:G], float(NODES - 1)).then_inc(padded, 1)
            pool.iota(iota_i[:, :], [[1, P]], base=0, channel_multiplier=0).then_inc(iotas, 1)
            pool.iota(wi_i[:, :], [[1, NW + 1]], base=0, channel_multiplier=0).then_inc(iotas, 1)
            pool.iota(part_i[:, :], [[0, 1]], base=0, channel_multiplier=1).then_inc(iotas, 1)
            nc.gpsimd.memset(S.ident[:, :], 0.0).then_inc(iotas, 1)
            nc.gpsimd.memset(lower[:, :], 0.0).then_inc(iotas, 1)
            pool.wait_ge(iotas, 5)
            pool.affine_select(out=S.ident[:, :], in_=S.ident[:, :], compare_op=ALU.not_equal, fill=1.0, base=0,
                               pattern=[[-1, P]], channel_multiplier=1).then_inc(consts_ready, 1)
            pool.affine_select(out=lower[:, :], in_=lower[:, :], compare_op=ALU.not_equal, fill=1.0, base=LO,
                               pattern=[[-1, P]], channel_multiplier=1).then_inc(consts_ready, 1)
            with pool.Fori(0, HN // 2) as i:
                for b in range(2):
                    pool.wait_ge(hist_lo, 2 * i + b + 1)
                    pool.sem_inc(S.pool_turn, 1)
                    pool.wait_ge(hist_used, 2 * i + b + 1)
                    pool.sem_inc(S.pool_turn, 1)
                    nc.gpsimd.tensor_tensor(w_lo[b][:, 0:LO, :], one_lo[b][:, :, :],
                                            S.w3[:, 0, bass.ds((2 * i + b) * HB, HB)].unsqueeze(1).to_broadcast([P, LO, HB]),
                                            ALU.mult).then_inc(part0_ready, 1)

        @block.vector
        def _(dve):
            n = [0]

            def link(ins):
                n[0] += 1
                ins.then_inc(step, 1)
                dve.wait_ge(step, n[0])

            link(nc.vector.memset(S.eps_ln[:, :], EPS_LN))
            link(nc.vector.memset(S.eps_n[:, :], EPS_N))
            nc.vector.memset(S.ones[:, :], 1.0).then_inc(consts_ready, 1)
            nc.vector.memset(S.zeros[:, :], 0.0).then_inc(consts_ready, 1)
            nc.vector.memset(S.q_col[:, :], 0.0).then_inc(consts_ready, 1)
            dve.wait_ge(iotas, 3)
            link(nc.vector.tensor_copy(S.iota[:, :], iota_i[:, :]))
            link(nc.vector.tensor_copy(digits[:, :, :], S.iota[:, 0:HI].unsqueeze(2).to_broadcast([P, HI, HB])))
            dve.wait_ge(src_in, 48)
            nc.vector.tensor_copy(src_f[:, :, :], nat_src[:, :, :]).then_inc(src_ready, 1)
            link(nc.vector.tensor_copy(thr[:, :], wi_i[:, :]))
            link(nc.vector.tensor_scalar(thr[:, :], thr[:, :], float(P), None, ALU.mult))
            link(nc.vector.tensor_copy(S.base[:, :], thr[:, 0:NW]))
            link(nc.vector.tensor_single_scalar(part_i[:, :], part_i[:, :], U - 1, ALU.bitwise_and))
            link(nc.vector.tensor_copy(first[:, :], part_i[:, :]))
            link(nc.vector.tensor_scalar(first[:, :], first[:, :], 0.0, None, ALU.is_equal))
            dve.wait_ge(dst_in, 48)
            nc.vector.tensor_copy(dst_f[:, :, :], nat_dst[:, :, :]).then_inc(dst_ready, 1)
            dve.wait_ge(columns_ready, 4)
            link(nc.vector.tensor_single_scalar(digit_i[:, :], S.src_col[:, :], LO - 1, ALU.bitwise_and))
            link(nc.vector.tensor_copy(lo[:, :], digit_i[:, :]))
            link(nc.vector.tensor_single_scalar(digit_i[:, :], S.src_col[:, :], 6, ALU.logical_shift_right))
            link(nc.vector.tensor_copy(hi[:, :], digit_i[:, :]))
            dve.wait_ge(columns_ready, 8)
            link(nc.vector.tensor_copy(S.w3[:, 0, :], S.w_col[:, :]))
            link(nc.vector.tensor_tensor(w_rest[:, :], S.w_col[:, :], S.w3[:, 0, :], ALU.subtract))
            link(nc.vector.tensor_copy(S.w3[:, 1, :], w_rest[:, :]))
            link(nc.vector.tensor_tensor(w_rest[:, :], w_rest[:, :], S.w3[:, 1, :], ALU.subtract))
            link(nc.vector.tensor_copy(S.w3[:, 2, :], w_rest[:, :]))

            def one_hots(i0, i1):
                with dve.Fori(i0, i1) as i:
                    for b in range(2):
                        k = 2 * i + b
                        at = bass.ds(k * HB, HB)
                        dve.wait_ge(hist_used, k + 1)
                        dve.wait_ge(part0_ready, k + 1)
                        nc.vector.tensor_tensor(one_lo[b][:, :, :], digits[:, 0:LO, :], lo[:, at].unsqueeze(1).to_broadcast([P, LO, HB]), ALU.is_equal).then_inc(hist_lo, 1)
                        nc.vector.tensor_tensor(one_hi[b][:, :, :], digits[:, :, :], hi[:, at].unsqueeze(1).to_broadcast([P, HI, HB]), ALU.is_equal).then_inc(hist_hi, 1)
                        dve.wait_ge(hist_lo, k + 1)
                        for part in (1, 2):
                            nc.vector.tensor_tensor(w_lo[b][:, part * LO:(part + 1) * LO, :], one_lo[b][:, :, :],
                                                    S.w3[:, part, at].unsqueeze(1).to_broadcast([P, LO, HB]), ALU.mult).then_inc(parts_ready, 1)

            one_hots(0, HN // 4)
            dve.wait_ge(shift_in, 48)
            dve.wait_ge(padded, 8)
            dve.wait_ge(dst_ready, 1)
            link(nc.vector.tensor_copy(t0[:, 0:G - 1], dst_f[:, 0:G - 1, 0]))
            link(nc.vector.tensor_copy(t0[0:LASTG, G - 1:G], dst_f[0:LASTG, G - 1, 0:1]))
            link(nc.vector.tensor_tensor(nat_dst[:, :, :], nat_dst[:, :, :], shifted[:, :, :], ALU.is_gt))
            link(nc.vector.tensor_reduce(viol[:, 0:1], nat_dst[:, :, :], AX.XY, ALU.max))
            nc.vector.memset(viol[:, 1:2], 0.0).then_inc(tables_in, 1)
            link(nc.vector.tensor_tensor(cmp[:, :, :], t0[:, :].unsqueeze(1).to_broadcast([P, NW + 1, G]),
                                         thr[:, :].unsqueeze(2).to_broadcast([P, NW + 1, G]), ALU.is_lt))
            nc.vector.tensor_reduce(below[:, :], cmp[:, :, :], AX.X, ALU.add).then_inc(tables_in, 1)
            dve.wait_ge(x_in, 32)
            dve.sem_inc(S.dve_turn, 1)
            with dve.Fori(0, NW) as w:
                nc.vector.bn_stats(stats[:, bass.ds(w, 1), :], xin[:, bass.ds(w, 1), :])
            nc.vector.memset(rstd[:, :], 0.0).then_inc(norm_ready, 1)
            dve.wait_ge(norm_ready, 1)
            link(nc.vector.tensor_tensor(mv[:, :, :], stats[:, :, 1:3], stats[:, :, 4:6], ALU.add))
            link(nc.vector.tensor_tensor(std[:, :], stats[:, :, 1], stats[:, :, 4], ALU.subtract))
            link(nc.vector.tensor_tensor(nbias[:, :], std[:, :], std[:, :], ALU.mult))
            link(nc.vector.tensor_scalar(mv[:, :, 0], mv[:, :, 0], 0.5, None, ALU.mult))
            link(nc.vector.tensor_scalar(mv[:, :, 1], mv[:, :, 1], 1.0 / D, None, ALU.mult))
            link(nc.vector.scalar_tensor_tensor(mv[:, :, 1], nbias[:, :], 0.25, mv[:, :, 1], ALU.mult, ALU.add))
            nc.vector.memset(rstd[:, :], 0.0).then_inc(var_ready, 1)
            dve.wait_ge(std_ready, 1)
            link(nc.vector.reciprocal(rstd[:, :], std[:, :]))
            link(nc.vector.tensor_tensor(nbias[:, :], mv[:, :, 0], rstd[:, :], ALU.mult))
            nc.vector.tensor_scalar(nbias[:, :], nbias[:, :], -1.0, None, ALU.mult).then_inc(norm_ready, 1)
            one_hots(HN // 4, HN // 2)
            dve.wait_ge(tables_summed, 1)
            row = lambda k: rowf[0:1, k, :]
            FIRST, CSS, CES, ALLC, T1, T2 = range(6)
            fl = S.sorted_f[0:1, 0:1]
            nf = S.sorted_f[0:1, 1:2]
            link(nc.vector.tensor_copy(row(FIRST), pcnt[0:1, :]))
            link(nc.vector.tensor_scalar(fl, pviol[0:1, 0:1], 0.5, None, ALU.is_lt))
            link(nc.vector.tensor_scalar(nf, fl, -1.0, 1.0, ALU.mult, ALU.add))
            link(nc.vector.tensor_scalar(row(CSS), row(FIRST), -1.0, 0.0, ALU.add, ALU.max))
            link(nc.vector.tensor_scalar(row(CES), row(FIRST), 1.0, None, ALU.max))
            link(nc.vector.tensor_scalar(row(ALLC), thr[0:1, :], float(C) / P, nf, ALU.mult, ALU.mult))
            a, b_ = slice(0, NW), slice(1, NW + 1)
            tab = lambda k: S.tab_f[0:1, k, 0:NW]
            link(nc.vector.memset(S.tab_f[:, :, :], 0.0))
            link(nc.vector.tensor_scalar(rowf[0:1, T1, :], row(CSS), fl, None, ALU.mult))
            link(nc.vector.tensor_tensor(tab(T_CS), rowf[0:1, T1, a], rowf[0:1, ALLC, a], ALU.add))
            link(nc.vector.tensor_scalar(rowf[0:1, T2, :], row(CES), fl, None, ALU.mult))
            link(nc.vector.tensor_tensor(tab(T_CE), rowf[0:1, T2, b_], rowf[0:1, ALLC, b_], ALU.add))
            link(nc.vector.tensor_scalar(tab(T_OFF), thr[0:1, a], 1.0 / P, fl, ALU.mult, ALU.mult))
            link(nc.vector.tensor_scalar(tab(T_REL), tab(T_CE), fl, None, ALU.subtract))
            link(nc.vector.tensor_copy(S.tab_f[0:1, T_REL, NW - 1:NW], S.tab_f[0:1, T_CE, NW - 1:NW]))
            link(nc.vector.tensor_scalar(S.tab_f[0:1, T_RND, 0:1], nf, float((NW - 1) * ROUNDS), float(ROUNDS), ALU.mult, ALU.add))
            link(nc.vector.tensor_copy(S.tab[:, :, :], S.tab_f[:, :, :].rearrange("a k w -> a w k")))
            dve.wait_ge(hist_done, 1)
            nc.vector.tensor_copy(hist[:, :], phist[:, :]).then_inc(hist_ready, 1)
            dve.wait_ge(lo_done, 1)
            nc.vector.tensor_copy(by_lo[:, :, :], p_lo[:, :].rearrange("p (w t) -> p t w", t=2)).then_inc(lo_ready, 1)
            dve.wait_ge(deg_done, 1)
            nc.vector.tensor_copy(S.deg[:, :], pdeg[:, :]).then_inc(deg_ready, 1)

        @block.scalar
        def _(act):
            k = 0
            for a, cols in enumerate((S.src_col, S.w_col, S.dst_col)):
                for q in range(4):
                    g0, g1 = 4 * q, min(4 * q + 4, G)
                    act.wait_ge(nat_turned, G * a + g1)
                    c0, c1 = g0 * P, min(g1 * P, TC)
                    nc.scalar.copy(cols[:, c0:c1], pt[k % 2][:, 0:g1 - g0, :].rearrange("p g e -> p (g e)")[:, 0:c1 - c0]).then_inc(columns_ready, 1)
                    k += 1
            act.wait_ge(var_ready, 1)
            nc.scalar.activation(std[:, :], mv[:, :, 1], ACT.Sqrt, bias=S.eps_ln[:, :]).then_inc(std_ready, 1)
            act.wait_ge(norm_ready, 2)
            with act.Fori(0, NW - 1) as w:
                nc.scalar.activation(xin[:, bass.ds(w, 1), :], xin[:, bass.ds(w, 1), :], ACT.Identity,
                                     bias=nbias[:, bass.ds(w, 1)], scale=rstd[:, bass.ds(w, 1)])
            nc.scalar.activation(xin[:, NW - 1, :], xin[:, NW - 1, :], ACT.Identity,
                                 bias=nbias[:, NW - 1:NW], scale=rstd[:, NW - 1:NW]).then_inc(rows_ready, 1)

        @block.tensor
        def _(pe):
            pe.wait_ge(consts_ready, 5)
            k = 0
            for s, count, nat in ((src_ready, 1, src_f), (w_in, 48, nat_w), (dst_ready, 1, dst_f)):
                pe.wait_ge(s, count)
                for q in range(4):
                    if k >= 2:
                        pe.wait_ge(columns_ready, k - 1)
                    for g in range(4 * q, min(4 * q + 4, G)):
                        nc.tensor.transpose(pt[k % 2][:, g - 4 * q, :], nat[:, g, :], S.ident[:, :]).then_inc(nat_turned, 1)
                    k += 1

            def count(i0, i1):
                with pe.Fori(i0, i1) as i:
                    for b in range(2):
                        k = 2 * i + b
                        pe.wait_ge(hist_hi, k + 1)
                        pe.wait_ge(part0_ready, k + 3)
                        pe.wait_ge(parts_ready, 2 * k + 2)
                        for j in range(HB):
                            last = nc.tensor.matmul(phist[:, :], one_hi[b][:, :, j], w_lo[b][:, :, j], start=False, stop=False)
                        last.then_inc(hist_used, 1)

            pe.sem_inc(hist_used, 2)
            pe.sem_inc(part0_ready, 2)
            nc.tensor.matmul(phist[:, :], S.zeros[:, 0:HI], S.zeros[:, 0:3 * LO], start=True, stop=False)
            count(0, HN // 4)
            pe.wait_ge(tables_in, 2)
            nc.tensor.matmul(pcnt[0:1, :], first[:, :], below[:, :], start=True, stop=True)
            nc.tensor.matmul(pviol[0:1, :], S.ones[:, 0:1], viol[:, :], start=True, stop=True).then_inc(tables_summed, 1)
            count(HN // 4, HN // 2)
            nc.tensor.matmul(phist[:, :], S.zeros[:, 0:HI], S.zeros[:, 0:3 * LO], start=False, stop=True).then_inc(hist_done, 1)
            pe.wait_ge(hist_ready, 1)
            for part in range(3):
                last = nc.tensor.matmul(p_lo[:, :], hist[:, part * LO:(part + 1) * LO], S.ident[0:HI, 0:HI], start=part == 0, stop=part == 2)
            last.then_inc(lo_done, 1)
            pe.wait_ge(lo_ready, 1)
            nc.tensor.matmul(pdeg[:, :], S.ident[0:LO, :], by_lo[:, 0, :], start=True, stop=False)
            nc.tensor.matmul(pdeg[:, :], lower[:, :], by_lo[:, 1, :], start=False, stop=True).then_inc(deg_done, 1)


def gnn_layer(nc, S, table, width, weight, bias, h_out, first, x=None, Wp=None, bp=None, Wg=None, bg=None):
    with ExitStack() as ctx:
        sb = lambda n, s, d=F32: ctx.enter_context(nc.sbuf_tensor(n, s, d))
        ps = lambda n, s: bank(nc, ctx, n, s)
        t = "a" if first else "b"
        alloc = semaphores(nc, ctx)
        sem = lambda n: alloc(n + t)
        ring = sb("ring" + t, [P, RING * U, width])
        staged = sb("staged" + t, [P, RING * U], I32)
        sel = sb("sel" + t, [P, U, P])
        win = sb("win" + t, [P, P])
        wt = sb("wt" + t, [P, KD, D])
        brow = sb("brow" + t, [1, D])
        agg = sb("agg" + t, [P, D])
        aggT = sb("aggT" + t, [P, KD, P])
        h = sb("h" + t, [P, D])
        if first:
            nodes = sb("nodes", [P, P, U], BF16)
            near_a, near = sb("near_a", [P, U], BF16), sb("near", [P, U], BF16)
            mark = sb("mark", [P, P, U], BF16)
            w3_here = sb("w3_here", [P, U, 3], BF16)
            hot = sb("hot", [P, 2 * P, U], BF16)
            reach = sb("reach", [P, U, P])
            near_f, dib_w = sb("near_f", [P, U]), sb("dib_w", [P, P])
            di3 = sb("di3", [P, 3])
            dib = sb("dib", [P, NW * P])
            q8, x8, y8 = sb("q8", [P, U]), sb("x8", [P, U]), sb("y8", [P, 2, U])
            s8, n8 = sb("s8", [P, U]), sb("n8", [P, U])
            p_di = ps("p_di" + t, [P, 3])
            p_dib = ps("p_dib" + t, [P, P])
        p_agg = ps("p_agg" + t, [P, D])
        p_t = ps("p_t" + t, [P, KD, P])
        p_h = ps("p_h" + t, [P, D])
        if not first:
            wp, bprow = sb("wp", [P, KD, D]), sb("bprow", [1, D])
            wg, bgrow = sb("wg", [P, KD, NE]), sb("bgrow", [1, NE])
            hT = sb("hT", [P, KD, P])
            x2w = sb("x2w", [P, D])
            st, mv, sd, rs = sb("st", [P, 6]), sb("mv2", [P, 2]), sb("sd", [P, 1]), sb("rs", [P, 1])
            xn, xnT = sb("xn", [P, D]), sb("xnT", [P, KD, P])
            p_hT, p_o, p_xT, p_g = ps("p_hT", [P, KD, P]), ps("p_o", [P, D]), ps("p_xT", [P, KD, P]), ps("p_g", [P, NE])
            x_pad, x_in = sem("x_pad"), sem("x_in2")
            product_ready, roots_ready, norm_step = sem("product_ready"), sem("roots_ready"), sem("norm_step")
            h_turned, hT_ready, o_done, post = sem("h_turned"), sem("hT_ready"), sem("o_done"), sem("post")
            var_ready, sd_ready, xn_ready = sem("var_ready2"), sem("sd_ready"), sem("xn_ready")
            xn_turned, xnT_ready, gate_done, gate_ready, xn_stored = sem("xn_turned"), sem("xnT_ready"), sem("gate_done"), sem("gate_ready"), sem("xn_stored")

        row_in = [sem(f"row_in{s}_") for s in range(RING)]
        idx_staged, arrived, released = sem("idx_staged"), sem("arrived"), sem("released")
        weights_in = sem("weights_in")
        nodes_ready, dib_here, near_a_ready, near_ready, win_ready, mark_ready, mark_used = sem("nodes_ready"), sem("dib_here"), sem("near_a_ready"), sem("near_ready"), sem("win_ready"), sem("mark_ready"), sem("mark_used")
        di_done, di3_ready, dib_done, dib_ready = sem("di_done"), sem("di3_ready"), sem("dib_done"), sem("dib_ready")
        hot_ready, q_ready, do_ready, kept = sem("hot_ready"), sem("q_ready"), sem("do_ready"), sem("kept")
        x_ready, x_eps_ready, inverse_ready = sem("x_ready"), sem("x_eps_ready"), sem("inverse_ready")
        root_ready, norm_ready = sem("root_ready"), sem("norm_ready")
        sel_ready, sel_used = sem("sel_ready"), sem("sel_used")
        agg_done, agg_copied, agg_turned, aggT_ready = sem("agg_done"), sem("agg_copied"), sem("agg_turned"), sem("aggT_ready")
        h_done, h_ready, h_stored = sem("h_done"), sem("h_ready"), sem("h_stored")
        block = ctx.enter_context(nc.Block())

        def steps(eng, step):
            there = lambda w: 0 <= w < NW
            for w in range(3):
                step(w, there)
            with eng.Fori(3, NW) as w:
                step(w, lambda w: True)
            for w in range(NW, NW + 3):
                step(w, there)

        def entries(eng, w, n):
            at = S.tab[0:1, bass.ds(w, 1), 0:n]
            return nc.values_load_multi_w_load_instructions(at, engines=[eng.engine], min_val=0, max_val=NW * C)[1]

        def visits(eng, w):
            return entries(eng, w, 3)

        @block.gpsimd
        def _(pool):
            rounds = pool.value_load(S.tab[0:1, 0, T_RND:T_RND + 1], min_val=ROUNDS, max_val=ROUNDS * NW)

            def stage(slot, at):
                nc.gpsimd.tensor_copy(staged[:, slot * U:(slot + 1) * U], S.src_col[:, bass.ds(at * (RING * U) + slot * U, U)]).then_inc(idx_staged, 1)

            stage(0, 0)
            with pool.Fori(0, rounds) as it:
                here = it % ROUNDS
                there = (it + 1) % ROUNDS
                for slot in range(RING):
                    pool.wait_ge(released, RING * it + slot + 2)
                    pool.sem_inc(S.pool_turn, 1)
                    if slot < RING - 1:
                        stage(slot + 1, here)
                    else:
                        stage(0, there)
                    pool.wait_ge(idx_staged, RING * it + slot + 1)
                    pool.sem_inc(S.pool_turn, 1)
                    for k in range(slot * U, (slot + 1) * U):
                        pool.indirect_dma_start(out=ring[:, k, :], out_offset=None, in_=table[:, :],
                                                in_offset=bass.IndirectOffsetOnAxis(ap=staged[:, k:k + 1], axis=0)).then_inc(row_in[slot], 16)

        @block.sync
        def _(sp):
            sp.dma_start(wt[:, :, :], weight.rearrange("(k p) n -> p k n", p=P)).then_inc(weights_in, 16)
            sp.dma_start(brow[:, :], bias.rearrange("(a n) -> a n", a=1)).then_inc(weights_in, 16)
            if not first:
                sp.dma_start(wp[:, :, :], Wp.rearrange("(k p) n -> p k n", p=P)).then_inc(weights_in, 16)
                sp.dma_start(wg[:, :, :], Wg.rearrange("(k p) n -> p k n", p=P)).then_inc(weights_in, 16)
                sp.dma_start(bprow[:, :], bp.rearrange("(a n) -> a n", a=1)).then_inc(weights_in, 16)
                sp.dma_start(bgrow[:, :], bg.rearrange("(a n) -> a n", a=1)).then_inc(weights_in, 16)
                sp.wait_ge(x_pad, 1)
                sp.dma_start(S.x2[:, 0:NW - 1, :], x[0:(NW - 1) * P, :].rearrange("(w p) d -> p w d", p=P)).then_inc(x_in, 16)
                sp.dma_start(S.x2[0:LASTW, NW - 1, :], x[(NW - 1) * P:NODES, :]).then_inc(x_in, 16)
            rounds = sp.value_load(S.tab[0:1, 0, T_RND:T_RND + 1], min_val=ROUNDS, max_val=ROUNDS * NW)
            with sp.Fori(0, rounds) as it:
                for s in range(RING):
                    sp.wait_ge(row_in[s], 16 * U * (it + 1))
                    sp.sem_inc(arrived, 1)

        @block.vector
        def _(dve):
            every = lambda cols: cols.unsqueeze(1).to_broadcast([P, P, U])

            def marks(w):
                cs, ce, off = visits(dve, w)
                with dve.Fori(cs, ce) as c:
                    v = c + off
                    here = bass.ds((c % C) * U, U)
                    dve.wait_ge(mark_used, v)
                    nc.vector.tensor_scalar(near_a[:, :], S.dst_col[:, here], S.base[:, bass.ds(w, 1)], None, ALU.subtract).then_inc(near_a_ready, 1)
                    nc.vector.tensor_copy(w3_here[:, :, :], S.w3[:, :, here].rearrange("p k j -> p j k")).then_inc(mark_ready, 1)
                    dve.wait_ge(near_a_ready, v + 1)
                    nc.vector.tensor_tensor(mark[:, :, :], nodes[:, :, :], every(near_a[:, :]), ALU.is_equal).then_inc(mark_ready, 1)

            def find(w, c, v, before):
                here = bass.ds((c % C) * U, U)
                at = bass.ds((v % 2) * P, P)
                if before:
                    product(c + (C - 1))
                dve.wait_ge(hot_ready, v)
                nc.vector.tensor_scalar(near_f[:, :], S.dst_col[:, here], S.base[:, bass.ds(w, 1)], None, ALU.subtract).then_inc(near_ready, 1)
                nc.vector.tensor_scalar(near[:, :], S.dst_col[:, here], S.base[:, bass.ds(w, 1)], None, ALU.subtract).then_inc(near_ready, 1)
                if before:
                    plus_eps(v)
                dve.wait_ge(arrived, c + 1)
                dve.sem_inc(S.dve_turn, 1)
                nc.vector.tensor_copy(S.do_col[:, here].unsqueeze(2), ring[:, bass.ds((c % RING) * U, U), D:ROW1]).then_inc(do_ready, 1)
                if before:
                    invert(v)
                dve.wait_ge(kept, v)
                dve.wait_ge(near_ready, 2 * v + 2)
                for j in range(U):
                    nc.vector.scalar_tensor_tensor(reach[:, j, :], S.iota[:, :], near_f[:, j:j + 1], dib_w[:, :], ALU.is_equal, ALU.mult,
                                                   accum_out=q8[:, j:j + 1]).then_inc(q_ready, 1)
                dve.wait_ge(sel_ready, v * U)
                nc.vector.tensor_tensor(hot[:, at, :], nodes[:, :, :], every(near[:, :]), ALU.is_equal).then_inc(hot_ready, 1)
                dve.wait_ge(q_ready, U * v + U)
                nc.vector.tensor_tensor(S.q_col[:, here], S.q_col[:, here], q8[:, :], ALU.add).then_inc(kept, 1)
                if before:
                    norms(c + (C - 1), v)

            def product(c):
                nc.vector.tensor_tensor(x8[:, :], q8[:, :], S.do_col[:, bass.ds((c % C) * U, U)], ALU.mult).then_inc(x_ready, 1)

            def plus_eps(v):
                dve.wait_ge(x_ready, v)
                nc.vector.tensor_scalar(x8[:, :], x8[:, :], EPS_N, None, ALU.add).then_inc(x_eps_ready, 1)

            def invert(v):
                dve.wait_ge(x_eps_ready, v)
                nc.vector.reciprocal(y8[:, bass.ds((v + 1) % 2, 1), :], x8[:, :].unsqueeze(1)).then_inc(inverse_ready, 1)

            def norms(c, v):
                dve.wait_ge(root_ready, v)
                nc.vector.tensor_tensor(n8[:, :], s8[:, :], S.w_col[:, bass.ds((c % C) * U, U)], ALU.mult).then_inc(norm_ready, 1)

            def inverses(w):
                cs, ce, off = visits(dve, w)
                dve.wait_ge(dib_ready, w + 1)
                dve.wait_ge(q_ready, U * (cs + off))
                nc.vector.tensor_copy(dib_w[:, :], dib[:, bass.ds(w * P, P)]).then_inc(dib_here, 1)
                dve.wait_ge(dib_here, w + 1)
                find(w, cs, cs + off, False)
                with dve.If(cs + 1 < ce):
                    with dve.Fori(cs + 1, ce) as c:
                        dve.wait_ge(do_ready, c + off)
                        find(w, c, c + off, True)
                v = ce + off
                dve.wait_ge(do_ready, v)
                product(ce + (C - 1))
                plus_eps(v)
                invert(v)
                dve.wait_ge(sel_ready, v * U)
                norms(ce + (C - 1), v)

            def window(w):
                cs, ce, off = visits(dve, w)
                dve.wait_ge(sel_ready, U * (cs + off))
                nc.vector.tensor_scalar(win[:, :], S.iota[:, :], S.base[:, bass.ds(w, 1)], None, ALU.add).then_inc(win_ready, 1)
                dve.wait_ge(win_ready, w + 1)
                dve.sem_inc(S.dve_turn, 1)
                with dve.Fori(cs, ce) as c:
                    tile = (c % C) * U
                    v = c + off
                    for j in range(U):
                        dve.wait_ge(sel_used, v * U + j + 1)
                        nc.vector.tensor_scalar(sel[:, j, :], win[:, :], S.dst_col[:, bass.ds(tile + j, 1)],
                                                S.q_col[:, bass.ds(tile + j, 1)], ALU.is_equal, ALU.mult).then_inc(sel_ready, 1)

            def residual(w):
                dve.wait_ge(o_done, w + 1)
                nc.vector.tensor_tensor(x2w[:, :].unsqueeze(1), p_o.unsqueeze(1), S.x2[:, bass.ds(w, 1), :], ALU.add).then_inc(post, 1)
                dve.wait_ge(post, 5 * w + 1)
                dve.sem_inc(S.dve_turn, 1)
                nc.vector.tensor_copy(S.x2[:, bass.ds(w, 1), :], x2w[:, :].unsqueeze(1)).then_inc(post, 1)
                nc.vector.bn_stats(st[:, :], x2w[:, :]).then_inc(post, 1)
                dve.wait_ge(post, 5 * w + 3)
                dve.sem_inc(S.dve_turn, 1)
                nc.vector.bn_aggr(mv[:, :], st[:, :]).then_inc(var_ready, 1)
                dve.wait_ge(sd_ready, w + 1)
                nc.vector.reciprocal(rs[:, :], sd[:, :]).then_inc(post, 1)
                dve.wait_ge(post, 5 * w + 4)
                dve.wait_ge(xn_stored, 16 * w)
                dve.wait_ge(xn_turned, KD * w)
                dve.sem_inc(S.dve_turn, 1)
                nc.vector.tensor_scalar(xn[:, :], x2w[:, :], mv[:, 0:1], rs[:, 0:1], ALU.subtract, ALU.mult).then_inc(xn_ready, 1)
                dve.wait_ge(xn_ready, w + 1)
                dve.sem_inc(post, 1)

            if first:
                nc.vector.tensor_copy(nodes[:, :, :], S.iota[:, :].unsqueeze(2).to_broadcast([P, P, U])).then_inc(nodes_ready, 1)
                dve.wait_ge(nodes_ready, 1)
                marks(0)
                with dve.Fori(0, EARLY) as w:
                    for k in range(AHEAD):
                        marks(AHEAD * w + k + 1)
                    inverses(w)
                with dve.Fori(EARLY, NW) as w:
                    inverses(w)
            else:
                nc.vector.tensor_tensor(S.q_col[:, :], S.q_col[:, :], S.do_col[:, :], ALU.mult).then_inc(product_ready, 1)
                dve.wait_ge(roots_ready, 1)
                nc.vector.reciprocal(S.q_col[:, :], S.q_col[:, :]).then_inc(norm_step, 1)
                dve.wait_ge(norm_step, 1)
                nc.vector.tensor_tensor(S.q_col[:, :], S.q_col[:, :], S.w_col[:, :], ALU.mult).then_inc(norm_step, 1)
                dve.wait_ge(norm_step, 2)
                nc.vector.memset(S.x2[:, NW - 1, :], 0.0).then_inc(x_pad, 1)
                dve.wait_ge(x_in, 32)

                def step(w, on):
                    if on(w):
                        window(w)
                    if on(w - 2):
                        residual(w - 2)

                steps(dve, step)

        @block.tensor
        def _(pe):
            pe.sem_inc(sel_used, U)
            pe.sem_inc(released, RING)
            pe.wait_ge(weights_in, 32 if first else 96)

            def count(w):
                cs, ce, off = visits(pe, w)
                nc.tensor.matmul(p_di[:, :], S.zeros[:, 0:P], S.zeros[:, 0:3], start=True, stop=False)
                with pe.Fori(cs, ce) as c:
                    pe.wait_ge(mark_ready, 2 * (c + off) + 2)
                    for j in range(U):
                        last = nc.tensor.matmul(p_di[:, :], mark[:, :, j], w3_here[:, j, :], start=False, stop=False)
                    last.then_inc(mark_used, 1)
                nc.tensor.matmul(p_di[:, :], S.zeros[:, 0:P], S.zeros[:, 0:3], start=False, stop=True).then_inc(di_done, 1)

            def spread(w):
                pe.wait_ge(di3_ready, w + 1)
                for k in range(3):
                    last = nc.tensor.matmul(p_dib[:, :], di3[:, k:k + 1].to_broadcast([P, P]), S.ident[:, :], start=k == 0, stop=k == 2)
                last.then_inc(dib_done, 1)

            def window(w):
                cs, ce, off, rel = entries(pe, w, 4)
                nc.tensor.matmul(p_agg[:, :], S.zeros[:, 0:P], S.zeros[:, 0:D], start=True, stop=False)
                ahead = U if first else 0
                with pe.Fori(cs, ce) as c:
                    slot = (c % RING) * U
                    v = c + off
                    pe.wait_ge(arrived, c + 1)
                    for j in range(U):
                        pe.wait_ge(sel_ready, v * U + j + 1 + ahead)
                        nc.tensor.matmul(p_agg[:, :], sel[:, j, :], ring[:, bass.ds(slot + j, 1), 0:D], start=False, stop=False).then_inc(sel_used, 1)
                    with pe.If(c < rel):
                        nc.tensor.matmul(p_agg[:, 0:1], S.zeros[:, 0:P], S.zeros[:, 0:1], start=False, stop=False).then_inc(released, 1)
                nc.tensor.matmul(p_agg[:, :], S.zeros[:, 0:P], S.zeros[:, 0:D], start=False, stop=True).then_inc(agg_done, 1)

            def turn(w):
                pe.wait_ge(agg_copied, w + 1)
                for k in range(KD):
                    nc.tensor.transpose(p_t[:, k, :], agg[:, k * P:(k + 1) * P], S.ident[:, :]).then_inc(agg_turned, 1)

            def dense(w):
                pe.wait_ge(aggT_ready, w + 1)
                pe.wait_ge(h_ready, w)
                nc.tensor.matmul(p_h[:, :], S.ones[0:1, :], brow[:, :], start=True, stop=False)
                for k in range(KD):
                    last = nc.tensor.matmul(p_h[:, :], aggT[:, k, :], wt[:, k, :], start=False, stop=k == KD - 1)
                last.then_inc(h_done, 1)

            def turn_h(w):
                pe.wait_ge(h_ready, w + 1)
                for k in range(KD):
                    nc.tensor.transpose(p_hT[:, k, :], h[:, k * P:(k + 1) * P], S.ident[:, :]).then_inc(h_turned, 1)

            def project(w):
                pe.wait_ge(hT_ready, w + 1)
                pe.wait_ge(post, 5 * w)
                nc.tensor.matmul(p_o[:, :], S.ones[0:1, :], bprow[:, :], start=True, stop=False)
                for k in range(KD):
                    last = nc.tensor.matmul(p_o[:, :], hT[:, k, :], wp[:, k, :], start=False, stop=k == KD - 1)
                last.then_inc(o_done, 1)

            def gate(w):
                pe.wait_ge(xn_ready, w + 1)
                for k in range(KD):
                    nc.tensor.transpose(p_xT[:, k, :], xn[:, k * P:(k + 1) * P], S.ident[:, :]).then_inc(xn_turned, 1)
                pe.wait_ge(xnT_ready, w + 1)
                nc.tensor.matmul(p_g[:, :], S.ones[0:1, :], bgrow[:, :], start=True, stop=False)
                for k in range(KD):
                    last = nc.tensor.matmul(p_g[:, :], xnT[:, k, :], wg[:, k, :], start=False, stop=k == KD - 1)
                last.then_inc(gate_done, 1)

            if first:
                for w in range(AHEAD + 1):
                    count(w)
                    spread(w)
                window(0)
                with pe.Fori(1, EARLY) as w:
                    count(AHEAD * w + 1)
                    turn(w - 1)
                    spread(AHEAD * w + 1)
                    dense(w - 1)
                    for k in range(1, AHEAD):
                        count(AHEAD * w + k + 1)
                        spread(AHEAD * w + k + 1)
                    window(w)
                with pe.Fori(EARLY, NW) as w:
                    turn(w - 1)
                    dense(w - 1)
                    window(w)
                turn(NW - 1)
                dense(NW - 1)
            else:
                def step(w, on):
                    if on(w - 1):
                        turn(w - 1)
                    if on(w - 2):
                        turn_h(w - 2)
                    if on(w - 1):
                        dense(w - 1)
                    if on(w - 2):
                        project(w - 2)
                    if on(w - 3):
                        gate(w - 3)
                    if on(w):
                        window(w)

                steps(pe, step)

        @block.scalar
        def _(act):
            def parts(w):
                act.wait_ge(di_done, w + 1)
                nc.scalar.copy(di3[:, :], p_di[:, :]).then_inc(di3_ready, 1)

            def spread(w):
                act.wait_ge(dib_done, w + 1)
                nc.scalar.copy(dib[:, bass.ds(w * P, P)], p_dib[:, :]).then_inc(dib_ready, 1)

            def selections(w):
                cs, ce, off = visits(act, w)
                with act.Fori(cs, ce) as c:
                    v = c + off
                    at = bass.ds((v % 2) * P, P)
                    act.wait_ge(inverse_ready, v + 1)
                    nc.scalar.activation(s8[:, :].unsqueeze(1), y8[:, bass.ds(v % 2, 1), :], ACT.Sqrt).then_inc(root_ready, 1)
                    act.wait_ge(norm_ready, v + 1)
                    for j in range(U):
                        act.wait_ge(sel_used, v * U + j + 1)
                        nc.scalar.activation(sel[:, j:j + 1, :], hot[:, at, j].unsqueeze(1), ACT.Copy, scale=n8[:, j:j + 1]).then_inc(sel_ready, 1)

            def summed(w):
                act.wait_ge(agg_done, w + 1)
                nc.scalar.copy(agg[:, :], p_agg[:, :]).then_inc(agg_copied, 1)

            def turned(w):
                act.wait_ge(agg_turned, KD * (w + 1))
                nc.scalar.copy(aggT[:, :, :], p_t[:, :, :]).then_inc(aggT_ready, 1)

            def hidden(w):
                act.wait_ge(h_done, w + 1)
                if first:
                    act.wait_ge(h_stored, 16 * w)
                    nc.scalar.activation(h[:, :], p_h[:, :], ACT.Relu).then_inc(h_ready, 1)
                    act.wait_ge(h_ready, w + 1)
                    act.dma_start(h_out[bass.ds(w * P, P), :], h[:, :]).then_inc(h_stored, 16)
                else:
                    nc.scalar.activation(h[:, :], p_h[:, :], ACT.Relu).then_inc(h_ready, 1)

            def turned_h(w):
                act.wait_ge(h_turned, KD * (w + 1))
                act.wait_ge(o_done, w)
                nc.scalar.copy(hT[:, :, :], p_hT[:, :, :]).then_inc(hT_ready, 1)

            def deviation(w):
                act.wait_ge(var_ready, w + 1)
                nc.scalar.activation(sd[:, :], mv[:, 1:2], ACT.Sqrt, bias=S.eps_ln[:, :]).then_inc(sd_ready, 1)

            def gate(w):
                act.wait_ge(xn_ready, w + 1)
                act.dma_start(h_out[bass.ds(w * P, P), :], xn[:, :]).then_inc(xn_stored, 16)
                act.wait_ge(xn_turned, KD * (w + 1))
                nc.scalar.copy(xnT[:, :, :], p_xT[:, :, :]).then_inc(xnT_ready, 1)
                act.wait_ge(gate_done, w + 1)
                nc.scalar.copy(S.logits[:, bass.ds(w, 1), :], p_g[:, :].unsqueeze(1)).then_inc(gate_ready, 1)

            if first:
                act.sem_inc(sel_ready, U)
                for w in range(AHEAD + 1):
                    parts(w)
                    spread(w)
                selections(0)
                with act.Fori(1, EARLY) as w:
                    summed(w - 1)
                    parts(AHEAD * w + 1)
                    turned(w - 1)
                    spread(AHEAD * w + 1)
                    for k in range(1, AHEAD):
                        parts(AHEAD * w + k + 1)
                        spread(AHEAD * w + k + 1)
                    selections(w)
                    hidden(w - 1)
                with act.Fori(EARLY, NW) as w:
                    summed(w - 1)
                    turned(w - 1)
                    selections(w)
                    hidden(w - 1)
                summed(NW - 1)
                turned(NW - 1)
                hidden(NW - 1)
                act.wait_ge(h_stored, 16 * NW)
            else:
                act.wait_ge(product_ready, 1)
                nc.scalar.activation(S.q_col[:, :], S.q_col[:, :], ACT.Sqrt, bias=S.eps_n[:, :]).then_inc(roots_ready, 1)

                def step(w, on):
                    if on(w - 1):
                        summed(w - 1)
                        turned(w - 1)
                    if on(w - 2):
                        turned_h(w - 2)
                    if on(w - 1):
                        hidden(w - 1)
                    if on(w - 3):
                        gate(w - 3)
                    if on(w - 2):
                        deviation(w - 2)

                steps(act, step)
                act.wait_ge(xn_stored, 16 * NW)


def route(nc, S, xn_rows, acc):
    with ExitStack() as ctx:
        sb = lambda n, s, d=F32: ctx.enter_context(nc.sbuf_tensor(n, s, d))
        ps = lambda n, s: bank(nc, ctx, n, s)
        sem = semaphores(nc, ctx)
        TOK = [P, NW, NE]
        one1, one2, both, score, rest, place = (sb(n, TOK) for n in ("one1", "one2", "both", "score", "rest", "place"))
        total, upto = sb("total", TOK), sb("upto", TOK)
        m1, m2, top, ex = (sb(n, [P, NW]) for n in ("m1", "m2", "top", "ex"))
        prio, region = sb("prio", [P, NE]), sb("region", [P, NE])
        ones_nw = sb("ones_nw", [P, NW])
        pos_f = sb("pos_f", [P, NW, 2])
        before = sb("before", [P, P])
        count_i = sb("count_i", [P, NE], I32)
        batch = sb("batch", [P, 3, NE])
        zero_rows = sb("zero_rows", [P, D])
        pos_i, digit_i = sb("pos_i", [P, NW, 2], I32), sb("digit_i2", [P, NW, 2], I32)
        pos_lo, pos_hi = sb("pos_lo", [P, NW * 2]), sb("pos_hi", [P, NW * 2])
        share = sb("share", [P, NW, 2])
        token_i, token = sb("token_i", [P, NW, 2], I32), sb("token", [P, NW, 2])
        dump_i, dump = sb("dump_i", [P, SLOTS], I32), sb("dump", [P, SLOTS])
        slot_i, slot = sb("slot_i", [P, SLOTS], I32), sb("slot", [P, SLOTS])
        one_lo = [sb(f"place_lo{b}", [P, LT, P]) for b in range(2)]
        one_hi = [sb(f"place_hi{b}", [P, LT, SLOTS]) for b in range(2)]
        value = [sb(f"value{b}", [P, LT, 2, SLOTS]) for b in range(2)]
        found, empty = sb("found", [P, 2, SLOTS]), sb("empty", [P, SLOTS])
        p_rank, p_total, p_list = ps("p_rank", TOK), ps("p_total", TOK), ps("p_list", [P, 2, SLOTS])
        before_ready, step, d_ready, e_ready = sem("before_ready"), sem("step_d"), sem("d_ready"), sem("e_ready")
        both_ready, ranked, pos_ready, zero_ready = sem("both_ready"), sem("ranked"), sem("pos_ready"), sem("zero_ready")
        index_ready, lo_made, hi_made, token_made = sem("index_ready"), sem("lo_made"), sem("hi_made"), sem("token_made")
        share_made, value_used, list_done, stored = sem("share_made"), sem("value_used"), sem("list_done"), sem("stored_d")
        block = ctx.enter_context(nc.Block())

        @block.vector
        def _(dve):
            n = [0]

            def link(ins):
                n[0] += 1
                ins.then_inc(step, 1)
                dve.wait_ge(step, n[0])

            wide = lambda t: t[:, :].unsqueeze(2).to_broadcast(TOK)
            per = lambda t: t[:, :].unsqueeze(1).to_broadcast(TOK)
            nc.vector.memset(zero_rows[:, :], 0.0).then_inc(zero_ready, 1)
            link(nc.vector.memset(ones_nw[:, :], 1.0))
            link(nc.vector.tensor_scalar(prio[:, :], S.iota[:, 0:NE], -1.0, float(NE), ALU.mult, ALU.add))
            for logits, m, one in ((S.logits, m1, one1), (rest, m2, one2)):
                link(nc.vector.tensor_reduce(m[:, :], logits[:, :, :], AX.X, ALU.max))
                link(nc.vector.tensor_tensor(score[:, :, :], logits[:, :, :], wide(m), ALU.is_equal))
                link(nc.vector.tensor_tensor(score[:, :, :], score[:, :, :], per(prio), ALU.mult))
                link(nc.vector.tensor_reduce(top[:, :], score[:, :, :], AX.X, ALU.max))
                link(nc.vector.tensor_tensor(one[:, :, :], score[:, :, :], wide(top), ALU.is_equal))
                if one is one1:
                    link(nc.vector.scalar_tensor_tensor(rest[:, :, :], one1[:, :, :], -3e38, S.logits[:, :, :], ALU.mult, ALU.add))
            nc.vector.tensor_tensor(both[:, :, :], one1[:, :, :], one2[:, :, :], ALU.add).then_inc(both_ready, 1)
            nc.vector.tensor_tensor(m2[:, :], m2[:, :], m1[:, :], ALU.subtract).then_inc(d_ready, 1)
            dve.wait_ge(e_ready, 1)
            link(nc.vector.tensor_scalar(m1[:, :], ex[:, :], 1.0, None, ALU.add))
            link(nc.vector.reciprocal(share[:, :, 0], m1[:, :]))
            link(nc.vector.tensor_tensor(share[:, :, 1], ex[:, :], share[:, :, 0], ALU.mult))
            dve.wait_ge(ranked, 1)
            link(nc.vector.tensor_copy(total[:, :, :], p_total[:, :, :]))
            for e in range(NE):
                last = nc.vector.tensor_tensor_scan(upto[:, :, e], ones_nw[:, :], total[:, :, e], 0.0, ALU.mult, ALU.add)
                if e < NE - 1:
                    last.then_inc(pos_ready, 1)
            link(last)
            dve.wait_ge(pos_ready, NE - 1)
            link(nc.vector.tensor_scalar(batch[:, 0, :], upto[:, NW - 1, :], float(B - 1), None, ALU.add))
            link(nc.vector.tensor_copy(count_i[:, :], batch[:, 0, :]))
            link(nc.vector.tensor_single_scalar(count_i[:, :], count_i[:, :], 8, ALU.logical_shift_right))
            link(nc.vector.tensor_copy(batch[:, 0, :], count_i[:, :]))
            link(nc.vector.tensor_scalar(batch[:, 0, :], batch[:, 0, :], 1.0, None, ALU.max))
            link(nc.vector.tensor_tensor_scan(batch[:, 1, :], ones_nw[:, 0:NE], batch[:, 0, :], 0.0, ALU.mult, ALU.add))
            link(nc.vector.tensor_tensor(batch[:, 2, :], batch[:, 1, :], batch[:, 0, :], ALU.subtract))
            link(nc.vector.tensor_scalar(region[:, :], batch[:, 2, :], float(B), None, ALU.mult))
            link(nc.vector.tensor_copy(S.etab[0:1, 1, :], batch[0:1, 1, :]))
            link(nc.vector.tensor_copy(S.etab[0:1, 0, :], batch[0:1, 2, :]))
            link(nc.vector.tensor_tensor(place[:, :, :], upto[:, :, :], total[:, :, :], ALU.subtract))
            link(nc.vector.tensor_tensor(place[:, :, :], place[:, :, :], p_rank[:, :, :], ALU.add))
            link(nc.vector.tensor_tensor(place[:, :, :], place[:, :, :], per(region), ALU.add))
            for k, one in enumerate((one1, one2)):
                link(nc.vector.tensor_tensor(score[:, :, :], place[:, :, :], one[:, :, :], ALU.mult))
                link(nc.vector.tensor_reduce(pos_f[:, :, k], score[:, :, :], AX.X, ALU.add))
            link(nc.vector.tensor_copy(pos_i[:, :, :], pos_f[:, :, :]))
            link(nc.vector.tensor_single_scalar(digit_i[:, :, :], pos_i[:, :, :], P - 1, ALU.bitwise_and))
            link(nc.vector.tensor_copy(pos_lo[:, :], digit_i[:, :, :].rearrange("p w k -> p (w k)")))
            link(nc.vector.tensor_single_scalar(digit_i[:, :, :], pos_i[:, :, :], 7, ALU.logical_shift_right))
            link(nc.vector.tensor_copy(pos_hi[:, :], digit_i[:, :, :].rearrange("p w k -> p (w k)")))
            dve.wait_ge(index_ready, 3)
            link(nc.vector.tensor_copy(token[:, :, :], token_i[:, :, :]))
            link(nc.vector.tensor_copy(dump[:, :], dump_i[:, :]))
            nc.vector.tensor_copy(slot[:, :], slot_i[:, :]).then_inc(pos_ready, 1)
            dve.wait_ge(pos_ready, NE)
            dve.sem_inc(S.dve_turn, 1)
            flat = token[:, :, :].rearrange("p w k -> p (w k)")
            with dve.Fori(0, LSTEPS // 2) as i:
                for b in range(2):
                    k = 2 * i + b
                    at = bass.ds(k * LT, LT)
                    dve.wait_ge(value_used, k + 1)
                    dve.wait_ge(share_made, k + 1)
                    nc.vector.tensor_tensor(one_hi[b][:, :, :], slot[:, :].unsqueeze(1).to_broadcast([P, LT, SLOTS]),
                                            pos_hi[:, at].unsqueeze(2).to_broadcast([P, LT, SLOTS]), ALU.is_equal).then_inc(hi_made, 1)
                    nc.vector.tensor_tensor(one_lo[b][:, :, :], S.iota[:, :].unsqueeze(1).to_broadcast([P, LT, P]),
                                            pos_lo[:, at].unsqueeze(2).to_broadcast([P, LT, P]), ALU.is_equal).then_inc(lo_made, 1)
                    dve.wait_ge(hi_made, k + 1)
                    nc.vector.tensor_tensor(value[b][:, :, 0, :], one_hi[b][:, :, :],
                                            flat[:, at].unsqueeze(2).to_broadcast([P, LT, SLOTS]), ALU.mult).then_inc(token_made, 1)
            dve.wait_ge(list_done, 1)
            link(nc.vector.tensor_copy(found[:, :, :], p_list[:, :, :]))
            link(nc.vector.tensor_copy(S.share_at[:, :], found[:, 1, :]))
            link(nc.vector.tensor_scalar(empty[:, :], found[:, 0, :], 0.0, None, ALU.is_equal))
            link(nc.vector.tensor_tensor(empty[:, :], empty[:, :], dump[:, :], ALU.mult))
            link(nc.vector.tensor_tensor(empty[:, :], empty[:, :], found[:, 0, :], ALU.add))
            link(nc.vector.tensor_scalar(empty[:, :], empty[:, :], -1.0, None, ALU.add))
            link(nc.vector.tensor_copy(S.row_at[:, :], empty[:, :]))

        @block.scalar
        def _(act):
            act.wait_ge(d_ready, 1)
            nc.scalar.activation(ex[:, :], m2[:, :], ACT.Exp).then_inc(e_ready, 1)

        @block.tensor
        def _(pe):
            pe.wait_ge(before_ready, 2)
            pe.wait_ge(both_ready, 1)
            nc.tensor.matmul(p_rank[:, :, :], before[:, :], both[:, :, :], start=True, stop=True)
            nc.tensor.matmul(p_total[:, :, :], S.ones[:, :], both[:, :, :], start=True, stop=True).then_inc(ranked, 1)

            nc.tensor.matmul(p_list[:, :, :], S.zeros[:, 0:P], S.zeros[:, 0:2 * SLOTS], start=True, stop=False)
            pe.sem_inc(value_used, 2)
            with pe.Fori(0, LSTEPS // 2) as i:
                for b in range(2):
                    k = 2 * i + b
                    pe.wait_ge(lo_made, k + 1)
                    pe.wait_ge(token_made, k + 1)
                    pe.wait_ge(share_made, k + 3)
                    for j in range(LT):
                        last = nc.tensor.matmul(p_list[:, :, :], one_lo[b][:, j, :], value[b][:, j, :, :], start=False, stop=False)
                    last.then_inc(value_used, 1)
            nc.tensor.matmul(p_list[:, 0, 0:1], S.zeros[:, 0:P], S.zeros[:, 0:1], start=False, stop=True).then_inc(list_done, 1)

        @block.sync
        def _(sp):
            sp.dma_start(acc[0:PADN, :].rearrange("(w p) d -> p w d", p=P), S.x2[:, :, :]).then_inc(stored, 16)
            sp.wait_ge(zero_ready, 1)
            for rows in (acc, xn_rows):
                sp.dma_start(rows[PADN:PADN + DUMP, :].rearrange("(w p) d -> p w d", p=P), zero_rows[:, :].unsqueeze(1).to_broadcast([P, DUMP // P, D])).then_inc(stored, 16)
            sp.wait_ge(stored, 48)

        @block.gpsimd
        def _(pool):
            nc.gpsimd.memset(before[:, :], 1.0).then_inc(before_ready, 1)
            pool.wait_ge(before_ready, 1)
            pool.affine_select(out=before[:, :], in_=before[:, :], compare_op=ALU.is_gt, fill=0.0, base=0,
                               pattern=[[1, P]], channel_multiplier=-1).then_inc(before_ready, 1)
            pool.iota(token_i[:, :, :], [[P, NW], [0, 2]], base=1, channel_multiplier=1).then_inc(index_ready, 1)
            pool.iota(dump_i[:, :], [[0, SLOTS // HALVES], [P, HALVES]], base=PADN + 1, channel_multiplier=1).then_inc(index_ready, 1)
            pool.iota(slot_i[:, :], [[1, SLOTS]], base=0, channel_multiplier=0).then_inc(index_ready, 1)
            pool.sem_inc(share_made, 2)
            flat = share[:, :, :].rearrange("p w k -> p (w k)")
            with pool.Fori(0, LSTEPS // 2) as i:
                for b in range(2):
                    k = 2 * i + b
                    pool.wait_ge(hi_made, k + 1)
                    pool.sem_inc(S.pool_turn, 1)
                    pool.wait_ge(value_used, k + 1)
                    pool.sem_inc(S.pool_turn, 1)
                    nc.gpsimd.tensor_tensor(value[b][:, :, 1, :], one_hi[b][:, :, :],
                                            flat[:, bass.ds(k * LT, LT)].unsqueeze(2).to_broadcast([P, LT, SLOTS]), ALU.mult).then_inc(share_made, 1)


def experts(nc, S, xn_rows, acc, W1, b1, W2, b2, out):
    with ExitStack() as ctx:
        sb = lambda n, s, d=F32: ctx.enter_context(nc.sbuf_tensor(n, s, d))
        ps = lambda n, s: bank(nc, ctx, n, s)
        sem = semaphores(nc, ctx)
        w1 = [sb(f"w1_{p}", [P, KD, H]) for p in range(2)]
        w2 = [sb(f"w2_{p}", [P, KH, D]) for p in range(2)]
        b1n, b1T = sb("b1n", [NE * KH, P]), sb("b1T", [P, NE * KH])
        b2b = sb("b2b", [P, NE, D])
        xb, xT = sb("xb", [P, HALVES, D]), sb("xT", [P, KD, B])
        hid = sb("hid", [P, KH, B])
        y, raw = sb("y", [P, HALVES, D]), sb("raw", [P, HALVES, D])
        row_x, row_y = sb("row_x", [P, HALVES], I32), sb("row_y", [P, HALVES], I32)
        p_x, p_b = ps("p_x", [P, KD, B]), ps("p_b", [P, NE * KH])
        p_y = [ps(f"p_y{t}", [P, D]) for t in range(HALVES)]
        p_h = [ps(f"p_hid{i}", [P, B]) for i in range(4)]
        w_in = [sem(f"w_in{p}") for p in range(2)]
        w_used, bias_in, b1_turned, b1_ready = sem("w_used"), sem("bias_in"), sem("b1_turned"), sem("b1_ready")
        x_in, x_turned, xT_ready, hid_done, hid_ready = sem("x_in3"), sem("x_turned"), sem("xT_ready"), sem("hid_done"), sem("hid_ready")
        y_done, raw_ready, y_ready, y_added = sem("y_done"), sem("raw_ready"), sem("y_ready"), sem("y_added")
        row_x_ready, row_y_ready, out_stored, all_added = sem("row_x_ready"), sem("row_y_ready"), sem("out_stored"), sem("all_added")
        TURNS = KD * HALVES
        block = ctx.enter_context(nc.Block())

        def batches(eng, e):
            return (eng.value_load(S.etab[0:1, 0, bass.ds(e, 1)], min_val=0, max_val=MAXB - 1),
                    eng.value_load(S.etab[0:1, 1, bass.ds(e, 1)], min_val=1, max_val=MAXB))

        def used(eng):
            return eng.value_load(S.etab[0:1, 1, NE - 1:NE], min_val=NE, max_val=MAXB)

        @block.sync
        def _(sp):
            sp.dma_start(b1n[:, :], b1.rearrange("e (k p) -> (e k) p", p=P)).then_inc(bias_in, 16)
            sp.dma_start(b2b[:, :, :], b2.rearrange("e d -> (e d)").partition_broadcast(P)).then_inc(bias_in, 16)

            def load(e, p):
                sp.wait_ge(w_used, e)
                sp.dma_start(w1[p][:, :, :], W1[bass.ds(e, 1), :, :].rearrange("a (k p) n -> p (a k) n", p=P)).then_inc(w_in[p], 16)
                sp.dma_start(w2[p][:, :, :], W2[bass.ds(e, 1), :, :].rearrange("a (k p) n -> p (a k) n", p=P)).then_inc(w_in[p], 16)

            with sp.Fori(0, NE // 2) as pair:
                for p in range(2):
                    load(pair * 2 + p, p)
            sp.wait_ge(all_added, 1)
            sp.dma_start(out[:, :], acc[0:NODES, :]).then_inc(out_stored, 16)
            sp.wait_ge(out_stored, 16)

        @block.scalar
        def _(act):
            act.wait_ge(b1_turned, 1)
            nc.scalar.copy(b1T[:, :], p_b).then_inc(b1_ready, 1)
            act.wait_ge(b1_ready, 1)
            with act.Fori(0, NE) as e:
                g0, g1 = batches(act, e)
                with act.Fori(g0, g1) as g:
                    act.wait_ge(y_done, g)
                    for k in range(KH):
                        act.wait_ge(hid_done, g * KH + k + 1)
                        nc.scalar.activation(hid[:, k, :], p_h[k % 4], ACT.Gelu, bias=b1T[:, bass.ds(e * KH + k, 1)]).then_inc(hid_ready, 1)

        @block.tensor
        def _(pe):
            def turn(g):
                pe.wait_ge(x_in, 16 * HALVES * (g + 1))
                for t in range(HALVES):
                    for k in range(KD):
                        nc.tensor.transpose(p_x[:, k, t * P:(t + 1) * P], xb[:, t, k * P:(k + 1) * P], S.ident[:, :]).then_inc(x_turned, 1)

            pe.sem_inc(w_used, 1)
            pe.wait_ge(bias_in, 32)
            nc.tensor.transpose(p_b, b1n[:, :], S.ident[0:NE * KH, 0:NE * KH]).then_inc(b1_turned, 1)
            turn(0)
            with pe.Fori(0, NE // 2) as pair:
                for p in range(2):
                    g0, g1 = batches(pe, pair * 2 + p)
                    pe.wait_ge(w_in[p], 32 * (pair + 1))
                    pe.sem_inc(S.pe_turn, 1)
                    with pe.Fori(g0, g1) as g:
                        pe.wait_ge(xT_ready, g + 1)
                        for k in range(KH):
                            if k >= 4:
                                pe.wait_ge(hid_ready, g * KH + k - 3)
                            for d in range(KD):
                                last = nc.tensor.matmul(p_h[k % 4], w1[p][:, d, k * P:(k + 1) * P], xT[:, d, :], start=d == 0, stop=d == KD - 1)
                            last.then_inc(hid_done, 1)
                        turn(g + 1)
                        pe.wait_ge(raw_ready, HALVES * g)
                        for k in range(KH):
                            pe.wait_ge(hid_ready, g * KH + k + 1)
                            for t in range(HALVES):
                                last = nc.tensor.matmul(p_y[t], hid[:, k, t * P:(t + 1) * P], w2[p][:, k, :], start=k == 0, stop=k == KH - 1)
                        last.then_inc(y_done, 1)
                    nc.tensor.matmul(p_b[:, 0:1], S.zeros[:, 0:P], S.zeros[:, 0:1], start=True, stop=True).then_inc(w_used, 1)

        @block.vector
        def _(dve):
            dve.wait_ge(x_turned, TURNS)
            nc.vector.tensor_copy(xT[:, :, :], p_x[:, :, :]).then_inc(xT_ready, 1)
            with dve.Fori(0, NE) as e:
                g0, g1 = batches(dve, e)
                with dve.Fori(g0, g1) as g:
                    dve.wait_ge(x_turned, TURNS * (g + 2))
                    dve.sem_inc(S.dve_turn, 1)
                    nc.vector.tensor_copy(xT[:, :, :], p_x[:, :, :]).then_inc(xT_ready, 1)
                    dve.wait_ge(y_done, g + 1)
                    dve.wait_ge(y_added, 16 * HALVES * g)
                    dve.sem_inc(S.dve_turn, 1)
                    for t in range(HALVES):
                        nc.vector.tensor_tensor(raw[:, t:t + 1, :], p_y[t].unsqueeze(1), b2b[:, bass.ds(e, 1), :], ALU.add).then_inc(raw_ready, 1)
                    dve.wait_ge(raw_ready, HALVES * (g + 1))
                    dve.sem_inc(S.dve_turn, 1)
                    for t in range(HALVES):
                        nc.vector.tensor_scalar(y[:, t, :], raw[:, t, :], S.share_at[:, bass.ds(g * HALVES + t, 1)], None, ALU.mult).then_inc(y_ready, 1)

        @block.gpsimd
        def _(pool):
            def gather(g):
                nc.gpsimd.tensor_copy(row_x[:, :], S.row_at[:, bass.ds(g * HALVES, HALVES)]).then_inc(row_x_ready, 1)
                pool.wait_ge(row_x_ready, g + 1)
                pool.sem_inc(S.pool_turn, 1)
                for t in range(HALVES):
                    pool.indirect_dma_start(out=xb[:, t, :], out_offset=None, in_=xn_rows[:, :],
                                            in_offset=bass.IndirectOffsetOnAxis(ap=row_x[:, t:t + 1], axis=0)).then_inc(x_in, 16)

            last = used(pool)
            gather(0)
            pool.wait_ge(x_turned, TURNS)
            gather(1)
            with pool.Fori(0, last) as g:
                pool.wait_ge(x_turned, TURNS * (g + 2))
                pool.sem_inc(S.pool_turn, 1)
                gather(g + 2)
                pool.wait_ge(y_added, 16 * HALVES * g)
                pool.sem_inc(S.pool_turn, 1)
                nc.gpsimd.tensor_copy(row_y[:, :], S.row_at[:, bass.ds(g * HALVES, HALVES)]).then_inc(row_y_ready, 1)
                pool.wait_ge(row_y_ready, g + 1)
                pool.sem_inc(S.pool_turn, 1)
                pool.wait_ge(y_ready, HALVES * (g + 1))
                pool.sem_inc(S.pool_turn, 1)
                for t in range(HALVES):
                    pool.indirect_dma_start(out=acc[:, :], out_offset=bass.IndirectOffsetOnAxis(ap=row_y[:, t:t + 1], axis=0),
                                            in_=y[:, t, :], in_offset=None, compute_op=ALU.add).then_inc(y_added, 16)
            pool.wait_ge(y_added, 16 * HALVES * last)
            pool.sem_inc(all_added, 1)
            pool.wait_ge(x_in, 16 * HALVES * (last + 2))
            pool.sem_inc(S.pool_turn, 1)


class Shared:
    pass


def build(nc, x, src, dst, edge_weight, W6, b6, W7, b7, Wp, bp, Wg, bg, W1, b1, W2, b2, out):
    rows1 = nc.dram_tensor("rows1", [PADN, ROW1], F32).ap()
    h6 = nc.dram_tensor("h6", [PADN, D], F32).ap()
    xn_rows = nc.dram_tensor("xn_rows", [PADN + DUMP, D], F32).ap()
    acc = nc.dram_tensor("acc", [PADN + DUMP, D], F32).ap()
    S = Shared()
    with ExitStack() as ctx:
        sb = lambda n, s, d=F32: ctx.enter_context(nc.sbuf_tensor(n, s, d))
        S.pool_turn = ctx.enter_context(nc.semaphore("pool_turn"))
        S.pe_turn = ctx.enter_context(nc.semaphore("pe_turn"))
        S.dve_turn = ctx.enter_context(nc.semaphore("dve_turn"))
        S.src_col = sb("src_col", [P, TC], I32)
        S.dst_col = sb("dst_col", [P, TC])
        S.w_col = sb("w_col", [P, TC])
        S.q_col = sb("q_col", [P, TC])
        S.do_col = sb("do_col", [P, TC])
        S.ident = sb("ident", [P, P])
        S.ones = sb("ones", [P, P])
        S.zeros = sb("zeros", [P, D], BF16)
        S.iota = sb("iota", [P, P])
        S.base = sb("base", [P, NW])
        S.eps_ln = sb("eps_ln", [P, 1])
        S.eps_n = sb("eps_n", [P, 1])
        S.deg = sb("deg", [P, NW])
        S.sorted_f = sb("sorted_f", [1, 2])
        S.tab_f = sb("tab_f", [1, 5, NW + 1])
        S.tab = sb("tab", [1, NW + 1, 5], I32)
        with nc.sbuf_tensor("w3", [P, 3, TC], BF16) as S.w3:
            load_edges_and_histogram(nc, x, src, dst, edge_weight, S, rows1)
            gnn_layer(nc, S, rows1, ROW1, W6, b6, h6, True)
        S.x2 = sb("x2", [P, NW, D])
        S.logits = sb("logits", [P, NW, NE])
        gnn_layer(nc, S, h6, D, W7, b7, xn_rows, False, x, Wp, bp, Wg, bg)
        S.row_at = sb("row_at", [P, SLOTS], I32)
        S.share_at = sb("share_at", [P, SLOTS])
        S.etab = sb("etab", [1, 2, NE], I32)
        route(nc, S, xn_rows, acc)
        experts(nc, S, xn_rows, acc, W1, b1, W2, b2, out)


_INS = ['x', 'src', 'dst', 'edge_weight', 'L0_gnn_W6', 'L0_gnn_b6', 'L0_gnn_W7', 'L0_gnn_b7', 'L0_gnn_Wp', 'L0_gnn_bp',
        'L0_ffn_Wg', 'L0_ffn_bg', 'L0_ffn_W1', 'L0_ffn_b1', 'L0_ffn_W2', 'L0_ffn_b2']


def kernel(**inputs):
    import numpy as _np
    import concourse.bacc as _bacc
    from concourse.bass_utils import run_bass_kernel_spmd as _run
    nc = _bacc.Bacc("TRN2", target_bir_lowering=False, num_devices=1)
    arrays, args = {}, []
    for name in _INS:
        a = _np.ascontiguousarray(inputs[name])
        arrays[f"in_{name}_dram"] = a
        args.append(nc.dram_tensor(f"in_{name}_dram", a.shape, mybir.dt.from_np(a.dtype), kind="ExternalInput").ap())
    o = nc.dram_tensor("out_0_dram", (NODES, D), F32, kind="ExternalOutput").ap()
    build(nc, *args, o)
    r = _run(nc, [arrays], core_ids=[0])
    return r.results[0]["out_0_dram"]
```
